# Optimizing a Trainium2 kernel written in Bass

```python
import numpy as np
import jax
import jax.numpy as jnp

def _softmax(x, axis=-1):
    return jax.nn.softmax(x, axis=axis)

def _gelu(x):
    return jax.nn.gelu(x, approximate=True)

def _silu(x):
    return jax.nn.silu(x)

def _sigmoid(x):
    return jax.nn.sigmoid(x)

def _layernorm(x, axis=-1, eps=1e-05):
    m = jnp.mean(x, axis=axis, keepdims=True)
    v = jnp.var(x, axis=axis, keepdims=True)
    return (x - m) / jnp.sqrt(v + eps)

def _scatter_add(tgt, idx, src, axis=0):
    return tgt.at[idx].add(src)

def _segment_sum(src, seg, n):
    return jax.ops.segment_sum(src, seg, n)
kernel_name = 'mk_xattn_seq_d4_seqx_r8_2917ed'

def setup_inputs(seed: int=0):
    np.random.seed(seed)
    _w = jnp.asarray

    def _rec_inputs():
        import jax
        import jax.numpy as jnp
        _rk = jax.random.key(seed)
        x = -0.0002928 + 1 * jax.random.normal(jax.random.fold_in(_rk, 1), (8, 256, 128), jnp.float32)
        _lenS = 256 - jax.random.randint(jax.random.fold_in(_rk, 7), (8,), 0, max(1, 256 // 4) + 1, jnp.int32)
        _lenS2 = 512 - jax.random.randint(jax.random.fold_in(_rk, 8), (8,), 0, max(1, 512 // 4) + 1, jnp.int32)
        _ctx_1024P = jax.random.normal(jax.random.fold_in(_rk, 11), (8, 16, 128), jnp.float32)
        _ctx_1024c = jax.random.dirichlet(jax.random.fold_in(_rk, 511), 0.3 * jnp.ones((16,), jnp.float32), (8, 512))
        _ctx_1024t = jnp.einsum('bsk,bkd->bsd', _ctx_1024c, _ctx_1024P)
        _ctx_1024t = _ctx_1024t * jax.lax.rsqrt(jnp.mean(jnp.square(_ctx_1024t)) + 1e-12) * 0.953939
        ctx_1024 = -1.39393e-06 + 0.999914 * (_ctx_1024t + 0.3 * jax.random.normal(jax.random.fold_in(_rk, 611), (8, 512, 128), jnp.float32))
        _validS = jnp.arange(256)[None, :] < _lenS[:, None]
        _validS2 = jnp.arange(512)[None, :] < _lenS2[:, None]
        _causal = jnp.tril(jnp.ones((256, 256), dtype=bool))
        mask_Bx1x1xS2_ff0 = jnp.where(jnp.ones((8, 1, 1, 512), dtype=bool), 0.0, -1000000000.0).astype(jnp.float32)
        return (x, ctx_1024, mask_Bx1x1xS2_ff0)
    x, ctx_1024, mask_Bx1x1xS2_ff0 = _rec_inputs()

    def _L0_xattn_setup():
        import jax, jax.numpy as jnp
        import numpy as np
        D_MODEL = 128
        N_HEADS = 16
        D_K = D_MODEL // N_HEADS
        D_FFN = 512
        EPS = 1e-06
        NEG_INF = -1000000000.0

        def _ln(x, scale, bias):
            mu = jnp.mean(x, axis=-1, keepdims=True)
            var = jnp.mean(jnp.square(x - mu), axis=-1, keepdims=True)
            return (x - mu) * jax.lax.rsqrt(var + EPS) * scale + bias

        def _attend(q, k, v, mask):
            scale = jax.lax.rsqrt(jnp.asarray(D_K, q.dtype))
            logits = jnp.einsum('bhqd,bhkd->bhqk', q, k) * scale
            if mask is not None:
                logits = jnp.where(mask, logits, jnp.asarray(NEG_INF, logits.dtype))
            w = jax.nn.softmax(logits.astype(jnp.float32), axis=-1).astype(q.dtype)
            return jnp.einsum('bhqk,bhkd->bhqd', w, v)

        def _heads(t, B, L):
            return jnp.transpose(t.reshape(B, L, N_HEADS, D_K), (0, 2, 1, 3))
        key = jax.random.key(seed)
        ks = jax.random.split(key, 16)
        B, L = (2, 256)
        s = lambda fan_in: 1.0 / np.sqrt(fan_in)
        return {'x': jax.random.normal(ks[0], (B, L, D_MODEL), jnp.float32), 'encoder_output': jax.random.normal(ks[1], (B, L, D_MODEL), jnp.float32), 'W_qkv': jax.random.normal(ks[2], (D_MODEL, 3 * D_MODEL), jnp.float32) * s(D_MODEL), 'W_self_out': jax.random.normal(ks[3], (D_MODEL, D_MODEL), jnp.float32) * s(D_MODEL), 'W_q': jax.random.normal(ks[4], (D_MODEL, D_MODEL), jnp.float32) * s(D_MODEL), 'W_kv': jax.random.normal(ks[5], (D_MODEL, 2 * D_MODEL), jnp.float32) * s(D_MODEL), 'W_cross_out': jax.random.normal(ks[6], (D_MODEL, D_MODEL), jnp.float32) * s(D_MODEL), 'W1': jax.random.normal(ks[7], (D_MODEL, D_FFN), jnp.float32) * s(D_MODEL), 'b1': jnp.zeros((D_FFN,), jnp.float32), 'W2': jax.random.normal(ks[8], (D_FFN, D_MODEL), jnp.float32) * s(D_FFN), 'b2': jnp.zeros((D_MODEL,), jnp.float32), 'ln1_scale': jnp.ones((D_MODEL,), jnp.float32), 'ln1_bias': jnp.zeros((D_MODEL,), jnp.float32), 'ln2_scale': jnp.ones((D_MODEL,), jnp.float32), 'ln2_bias': jnp.zeros((D_MODEL,), jnp.float32), 'ln3_scale': jnp.ones((D_MODEL,), jnp.float32), 'ln3_bias': jnp.zeros((D_MODEL,), jnp.float32)}
    _L0_xattn_all = _L0_xattn_setup()
    _L0_xattn_in = {k: v for k, v in _L0_xattn_all.items() if k in ('W_qkv', 'W_self_out', 'W_q', 'W_kv', 'W_cross_out', 'W1', 'b1', 'W2', 'b2', 'ln1_scale', 'ln1_bias', 'ln2_scale', 'ln2_bias', 'ln3_scale', 'ln3_bias')}
    del _L0_xattn_all

    def _L1_xattn_setup():
        import jax, jax.numpy as jnp
        import numpy as np
        D_MODEL = 128
        PROJ = 128
        LN_EPS = 1e-05
        key = jax.random.key(seed)
        ks = jax.random.split(key, 12)
        B, Q, N = (16, 16, 512)
        s = 1.0 / np.sqrt(D_MODEL)
        sp = 1.0 / np.sqrt(PROJ)
        return {'virtual_node': jax.random.normal(ks[0], (B, Q, D_MODEL), jnp.float32), 'node_features': jax.random.normal(ks[1], (B, N, D_MODEL), jnp.float32), 'Wq': jax.random.uniform(ks[2], (D_MODEL, PROJ), jnp.float32, -s, s), 'bq': jax.random.uniform(ks[3], (PROJ,), jnp.float32, -s, s), 'Wk': jax.random.uniform(ks[4], (D_MODEL, PROJ), jnp.float32, -s, s), 'bk': jax.random.uniform(ks[5], (PROJ,), jnp.float32, -s, s), 'Wv': jax.random.uniform(ks[6], (D_MODEL, PROJ), jnp.float32, -s, s), 'bv': jax.random.uniform(ks[7], (PROJ,), jnp.float32, -s, s), 'Wf': jax.random.uniform(ks[8], (PROJ, D_MODEL), jnp.float32, -sp, sp), 'bf': jax.random.uniform(ks[9], (D_MODEL,), jnp.float32, -sp, sp), 'ln_gamma': jnp.ones((D_MODEL,), jnp.float32), 'ln_beta': jnp.zeros((D_MODEL,), jnp.float32)}
    _L1_xattn_all = _L1_xattn_setup()
    _L1_xattn_in = {k: v for k, v in _L1_xattn_all.items() if k in ('Wq', 'bq', 'Wk', 'bk', 'Wv', 'bv', 'Wf', 'bf', 'ln_gamma', 'ln_beta')}
    del _L1_xattn_all

    def _L2_xattn_setup():
        import jax, jax.numpy as jnp
        import numpy as np
        D_MODEL = 128
        H = 16
        D_HEAD = D_MODEL // H
        EPS = 1e-05
        key = jax.random.key(seed)
        ks = jax.random.split(key, 10)
        bs, seq = (4, 256)
        scale = 1.0 / np.sqrt(D_MODEL)
        return {'q': jax.random.normal(ks[0], (bs, seq, D_MODEL), jnp.float32), 'k': jax.random.normal(ks[1], (bs, seq, D_MODEL), jnp.float32), 'v': jax.random.normal(ks[2], (bs, seq, D_MODEL), jnp.float32), 'zero_mask': jnp.zeros((bs, 1, 1, seq), jnp.float32), 'Wq': jax.random.normal(ks[3], (D_MODEL, D_MODEL), jnp.float32) * scale, 'Wk': jax.random.normal(ks[4], (D_MODEL, D_MODEL), jnp.float32) * scale, 'Wv': jax.random.normal(ks[5], (D_MODEL, D_MODEL), jnp.float32) * scale, 'Wo': jax.random.normal(ks[6], (D_MODEL, D_MODEL), jnp.float32) * scale, 'gamma': jnp.ones((D_MODEL,), jnp.float32), 'beta': jnp.zeros((D_MODEL,), jnp.float32)}
    _L2_xattn_all = _L2_xattn_setup()
    _L2_xattn_in = {k: v for k, v in _L2_xattn_all.items() if k in ('Wq', 'Wk', 'Wv', 'Wo', 'gamma', 'beta')}
    del _L2_xattn_all

    def _L3_xattn_setup():
        import jax, jax.numpy as jnp
        import numpy as np
        HIDDEN_NUMS = 64
        key = jax.random.key(seed)
        k1, k2, k3 = jax.random.split(key, 3)
        B, S, T, H2 = (32, 128, 64, 2 * HIDDEN_NUMS)
        target_hidden_states = jax.random.normal(k1, (B, T, H2), dtype=jnp.float32)
        hidden_states = jax.random.normal(k2, (B, S, H2), dtype=jnp.float32)
        trans_W = jax.random.uniform(k3, (4 * HIDDEN_NUMS, H2), dtype=jnp.float32, minval=-0.01, maxval=0.01)
        trans_b = jnp.zeros((H2,), dtype=jnp.float32)
        return {'target_hidden_states': target_hidden_states, 'hidden_states': hidden_states, 'trans_W': trans_W, 'trans_b': trans_b}
    _L3_xattn_all = _L3_xattn_setup()
    _L3_xattn_in = {k: v for k, v in _L3_xattn_all.items() if k in ('trans_W', 'trans_b')}
    del _L3_xattn_all
    return {'x': x, 'ctx_1024': ctx_1024, 'mask_Bx1x1xS2_ff0': mask_Bx1x1xS2_ff0, 'L0_xattn_W_qkv': _L0_xattn_in['W_qkv'], 'L0_xattn_W_self_out': _L0_xattn_in['W_self_out'], 'L0_xattn_W_q': _L0_xattn_in['W_q'], 'L0_xattn_W_kv': _L0_xattn_in['W_kv'], 'L0_xattn_W_cross_out': _L0_xattn_in['W_cross_out'], 'L0_xattn_W1': _L0_xattn_in['W1'], 'L0_xattn_b1': _L0_xattn_in['b1'], 'L0_xattn_W2': _L0_xattn_in['W2'], 'L0_xattn_b2': _L0_xattn_in['b2'], 'L0_xattn_ln1_scale': _L0_xattn_in['ln1_scale'], 'L0_xattn_ln1_bias': _L0_xattn_in['ln1_bias'], 'L0_xattn_ln2_scale': _L0_xattn_in['ln2_scale'], 'L0_xattn_ln2_bias': _L0_xattn_in['ln2_bias'], 'L0_xattn_ln3_scale': _L0_xattn_in['ln3_scale'], 'L0_xattn_ln3_bias': _L0_xattn_in['ln3_bias'], 'L1_xattn_Wq': _L1_xattn_in['Wq'], 'L1_xattn_bq': _L1_xattn_in['bq'], 'L1_xattn_Wk': _L1_xattn_in['Wk'], 'L1_xattn_bk': _L1_xattn_in['bk'], 'L1_xattn_Wv': _L1_xattn_in['Wv'], 'L1_xattn_bv': _L1_xattn_in['bv'], 'L1_xattn_Wf': _L1_xattn_in['Wf'], 'L1_xattn_bf': _L1_xattn_in['bf'], 'L1_xattn_ln_gamma': _L1_xattn_in['ln_gamma'], 'L1_xattn_ln_beta': _L1_xattn_in['ln_beta'], 'L2_xattn_Wq': _L2_xattn_in['Wq'], 'L2_xattn_Wk': _L2_xattn_in['Wk'], 'L2_xattn_Wv': _L2_xattn_in['Wv'], 'L2_xattn_Wo': _L2_xattn_in['Wo'], 'L2_xattn_gamma': _L2_xattn_in['gamma'], 'L2_xattn_beta': _L2_xattn_in['beta'], 'L3_xattn_trans_W': _L3_xattn_in['trans_W'], 'L3_xattn_trans_b': _L3_xattn_in['trans_b']}

def reference(x, ctx_1024, mask_Bx1x1xS2_ff0, L0_xattn_W_qkv, L0_xattn_W_self_out, L0_xattn_W_q, L0_xattn_W_kv, L0_xattn_W_cross_out, L0_xattn_W1, L0_xattn_b1, L0_xattn_W2, L0_xattn_b2, L0_xattn_ln1_scale, L0_xattn_ln1_bias, L0_xattn_ln2_scale, L0_xattn_ln2_bias, L0_xattn_ln3_scale, L0_xattn_ln3_bias, L1_xattn_Wq, L1_xattn_bq, L1_xattn_Wk, L1_xattn_bk, L1_xattn_Wv, L1_xattn_bv, L1_xattn_Wf, L1_xattn_bf, L1_xattn_ln_gamma, L1_xattn_ln_beta, L2_xattn_Wq, L2_xattn_Wk, L2_xattn_Wv, L2_xattn_Wo, L2_xattn_gamma, L2_xattn_beta, L3_xattn_trans_W, L3_xattn_trans_b):
    import jax
    import jax.numpy as jnp

    def _L0_xattn_ref(x, encoder_output, W_qkv, W_self_out, W_q, W_kv, W_cross_out, W1, b1, W2, b2, ln1_scale, ln1_bias, ln2_scale, ln2_bias, ln3_scale, ln3_bias):
        import jax, jax.numpy as jnp
        import numpy as np
        D_MODEL = 128
        N_HEADS = 16
        D_K = D_MODEL // N_HEADS
        D_FFN = 512
        EPS = 1e-06
        NEG_INF = -1000000000.0

        def _ln(x, scale, bias):
            mu = jnp.mean(x, axis=-1, keepdims=True)
            var = jnp.mean(jnp.square(x - mu), axis=-1, keepdims=True)
            return (x - mu) * jax.lax.rsqrt(var + EPS) * scale + bias

        def _attend(q, k, v, mask):
            scale = jax.lax.rsqrt(jnp.asarray(D_K, q.dtype))
            logits = jnp.einsum('bhqd,bhkd->bhqk', q, k) * scale
            if mask is not None:
                logits = jnp.where(mask, logits, jnp.asarray(NEG_INF, logits.dtype))
            w = jax.nn.softmax(logits.astype(jnp.float32), axis=-1).astype(q.dtype)
            return jnp.einsum('bhqk,bhkd->bhqd', w, v)

        def _heads(t, B, L):
            return jnp.transpose(t.reshape(B, L, N_HEADS, D_K), (0, 2, 1, 3))
        B, L, _ = x.shape
        Ls = encoder_output.shape[1]
        nx = _ln(x, ln1_scale, ln1_bias)
        qkv = nx @ W_qkv
        q, k, v = (_heads(qkv[..., i * D_MODEL:(i + 1) * D_MODEL], B, L) for i in range(3))
        causal = jnp.tril(jnp.ones((L, L), jnp.bool_))[None, None]
        ctx = _attend(q, k, v, causal)
        attn = jnp.transpose(ctx, (0, 2, 1, 3)).reshape(B, L, D_MODEL) @ W_self_out
        x = x + attn
        nx = _ln(x, ln2_scale, ln2_bias)
        q = _heads(nx @ W_q, B, L)
        kv = encoder_output @ W_kv
        k = _heads(kv[..., :D_MODEL], B, Ls)
        v = _heads(kv[..., D_MODEL:], B, Ls)
        ctx = _attend(q, k, v, None)
        attn = jnp.transpose(ctx, (0, 2, 1, 3)).reshape(B, L, D_MODEL) @ W_cross_out
        x = x + attn
        nx = _ln(x, ln3_scale, ln3_bias)
        ffn = jax.nn.relu(nx @ W1 + b1) @ W2 + b2
        return x + ffn

    def _L1_xattn_ref(virtual_node, node_features, Wq, bq, Wk, bk, Wv, bv, Wf, bf, ln_gamma, ln_beta):
        import jax, jax.numpy as jnp
        import numpy as np
        D_MODEL = 128
        PROJ = 128
        LN_EPS = 1e-05
        gelu = lambda x: jax.nn.gelu(x, approximate=False)
        q = gelu(jnp.einsum('bqd,dp->bqp', virtual_node, Wq) + bq)
        k = gelu(jnp.einsum('bnd,dp->bnp', node_features, Wk) + bk)
        v = gelu(jnp.einsum('bnd,dp->bnp', node_features, Wv) + bv)
        scores = jnp.einsum('bqp,bnp->bqn', q, k)
        w = jax.nn.softmax(scores, axis=-1)
        attended = jnp.einsum('bqn,bnp->bqp', w, v)
        out = jnp.einsum('bqp,pd->bqd', attended, Wf) + bf
        x = out + virtual_node
        mu = jnp.mean(x, axis=-1, keepdims=True)
        var = jnp.mean(jnp.square(x - mu), axis=-1, keepdims=True)
        return (x - mu) * jax.lax.rsqrt(var + LN_EPS) * ln_gamma + ln_beta

    def _L2_xattn_ref(q, k, v, zero_mask, Wq, Wk, Wv, Wo, gamma, beta):
        import jax, jax.numpy as jnp
        import numpy as np
        D_MODEL = 128
        H = 16
        D_HEAD = D_MODEL // H
        EPS = 1e-05
        bs, seq_q, _ = q.shape
        seq_k = k.shape[1]
        residual = q
        qh = (q @ Wq.T).reshape(bs, seq_q, H, D_HEAD).transpose(0, 2, 1, 3)
        kh = (k @ Wk.T).reshape(bs, seq_k, H, D_HEAD).transpose(0, 2, 1, 3)
        vh = (v @ Wv.T).reshape(bs, seq_k, H, D_HEAD).transpose(0, 2, 1, 3)
        att = jnp.einsum('bhqd,bhkd->bhqk', qh, kh) / np.sqrt(D_HEAD)
        att = att + zero_mask * -1000000000.0
        att = jax.nn.softmax(att, axis=-1)
        ctx = jnp.einsum('bhqk,bhkd->bhqd', att, vh)
        ctx = ctx.transpose(0, 2, 1, 3).reshape(bs, seq_q, D_MODEL)
        out = ctx @ Wo.T
        out = out + residual
        mu = jnp.mean(out, axis=-1, keepdims=True)
        var = jnp.var(out, axis=-1, keepdims=True)
        out = (out - mu) * jax.lax.rsqrt(var + EPS) * gamma + beta
        return out

    def _L3_xattn_ref(target_hidden_states, hidden_states, trans_W, trans_b):
        import jax, jax.numpy as jnp
        import numpy as np
        HIDDEN_NUMS = 64
        scores = jnp.einsum('bsd,btd->bst', hidden_states, target_hidden_states)
        attn = jax.nn.softmax(scores, axis=-1)
        ti = jnp.einsum('bst,btd->bsd', attn, target_hidden_states)
        cat = jnp.concatenate([hidden_states, ti], axis=-1)
        hi_new = jnp.tanh(jnp.einsum('bsf,fd->bsd', cat, trans_W) + trans_b)
        return hi_new + hidden_states
    x = _L0_xattn_ref(x, ctx_1024, L0_xattn_W_qkv, L0_xattn_W_self_out, L0_xattn_W_q, L0_xattn_W_kv, L0_xattn_W_cross_out, L0_xattn_W1, L0_xattn_b1, L0_xattn_W2, L0_xattn_b2, L0_xattn_ln1_scale, L0_xattn_ln1_bias, L0_xattn_ln2_scale, L0_xattn_ln2_bias, L0_xattn_ln3_scale, L0_xattn_ln3_bias)
    x = _L1_xattn_ref(x, ctx_1024, L1_xattn_Wq, L1_xattn_bq, L1_xattn_Wk, L1_xattn_bk, L1_xattn_Wv, L1_xattn_bv, L1_xattn_Wf, L1_xattn_bf, L1_xattn_ln_gamma, L1_xattn_ln_beta)
    x = _L2_xattn_ref(x, ctx_1024, ctx_1024, mask_Bx1x1xS2_ff0, L2_xattn_Wq, L2_xattn_Wk, L2_xattn_Wv, L2_xattn_Wo, L2_xattn_gamma, L2_xattn_beta)
    x = _L3_xattn_ref(ctx_1024, x, L3_xattn_trans_W, L3_xattn_trans_b)
    return x

_drawn_inputs = setup_inputs


def setup_inputs(seed=0):
    import zlib

    import numpy as np

    out = dict(_drawn_inputs(seed))
    spreads = {'L0_xattn_b1': (0.0, 0.1),
     'L0_xattn_b2': (0.0, 0.1),
     'L0_xattn_ln1_scale': (1.0, 0.2),
     'L0_xattn_ln1_bias': (0.0, 0.1),
     'L0_xattn_ln2_scale': (1.0, 0.2),
     'L0_xattn_ln2_bias': (0.0, 0.492),
     'L0_xattn_ln3_scale': (1.0, 0.2),
     'L0_xattn_ln3_bias': (0.0, 0.1),
     'L1_xattn_ln_gamma': (1.0, 0.2),
     'L1_xattn_ln_beta': (0.0, 0.1),
     'L2_xattn_gamma': (1.0, 0.2),
     'L2_xattn_beta': (0.0, 0.1),
     'L3_xattn_trans_b': (0.0, 0.1)}
    factors = {'L1_xattn_bq': 6.342, 'L1_xattn_bk': 8.0, 'L1_xattn_bv': 5.307}
    for name, (base, spread) in spreads.items():
        noise = np.random.default_rng([zlib.crc32(name.encode()), seed]).standard_normal(out[name].shape)
        drawn = base * np.exp(spread * noise) if base else spread * noise
        out[name] = jnp.asarray(drawn.astype(out[name].dtype))
    for name, factor in factors.items():
        out[name] = (out[name] * factor).astype(out[name].dtype)
    return out
```

```python
from contextlib import ExitStack

import numpy as np
import concourse.bass as bass
from concourse import mybir
from concourse.alu_op_type import AluOpType as ALU

B, LQ, LK, D = 8, 256, 512, 128
NH, DH = 16, 8
NPAIR, NQUAD = NH // 2, NH // 4
QT, KT = LQ // 128, LK // 128
F = 512
GROUPS = 8
HB = 64
R_MAX, R_MASK = 48, 51
NEG = -1.0e9
Q_PARTS = (0, 0, 0, 1, 1, 2)
K_PARTS = (0, 1, 2, 0, 1, 0)
S_USES = {"s": 4, "c": 8, "d": 8}
ST_UNITS = {"s": 2, "c": 4, "d": 4}
KTS = {"s": 2, "c": 4, "d": 4}



def quad_slot(seq, s, nm, st, pv, side):
    lanes = []
    if nm:
        lanes.append([("NMT", *nm, 0)])
    if s:
        T, n, q = s
        lanes.append([("S", T, n, q, u) for u in range(S_USES[T])])
    if st:
        T, n, q = st
        lanes.append([("ST", T, n, q, u) for u in range(ST_UNITS[T])])
    if pv:
        T, n, q = pv
        lanes.append([("PV", T, n, q, 0)])
    lanes.append(list(side))
    marks = []
    for lane in lanes:
        for k, x in enumerate(lane):
            marks.append(((k + 0.5) / len(lane), len(marks), x))
    seq += [x for _, _, x in sorted(marks, key=lambda m: m[:2])]
    if s:
        seq.append(("NM", *s, 0))


def phase1(i):
    seq = []
    a, c, z = i + 1, i, i + 2
    side = [
        [("CL", 0, c, 0, 0), ("LNS", 1, a - 1, 0, 0), ("CT", 0, c, 0, 0), ("LNZ", 1, a - 1, 0, 0), ("LNT", 1, a - 1, 0, 0), ("K", "c", c, 0, 0)],
        [("Q", "c", c, 0, 0), ("KW", "c", c, 0, 0), ("QW", "c", c, 0, 0), ("XR", 0, a, 0, 0), ("XLN", 0, z, 0, 0)],
        [("KL", "c", c, 0, 0), ("QL", "c", c, 0, 0)],
        [("V", "c", c, 0, 0), ("OUTA", "c", c - 1, 0, 0), ("OUTA", "c", c - 1, 1, 0), ("OUTB", "c", c - 1, 0, 0), ("OUTC", "c", c - 1, 0, 0), ("LNS", 0, z, 0, 0), ("LNZ", 0, z, 0, 0)],
        [("LNT", 0, z, 0, 0), ("LNS", 2, c - 1, 0, 0), ("QK", "s", z, 0, 0), ("LNZ", 2, c - 1, 0, 0), ("LNT", 2, c - 1, 0, 0), ("QKW", "s", z, 0, 0), ("X1B", 0, c, 0, 0)],
        [("FF1", 0, c - 1, 0, 0), ("FF1", 0, c - 1, 1, 0), ("FF2", 0, c - 1, 0, 0)],
        [("QKL", "s", z, 0, 0)],
        [("V", "s", z, 0, 0), ("OUTA", "s", a, 0, 0), ("OUTA", "s", a, 1, 0), ("OUTB", "s", a, 0, 0), ("OUTC", "s", a, 0, 0)],
    ]
    stream = [("c", c - 1, 1), ("c", c - 1, 2), ("c", c - 1, 3)] + [("s", a, q) for q in range(4)] + [("c", c, q) for q in range(4)]
    for k in range(8):
        quad_slot(seq, stream[k + 3], stream[k + 2], stream[k + 1], stream[k], side[k])
    return seq


def phase2(i):
    seq = []

    def pre(T, m):
        return [
            [("XS", T, m, 0, 0), ("CL", 0, m, 0, 0), ("XT", T, m, 0, 0), ("CT", 0, m, 0, 0), ("G1", T, m, 0, 0), ("G1", T, m, 1, 0), ("G1", T, m, 2, 0)],
            [("L1S", T, m, 0, 0), ("L1S", T, m, 1, 0), ("K", T, m, 0, 0), ("KW", T, m, 0, 0), ("L1T", T, m, 0, 0), ("L1T", T, m, 1, 0), ("L1A", T, m, 0, 0), ("L1O", T, m, 0, 0), ("LNS", 3, m, 0, 0)],
            [("LNZ", 3, m, 0, 0), ("LNG", 3, m, 0, 0), ("YT", T, m, 0, 0), ("Q", T, m, 0, 0), ("QW", T, m, 0, 0)],
            [],
            [("KL", T, m, 0, 0), ("QL", T, m, 0, 0)],
            [("V", T, m, 0, 0)],
        ]

    def post(T, m):
        return [
            [("OUTA", T, m, 0, 0), ("OUTA", T, m, 1, 0), ("OUTB", T, m, 0, 0), ("OUTC", T, m, 0, 0), ("LNS", 4, m, 0, 0), ("CL3", T, m, 0, 0)],
            [("LNZ", 4, m, 0, 0), ("LNG", 4, m, 0, 0), ("CT3", T, m, 0, 0), ("Y2T", T, m, 0, 0), ("L3S", T, m, 0, 0), ("L3S", T, m, 1, 0), ("Y1B", T, m + 2, 0, 0)],
            [("L3N", T, m, 0, 0), ("L3T", T, m, 0, 0), ("L3T", T, m, 1, 0), ("L3A", T, m, 0, 0), ("L3H", T, m, 0, 0)],
        ]

    side = [[] for _ in range(8)]
    cb, db = 2 * i, 2 * i + 1
    pc, pd = pre("c", cb + 2), pre("d", db)
    for k, part in enumerate(pc):
        side[2 + k] += part
    for k, part in enumerate(pre("d", db + 2)[:2]):
        side[6 + k] += part
    for k, part in enumerate(pd[2:]):
        side[k] += part
    oc, od = post("c", cb), post("d", db - 2)
    side[7] += oc[0]
    for k, part in enumerate(post("c", cb - 2)[1:]):
        side[k] += part
    for k, part in enumerate(od):
        side[3 + k] += part
    stream = [("d", db - 2, 1), ("d", db - 2, 2), ("d", db - 2, 3)] + [("c", cb, q) for q in range(4)] + [("d", db, q) for q in range(4)]
    for k in range(8):
        quad_slot(seq, stream[k + 3], stream[k + 2], stream[k + 1], stream[k], side[k])
    return seq


def valid(step, phase):
    return 0 <= step[2] < B


MISC = {"NMT", "PV", "LNT", "QK", "K", "Q", "V", "OUTA", "OUTB", "OUTC", "CT", "FF1", "FF2", "WT", "XT", "G1", "L1S",
        "L1T", "L1A", "L1O", "YT", "CT3", "Y2T", "L3S", "L3T", "L3A", "L3H"}


class Counts:

    def __init__(self):
        self.misc = self.s = self.st = 0
        self.misc_used, self.misc_full = [0, 0], [0, 0]
        self.s_used, self.st_used = [0, 0], [0, 0]
        self.pt_used, self.mx_used = [0, 0], [0, 0]
        self.quads = {"s": 0, "c": 0, "d": 0}
        self.writes = {"s": 0, "k": 0, "q": 0}
        self.st_mark, self.done = {}, {}
        self.nT = {}
        self.last_nmt, self.last_load = {}, {}

    def resolve(self, step, phase):
        kind, T, n, q, u = step
        r = {"n": n}
        if phase == 2:
            r["j"] = n // 2
        key = (phase, T, n)
        if T in ("s", "c", "d") and kind in ("S", "NM", "NMT", "ST", "PV", "QL", "KL", "QKL", "V", "OUTA", "OUTB", "OUTC"):
            if key not in self.nT:
                self.nT[key] = self.quads[T]
                self.quads[T] += 1
            r["t"] = self.nT[key]
        if kind in MISC:
            b = self.misc % 2
            self.misc += 1
            r["bank"], r["free"] = b, self.misc_used[b]
            self.misc_used[b] += 1
            if kind != "PV":
                self.misc_full[b] += 1
                r["full"] = self.misc_full[b]
            self.done[(phase, kind, T, n, q)] = (b, self.misc_used[b])
        if kind == "S":
            b = self.s % 2
            self.s += 1
            r["bank"], r["free"] = b, self.s_used[b]
            self.s_used[b] += 1
            if u == 0:
                r["mx"] = self.mx_used[q % 2]
        if kind == "NM":
            r["s0"], r["s1"], r["mx"] = self.s_used[0], self.s_used[1], self.mx_used[q % 2]
            r["prev_b"], r["prev"] = self.last_nmt.get(q % 2, (0, 0))
        if kind == "NMT":
            r["mx"] = self.mx_used[q % 2]
            self.mx_used[q % 2] += 1
            self.last_nmt[q % 2] = self.done[(phase, "NMT", T, n, q)]
            self.done[(phase, "MX", T, n, q)] = (q % 2, self.mx_used[q % 2])
        if kind == "ST":
            b = self.st % 2
            self.st += 1
            r["bank"], r["free"] = b, self.st_used[b]
            self.st_used[b] += 1
            r["mx"] = self.done[(phase, "MX", T, n, q)][1]
            if u == 0:
                r["pt"] = self.pt_used[q % 2]
            if u == ST_UNITS[T] - 1:
                self.done[(phase, "EXP", T, n, q)] = tuple(self.st_used)
        if kind == "PV":
            self.pt_used[q % 2] += 1
            r["pt"] = self.pt_used[q % 2]
            r["st0"], r["st1"] = self.done[(phase, "EXP", T, n, q)]
        if kind in ("QK", "K", "Q"):
            w = {"QK": "s", "K": "k", "Q": "q"}[kind]
            r["w"] = self.writes[w]
            self.writes[w] += 1
            self.nT[(phase, "w", w, T, n)] = r["w"]
        if kind in ("QKW", "QKL", "KW", "KL", "QW", "QL"):
            r["w"] = self.nT[(phase, "w", {"QK": "s", "K": "k", "Q": "q"}[kind[:-1]], T, n)]
        if kind in ("QKW", "KW", "QW"):
            r["ldT_b"], r["ld"] = self.last_load.get(kind[:-1], (0, 0))
        if kind in ("QKL", "KL", "QL"):
            self.last_load[kind[:-1]] = ("scd".index(T), 32 * (r["t"] + 1))
            before = self.last_exp(T)
            r["e0"], r["e1"] = before
        ins = self.inputs(step, phase)
        for name, src in ins.items():
            r[name + "_b"], r[name] = self.done.get(src, (0, 0))
        return r

    def last_exp(self, T):
        best = (0, 0)
        for k, v in self.done.items():
            if k[1] == "EXP" and (k[2] == "c") == (T == "c"):
                best = max(best, v)
        return best

    def inputs(self, step, phase):
        kind, T, n, q, u = step
        p = phase
        if kind == "QK":
            return {"in": (p, "LNT", 0, n, 0)}
        if kind == "Q":
            return {"in": (p, "LNT", 1, n, 0)} if p == 1 else {"in": (p, "YT", T, n, 0)}
        if kind == "V":
            return {"in": (p, "LNT", 0, n, 0)} if T == "s" else {"in": (p, "CT", 0, n, 0)}
        if kind == "K":
            return {"in": (p, "CT", 0, n, 0)}
        if kind == "PV":
            return {"v": (p, "V", T, n, 0)}
        if kind == "OUTA":
            return {"in": (p, "PV", T, n, 3)}
        if kind == "OUTB":
            return {"in": (p, "OUTA", T, n, 1)}
        if kind == "OUTC":
            return {"in": (p, "OUTB", T, n, 0)}
        if kind == "LNS":
            src = {1: (1, "OUTC", "s", n, 0), 2: (1, "OUTC", "c", n, 0), 3: (2, "L1O", "cd"[n % 2], n, 0), 4: (2, "OUTC", "cd"[n % 2], n, 0)}.get(T)
            return {"in": src} if src else {}
        if kind == "X1B":
            return {"in": (1, "OUTC", "s", n, 0), "prev": (1, "OUTC", "c", n - 1, 0)}
        if kind == "Y1B":
            return {"prev": (2, "OUTC", T, n - 2, 0)}
        if kind == "FF1":
            return {"in": (p, "LNT", 2, n, 0)}
        if kind == "FF2":
            return {"in": (p, "FF1", 0, n, 1)}
        if kind == "CL":
            return {"prev": (p, "CT", 0, n - 1, 0)} if p == 1 or n else {"prev": (1, "CT", 0, B - 1, 0)}
        if kind == "XR":
            return {"prev": (1, "OUTC", "s", n - 1, 0)}
        if kind == "XS":
            return {"prev": (p, "L1O", "dc"[n % 2], n - 1, 0)}
        if kind == "G1":
            return {"in": (p, "XT", T, n, 0), "in2": (p, "CT", 0, n, 0)}
        if kind == "L1S":
            return {"in": (p, "G1", T, n, 1)}
        if kind == "L1T":
            return {"in": (p, "L1S", T, n, q)}
        if kind == "L1A":
            return {"in": (p, "L1T", T, n, 1)}
        if kind == "L1O":
            return {"in": (p, "L1A", T, n, 0), "ex": (p, "L1S", T, n, 1)}
        if kind == "L3S":
            return {"in": (p, "Y2T", T, n, 0), "in2": (p, "CT3", T, n, 0)}
        if kind == "L3N":
            return {"in": (p, "L3S", T, n, 1), "in2": (p, "L3S", T, n, 0)}
        if kind == "L3A":
            return {"in": (p, "L3T", T, n, 1)}
        if kind == "L3H":
            return {"in": (p, "L3A", T, n, 0)}
        return {}


def build_schedule():
    counts = Counts()
    its = []
    for phase, fn, lo, hi in ((1, phase1, -2, B + 1), (2, phase2, -2, B // 2 + 1)):
        for i in range(lo, hi):
            steps = [s for s in fn(i) if valid(s, phase)]
            if phase == 1 and i == lo:
                steps = [("WT", 0, 0, 0, 0)] + steps
            its.append((phase, i, [(s, counts.resolve(s, phase)) for s in steps]))
    parts, k = [], 0
    while k < len(its):
        run = 1

        def shape(it):
            return [(s[0], s[1], s[3], s[4], sorted(r)) for s, r in it[2]]

        def diff(x, y):
            return [r1[v] - r0[v] for (_, r0), (_, r1) in zip(x[2], y[2]) for v in sorted(r0)]

        while k + run < len(its) and its[k + run][0] == its[k][0] and shape(its[k + run]) == shape(its[k]):
            if run >= 2 and diff(its[k + run - 1], its[k + run]) != diff(its[k], its[k + 1]):
                break
            run += 1
        first = its[k][2]
        second = its[k + 1][2] if run > 1 else first
        banks = all(r0[x] == r1[x] for (_, r0), (_, r1) in zip(first, second) for x in r0 if x == "bank" or x.endswith("_b"))
        if run < 2 or not banks:
            run = 1
            second = first
        parts.append((its[k][0], run, [(s, {x: (r0[x], r1[x] - r0[x]) for x in r0}) for (s, r0), (_, r1) in zip(first, second)]))
        k += run
    return parts


def program(nc, a, out):
    f32, bf16 = mybir.dt.float32, mybir.dt.bfloat16
    ACT = mybir.ActivationFunctionType
    X = mybir.AxisListType.X
    parts = build_schedule()

    with ExitStack() as ctx:
        def sb(name, shape, dt=f32):
            return ctx.enter_context(nc.sbuf_tensor(name, shape, dt))

        def sem(name):
            return ctx.enter_context(nc.semaphore(name))

        def row(name, n):
            return a[name].rearrange("(o n) -> o n", o=1).to_broadcast([128, n])

        ident, identb = sb("ident", [128, 128]), sb("identb", [128, 128], bf16)
        causal = sb("causal", [128, 2 * 128])
        ones1 = sb("ones1", [1, 128])
        half = sb("half", [128, 2])
        w_qkv, w_kv0 = sb("w_qkv", [128, 3 * D]), sb("w_kv0", [128, 2 * D])
        w_q0 = sb("w_q0", [128, D])
        wqp = {"s": sb("wqp_s", [128, D]), 1: sb("wqp_1", [128, D]), 2: sb("wqp_2", [128, D])}
        wkp = {"s": sb("wkp_s", [128, D]), 1: sb("wkp_1", [128, D]), 2: sb("wkp_2", [128, D])}
        wv2, wo2 = sb("wv2", [128, D]), sb("wo2", [128, D])
        w_so, w_co = sb("w_so", [128, D]), sb("w_co", [128, D])
        w1, w2 = sb("w1", [128, F]), sb("w2", [128, F // 128, D])
        b1 = sb("b1", [128, F // 128])
        b2 = sb("b2", [1, D])
        lng, lnb = sb("lng", [128, 3]), sb("lnb", [128, 3])
        l1w = sb("l1w", [128, 4, D])
        l1b = sb("l1b", [128, 2])
        bv4 = sb("bv4", [1, KT, D])
        bfb = sb("bfb", [128, D])
        gb = {3: (sb("g3", [128, D]), sb("be3", [128, D])), 4: (sb("g4", [128, D]), sb("be4", [128, D]))}
        tw = sb("tw", [128, 2, D])
        tbb = sb("tbb", [128, D])

        QA = {T: sb(f"QA_{T}", [128, NPAIR, 2, LQ], bf16) for T in "cd"}
        KA = {T: sb(f"KA_{T}", [128, NPAIR, LK], bf16) for T in "cd"}
        V1 = {T: sb(f"V1_{T}", [128, KT, NH, 32]) for T in "cd"}
        CT = {T: sb(f"CT_{T}", [128, NQUAD, LQ]) for T in "cd"}
        for of in (QA, KA, V1, CT):
            of["s"] = of["d"]
        nk = {"s": LQ, "c": LK, "d": LK}
        PT = [sb(f"PT{k}", [128, 4, 2, 512]) for k in range(2)]
        first, second = PT[0][:, :, :, :].rearrange("k a b n -> k (a b n)"), PT[1][:, :, :, :].rearrange("k a b n -> k (a b n)")
        kone = first[0:16, 0:2048].bitcast(bf16).rearrange("r (p n) -> r p n", p=NPAIR)
        qone = first[0:16, 2048:3072].bitcast(bf16).rearrange("r (p n) -> r p n", p=NPAIR)
        mk, mkr = second[0:B, 0:LK], second[0:B, LK:2 * LK]
        mkp = second[0:B, 2 * LK:2 * LK + 3 * LK // 2].bitcast(bf16).rearrange("b (t n) -> b t n", t=3)
        w2raw = second[:, 2048:2048 + 4 * D].rearrange("k (t n) -> k t n", t=4)
        mx = [sb(f"mx{k}", [128, QT, 2, 2]) for k in range(2)]
        ng = [sb(f"ng{k}", [128, QT, 2, 2]) for k in range(2)]
        nr = [sb(f"nr{k}", [128, QT, 2, 2]) for k in range(2)]
        nms = [sb(f"nms{k}", [128, QT, 2, 3, 2], bf16) for k in range(2)]
        nmt = [sb(f"nmt{k}", [12, LQ], bf16) for k in range(2)]
        junk = sb("junk", [128, 2, 384], bf16)
        width = {"s": 2 * LQ, "k": LK, "q": LQ}
        full32 = {w: sb(f"f32_{w}", [128, width[w]]) for w in "skq"}
        rest32 = {w: sb(f"r32_{w}", [128, width[w]]) for w in "skq"}
        split = {w: sb(f"split_{w}", [128, 3, width[w]], bf16) for w in "skq"}
        rr = sb("rr", [128, QT, NQUAD, 4])
        cn, cnT = sb("cn", [128, QT, D]), sb("cnT", [128, LQ])

        xln, xr, x1, x1b, x2, x3 = (sb(n, [128, QT, D]) for n in ("xln", "xr", "x1", "x1b", "x2", "x3"))
        bst = sb("bst", [128, QT, 6])
        mv = [sb(f"mv{w}", [128, QT, 2]) for w in range(5)]
        ve = [sb(f"ve{w}", [128, QT]) for w in range(5)]
        rstd = [sb(f"rstd{w}", [128, QT]) for w in range(5)]
        zt = [sb(f"zt{w}", [128, QT, D]) for w in range(5)]
        nxT = [sb(f"nxT{w}", [128, LQ]) for w in range(3)]
        hT = sb("hT", [128, F // 128, LQ])
        cin, cin3 = sb("cin", [128, KT, D]), sb("cin3", [128, KT, D])
        ctxT = {T: sb(f"ctxT_{T}", [128, LK]) for T in "cd"}
        ctxT3 = sb("ctxT3", [128, LK])
        xl1, xb1, xo1 = (sb(n, [128, QT, D]) for n in ("xl1", "xb1", "xo1"))
        xT1, q1T, k1T, v1 = sb("xT1", [128, LQ]), sb("q1T", [128, LQ]), sb("k1T", [128, LK]), sb("v1", [128, KT, D])
        nm1, rs1, rr1 = sb("nm1", [128, QT]), sb("rs1", [128, QT]), sb("rr1", [128, QT])
        P1, P1T, attT = sb("P1", [128, QT, LK]), sb("P1T", [128, KT, LQ]), sb("attT", [128, LQ])
        y1 = {T: sb(f"y1_{T}", [128, QT, D]) for T in "cd"}
        yT1 = sb("yT1", [128, LQ])
        y1b = {T: sb(f"y1b_{T}", [128, QT, D]) for T in "cd"}
        xo2, y2, y2T = sb("xo2", [128, QT, D]), sb("y2", [128, QT, D]), sb("y2T", [128, LQ])
        nm3, rs3, rr3 = sb("nm3", [128, QT]), sb("rs3", [128, QT]), sb("rr3", [128, QT])
        P3, P3T, tiT = sb("P3", [128, QT, LK]), sb("P3T", [128, KT, LQ]), sb("tiT", [128, LQ])
        hb, ob = sb("hb", [128, QT, D]), sb("ob", [128, QT, D])

        PS = [ctx.enter_context(nc.psum_tensor(f"PS{k}", [128, 512], f32)) for k in range(2)]
        PST = [ctx.enter_context(nc.psum_tensor(f"PST{k}", [128, 1024], f32)) for k in range(2)]
        PM = [ctx.enter_context(nc.psum_tensor(f"PM{k}", [128, 512], f32)) for k in range(2)]

        scr = {w: nc.dram_tensor(f"scr_{w}", [GROUPS, 128, n], bf16).ap() for w, n in (("sq", LQ), ("sk", LQ), ("q", LQ), ("k", LK))}
        mscr = nc.dram_tensor("mscr", [B, 3, LK], bf16).ap()
        xs = nc.dram_tensor("xs", [B, 128, QT, D], f32).ap()

        s_full, s_free = [sem(f"s_full{k}") for k in range(2)], [sem(f"s_free{k}") for k in range(2)]
        st_full, st_free = [sem(f"st_full{k}") for k in range(2)], [sem(f"st_free{k}") for k in range(2)]
        m_full, m_free = [sem(f"m_full{k}") for k in range(2)], [sem(f"m_free{k}") for k in range(2)]
        pv_done = [sem(f"pv_done{k}") for k in range(2)]
        nm_split = [sem(f"nm_split{k}") for k in range(2)]
        nm_in = [sem(f"nm_in{k}") for k in range(2)]
        causal_cut = sem("causal_cut")
        q_in = {T: sem(f"q_in_{T}") for T in "scd"}
        k_in = {T: sem(f"k_in_{T}") for T in "scd"}
        split_done = {w: sem(f"split_done_{w}") for w in "skq"}
        scr_in = {w: sem(f"scr_in_{w}") for w in "skq"}
        stats = [sem(f"stats{w}") for w in range(5)]
        rstd_ok = [sem(f"rstd_ok{w}") for w in range(5)]
        z_ok = [sem(f"z_ok{w}") for w in range(5)]
        y_ok = {3: sem("y_ok3"), 4: sem("y_ok4")}
        x_in, xr_in, c_in, xs_in, c3_in = sem("x_in"), sem("xr_in"), sem("c_in"), sem("xs_in"), sem("c3_in")
        x1b_ok, xb_ok, y1b_ok = sem("x1b_ok"), sem("xb_ok"), {T: sem(f"y1b_ok_{T}") for T in "cd"}
        xs_out = sem("xs_out")
        nm1_ok, nm3_ok = sem("nm1_ok"), sem("nm3_ok")
        rr3_ok, p3_ok = sem("rr3_ok"), sem("p3_ok")
        th_ok, ob_ok, out_ok = sem("th_ok"), sem("ob_ok"), sem("out_ok")
        mask_in = sem("mask_in")
        w_in, id_ok, setup_v, setup_p, scr_const, mscr_ok = (sem(n) for n in ("w_in", "id_ok", "setup_v", "setup_p", "scr_const", "mscr_ok"))
        chains = {e: sem(f"chain_{e}") for e in ("dve", "pool", "act")}

        class Chain:

            def __init__(self, eng, name):
                self.eng, self.sem, self.at = eng, chains[name], 0

            def __call__(self, ins):
                self.at += 1
                ins.then_inc(self.sem, 1)
                self.eng.wait_ge(self.sem, self.at)

            def restart(self):
                if self.at:
                    self.eng.sem_clear(self.sem)
                self.at = 0

        passed = sem("passed")

        def apart(eng):
            eng.sem_inc(passed, 1)

        def walk(eng, table, chain=None):
            for phase, times, steps in parts:
                mine = [(s, r) for s, r in steps if s[0] in table]
                if not mine:
                    continue
                if chain:
                    chain.restart()
                if times == 1:
                    for s, r in mine:
                        table[s[0]](s, {x: v[0] for x, v in r.items()}, phase)
                    continue
                with eng.Fori(0, times) as i:
                    for s, r in mine:
                        table[s[0]](s, {x: v[0] if v[1] == 0 else i * v[1] + v[0] for x, v in r.items()}, phase)
                    if chain:
                        chain.restart()

        W_LOADS = []

        def load(dst, src):
            W_LOADS.append((dst, src))

        load(w_qkv[:, :], a["L0_xattn_W_qkv"]); load(w_so[:, :], a["L0_xattn_W_self_out"])
        load(w_q0[:, :], a["L0_xattn_W_q"]); load(w_kv0[:, :], a["L0_xattn_W_kv"]); load(w_co[:, :], a["L0_xattn_W_cross_out"])
        load(w1[:, :], a["L0_xattn_W1"]); load(w2[:, :, :], a["L0_xattn_W2"].rearrange("(k p) n -> p k n", p=128))
        load(b1[:, :], a["L0_xattn_b1"].rearrange("(k p) -> p k", p=128)); load(b2[:, :], a["L0_xattn_b2"].rearrange("(o n) -> o n", o=1))
        for w in range(3):
            load(lng[:, w:w + 1], a[f"L0_xattn_ln{w + 1}_scale"].rearrange("(p o) -> p o", o=1))
            load(lnb[:, w:w + 1], a[f"L0_xattn_ln{w + 1}_bias"].rearrange("(p o) -> p o", o=1))
        for k, name in enumerate(("Wq", "Wk", "Wv", "Wf")):
            load(l1w[:, k, :], a[f"L1_xattn_{name}"])
        load(l1b[:, 0:1], a["L1_xattn_bq"].rearrange("(p o) -> p o", o=1))
        load(l1b[:, 1:2], a["L1_xattn_bk"].rearrange("(p o) -> p o", o=1))
        for kt in range(KT):
            load(bv4[:, kt, :], a["L1_xattn_bv"].rearrange("(o n) -> o n", o=1))
        load(bfb[:, :], row("L1_xattn_bf", D))
        load(gb[3][0][:, :], row("L1_xattn_ln_gamma", D)); load(gb[3][1][:, :], row("L1_xattn_ln_beta", D))
        load(gb[4][0][:, :], row("L2_xattn_gamma", D)); load(gb[4][1][:, :], row("L2_xattn_beta", D))
        for k, name in enumerate(("Wq", "Wk", "Wv", "Wo")):
            load(w2raw[:, k, :], a[f"L2_xattn_{name}"])
        load(tw[:, :, :], a["L3_xattn_trans_W"].rearrange("(k p) n -> p k n", p=128))
        load(tbb[:, :], row("L3_xattn_trans_b", D))
        load(mk, a["mask_Bx1x1xS2_ff0"].rearrange("b o c n -> b (o c n)"))
        N_W = 16 * len(W_LOADS)

        x_dram = a["x"].rearrange("b (t p) d -> b p t d", p=128)
        c_dram = a["ctx_1024"].rearrange("b (t p) d -> b p t d", p=128)
        o_dram = out.rearrange("b (t p) d -> b p t d", p=128)

        block = ctx.enter_context(nc.Block())

        @block.sync
        def _(sp):
            for dst, src in W_LOADS:
                sp.dma_start(dst, src, allow_slow_non_contiguous=dst.shape[0] == 128 and dst.shape[-1] == F // 128).then_inc(w_in, 16)
            sp.wait_ge(setup_p, 1)
            for name, src, n in (("sq", qone, LQ), ("q", qone, LQ), ("sk", kone, LQ), ("k", kone, LK)):
                for j in range(2):
                    dst = scr[name].rearrange("g (j i p) n -> j g i p n", j=2, p=8)[j, 6:8]
                    sp.dma_start(dst, src[:, :, 0:n]).then_inc(scr_const, 16)
            sp.wait_ge(setup_v, 1)
            sp.dma_start(mscr, mkp).then_inc(mscr_ok, 16)
            sp.wait_ge(scr_const, 16 * 8)
            sp.wait_ge(mscr_ok, 16)

            def put(w, name, src, groups, lo=0):
                g, k = groups[0], len(groups)
                sp.dma_start(scr[name][g:g + k].rearrange("g r n -> r g n"), src).then_inc(scr_in[w], 16)

            def put_q(w, name, n, off=0):
                put(w, name, split[w][:, 0:1, off:off + n].to_broadcast([128, 3, n]), (0, 1, 2))
                put(w, name, split[w][:, 1:2, off:off + n].to_broadcast([128, 2, n]), (3, 4))
                put(w, name, split[w][:, 2:3, off:off + n], (5,))

            def put_k(w, name, n, off=0):
                put(w, name, split[w][:, 0:3, off:off + n], (0, 1, 2))
                put(w, name, split[w][:, 0:2, off:off + n], (3, 4))
                put(w, name, split[w][:, 0:1, off:off + n], (5,))

            def get_q(T, name, w):
                for j in range(2):
                    sp.dma_start(QA[T][HB * j:HB * j + HB, :, j, :],
                                 scr[name].rearrange("g (j i p) n -> j g i p n", j=2, p=8)[j]).then_inc(q_in[T], 16)

            def get_k(T, name, w):
                for j in range(2):
                    sp.dma_start(KA[T][HB * j:HB * j + HB, :, 0:nk[T]],
                                 scr[name].rearrange("g (j i p) n -> j g i p n", j=2, p=8)[j]).then_inc(k_in[T], 16)

            def scratch_free(w, r):
                sp.wait_ge(split_done[w], r["w"] + 1)
                apart(sp)
                T = "scd"[r["ldT_b"]]
                sp.wait_ge((q_in if w == "q" else k_in)[T], r["ld"])
                apart(sp)
                if w == "s":
                    sp.wait_ge(q_in[T], r["ld"])
                    apart(sp)

            def step_xln(s, r, p):
                sp.wait_ge(z_ok[0], r["n"])
                apart(sp)
                sp.dma_start(xln[:, :, :], x_dram[r["n"]]).then_inc(x_in, 16)

            def step_xr(s, r, p):
                sp.wait_ge(m_free[r["prev_b"]], r["prev"])
                apart(sp)
                sp.dma_start(xr[:, :, :], x_dram[r["n"]]).then_inc(xr_in, 16)

            def step_cl(s, r, p):
                sp.wait_ge(m_free[r["prev_b"]], r["prev"])
                apart(sp)
                sp.dma_start(cin[:, :, :], c_dram[r["n"]]).then_inc(c_in, 16)

            def step_cl3(s, r, p):
                sp.wait_ge(ob_ok, r["n"])
                apart(sp)
                sp.dma_start(cin3[:, :, :], c_dram[r["n"]]).then_inc(c3_in, 16)

            def step_xs(s, r, p):
                sp.wait_ge(xs_out, 16 * B)
                sp.wait_ge(m_free[r["prev_b"]], r["prev"])
                apart(sp)
                sp.dma_start(xl1[:, :, :], xs[r["n"]]).then_inc(xs_in, 16)

            def step_qkw(s, r, p):
                scratch_free("s", r)
                put_q("s", "sq", LQ)
                put_k("s", "sk", LQ, off=LQ)

            def step_qkl(s, r, p):
                sp.wait_ge(scr_in["s"], (r["w"] + 1) * 96)
                apart(sp)
                sp.wait_ge(st_free[0], r["e0"])
                apart(sp)
                sp.wait_ge(st_free[1], r["e1"])
                apart(sp)
                get_q("s", "sq", "s")
                get_k("s", "sk", "s")

            def step_kw(s, r, p):
                scratch_free("k", r)
                put_k("k", "k", LK)
                if p == 2:
                    for j in range(2):
                        dst = scr["k"].rearrange("g (j i p) n -> g j i p n", j=2, p=8)[6, j, 3:6]
                        sp.dma_start(dst, mscr[r["n"]].rearrange("t (o n) -> t o n", o=1).to_broadcast([3, 8, LK])).then_inc(mask_in, 16)

            def step_kl(s, r, p):
                sp.wait_ge(scr_in["k"], (r["w"] + 1) * 48)
                apart(sp)
                if p == 2:
                    sp.wait_ge(mask_in, (r["n"] + 1) * 32)
                    apart(sp)
                sp.wait_ge(st_free[0], r["e0"])
                apart(sp)
                sp.wait_ge(st_free[1], r["e1"])
                apart(sp)
                get_k(s[1], "k", "k")

            def step_qw(s, r, p):
                scratch_free("q", r)
                put_q("q", "q", LQ)

            def step_ql(s, r, p):
                sp.wait_ge(scr_in["q"], (r["w"] + 1) * 48)
                apart(sp)
                sp.wait_ge(st_free[0], r["e0"])
                apart(sp)
                sp.wait_ge(st_free[1], r["e1"])
                apart(sp)
                get_q(s[1], "q", "q")

            def step_nmt(s, r, p):
                T, q, par = s[1], s[3], s[3] % 2
                sp.wait_ge(m_free[r["bank"]], r["free"] + 1)
                apart(sp)
                for j in range(2):
                    sp.dma_start(QA[T][HB * j + R_MAX:HB * j + R_MAX + 3, 2 * q:2 * q + 2, j, :],
                                 nmt[par][6 * j:6 * j + 6, :]).then_inc(nm_in[par], 16)

            def step_ff2(s, r, p):
                sp.wait_ge(m_free[r["bank"]], r["free"] + 1)
                apart(sp)
                sp.dma_start(xs[r["n"]], x3[:, :, :]).then_inc(xs_out, 16)

            def step_l3h(s, r, p):
                sp.wait_ge(ob_ok, r["n"] + 1)
                apart(sp)
                sp.dma_start(o_dram[r["n"]], ob[:, :, :]).then_inc(out_ok, 16)

            walk(sp, {"XLN": step_xln, "XR": step_xr, "CL": step_cl, "CL3": step_cl3, "XS": step_xs, "QKW": step_qkw,
                      "QKL": step_qkl, "KW": step_kw, "KL": step_kl, "QW": step_qw, "QL": step_ql, "NMT": step_nmt,
                      "FF2": step_ff2, "L3H": step_l3h})
            sp.wait_ge(out_ok, 16 * B)

        @block.gpsimd
        def _(pool):
            chain = Chain(pool, "pool")
            pool.memset(kone, 0.0).then_inc(id_ok, 1)
            pool.memset(qone, 0.0).then_inc(id_ok, 1)
            pool.memset(ident[:, :], 0.0).then_inc(id_ok, 1)
            pool.memset(identb[:, :], 0.0).then_inc(id_ok, 1)
            pool.memset(causal[:, :], 0.0).then_inc(id_ok, 1)
            pool.memset(half[:, :], -0.5).then_inc(id_ok, 1)
            pool.wait_ge(id_ok, 6)
            for m in (ident, identb):
                chain(pool.affine_select(out=m[:, :], in_=m[:, :], compare_op=ALU.not_equal, fill=1.0, base=0,
                                         pattern=[[-1, 128]], channel_multiplier=1))
            chain(pool.affine_select(out=causal[:, 128:256], in_=causal[:, 128:256], compare_op=ALU.is_ge, fill=NEG, base=0,
                                     pattern=[[-1, 128]], channel_multiplier=1))
            chain(pool.affine_select(out=kone, in_=kone, compare_op=ALU.is_ge, fill=1.0, base=-3,
                                     pattern=[[0, NPAIR], [0, LK]], channel_multiplier=1))
            chain(pool.affine_select(out=qone, in_=qone, compare_op=ALU.is_ge, fill=1.0, base=-6,
                                     pattern=[[0, NPAIR], [0, LQ]], channel_multiplier=1))
            pool.affine_select(out=qone, in_=qone, compare_op=ALU.is_ge, fill=0.0, base=-3,
                               pattern=[[0, NPAIR], [0, LQ]], channel_multiplier=1).then_inc(setup_p, 1)
            pool.wait_ge(setup_p, 1)
            pool.wait_ge(w_in, N_W)

            def parts_of(w, r):
                chain(pool.tensor_tensor(rest32[w][:, :], full32[w][:, :], split[w][:, 0, :], ALU.subtract))
                chain(pool.tensor_copy(split[w][:, 1, :], rest32[w][:, :]))
                pool.tensor_tensor(split[w][:, 2, :], rest32[w][:, :], split[w][:, 1, :], ALU.subtract).then_inc(split_done[w], 1)

            def step_split(s, r, p):
                w = {"QK": "s", "K": "k", "Q": "q"}[s[0]]
                pool.wait_ge(m_free[r["bank"]], r["free"] + 1)
                apart(pool)
                parts_of(w, r)

            def step_nm(s, r, p):
                par = s[3] % 2
                pool.wait_ge(s_free[0], r["s0"])
                apart(pool)
                pool.wait_ge(s_free[1], r["s1"])
                apart(pool)
                pool.wait_ge(m_free[r["prev_b"]], r["prev"])
                apart(pool)
                chain(pool.tensor_scalar(ng[par][:, :, :, :], mx[par][:, :, :, :], -1.0, None, ALU.mult))
                chain(pool.tensor_copy(nms[par][:, :, :, 0, :], ng[par][:, :, :, :]))
                chain(pool.tensor_tensor(nr[par][:, :, :, :], ng[par][:, :, :, :], nms[par][:, :, :, 0, :], ALU.subtract))
                chain(pool.tensor_copy(nms[par][:, :, :, 1, :], nr[par][:, :, :, :]))
                pool.tensor_tensor(nms[par][:, :, :, 2, :], nr[par][:, :, :, :], nms[par][:, :, :, 1, :],
                                   ALU.subtract).then_inc(nm_split[par], 1)

            def step_st(s, r, p):
                if s[1] != "s":
                    return
                par, u = s[3] % 2, s[4]
                pool.wait_ge(st_free[r["bank"]], r["free"] + 1)
                apart(pool)
                d0 = PT[par][:, u, 0, :].rearrange("k (j n) -> k j n", j=2)[:, :, 0:128]
                d1 = PT[par][:, u, 1, 0:256].rearrange("k (j n) -> k j n", j=2)
                for k, d in enumerate((d0, d1)):
                    pool.affine_select(out=d, in_=d, compare_op=ALU.is_ge, fill=0.0, base=0,
                                       pattern=[[0, 2], [1, 128]], channel_multiplier=-1).then_inc(causal_cut, 1)

            def step_lns(s, r, p):
                w = s[1]
                pool.wait_ge(stats[w], r["n"] + 1)
                apart(pool)
                chain(pool.tensor_scalar(ve[w][:, :], mv[w][:, :, 1], 1e-6 if w < 3 else 1e-5, None, ALU.add))
                pool.tensor_tensor(rstd[w][:, :], ve[w][:, :], half[:, :], ALU.pow).then_inc(rstd_ok[w], 1)

            def step_x1b(s, r, p):
                pool.wait_ge(m_free[r["in_b"]], r["in"])
                apart(pool)
                pool.wait_ge(m_free[r["prev_b"]], r["prev"])
                apart(pool)
                pool.tensor_copy(x1b[:, :, :], x1[:, :, :]).then_inc(x1b_ok, 1)

            def step_y1b(s, r, p):
                pool.wait_ge(m_free[r["prev_b"]], r["prev"])
                apart(pool)
                pool.wait_ge(y_ok[3], r["n"] + 1)
                apart(pool)
                pool.tensor_copy(y1b[s[1]][:, :, :], y1[s[1]][:, :, :]).then_inc(y1b_ok[s[1]], 1)

            def step_xs(s, r, p):
                pool.wait_ge(xs_in, 16 * (r["n"] + 1))
                apart(pool)
                pool.wait_ge(m_free[r["prev_b"]], r["prev"])
                apart(pool)
                pool.tensor_tensor(xb1[:, :, :], xl1[:, :, :], bfb[:, :].rearrange("p (o n) -> p o n", o=1).to_broadcast([128, QT, D]),
                                   ALU.add).then_inc(xb_ok, 1)

            def step_lng(s, r, p):
                w = s[1]
                pool.wait_ge(z_ok[w], r["n"] + 1)
                apart(pool)
                if w == 3:
                    pool.wait_ge(y1b_ok["cd"[s[2] % 2]], r["j"])
                    apart(pool)
                T = "cd"[s[2] % 2]
                y = y1[T] if w == 3 else y2
                g, be = (t[:, :].rearrange("p (o n) -> p o n", o=1).to_broadcast([128, QT, D]) for t in gb[w])
                chain(pool.tensor_tensor(zt[w][:, :, :], zt[w][:, :, :], g, ALU.mult))
                pool.tensor_tensor(y[:, :, :], zt[w][:, :, :], be, ALU.add).then_inc(y_ok[w], 1)

            def step_l3n(s, r, p):
                pool.wait_ge(rr3_ok, r["n"] + 1)
                apart(pool)
                for st in range(QT):
                    ins = pool.tensor_scalar(P3[:, st, :], P3[:, st, :], rr3[:, st:st + 1], None, ALU.mult)
                ins.then_inc(p3_ok, 1)

            def step_l3h(s, r, p):
                pool.wait_ge(th_ok, r["n"] + 1)
                apart(pool)
                pool.wait_ge(out_ok, 16 * r["n"])
                apart(pool)
                pool.tensor_tensor(ob[:, :, :], hb[:, :, :], y2[:, :, :], ALU.add).then_inc(ob_ok, 1)

            walk(pool, {"QK": step_split, "K": step_split, "Q": step_split, "NM": step_nm, "ST": step_st, "LNS": step_lns,
                        "X1B": step_x1b, "Y1B": step_y1b, "XS": step_xs, "LNG": step_lng, "L3N": step_l3n, "L3H": step_l3h}, chain)

        @block.scalar
        def _(act):
            act.wait_ge(w_in, N_W)
            act.wait_ge(setup_v, 1)

            def step_st(s, r, p):
                T, q, u, par = s[1], s[3], s[4], s[3] % 2
                act.wait_ge(st_full[r["bank"]], r["free"] + 1)
                if u == 0:
                    act.wait_ge(pv_done[par], r["pt"])
                n = 1024 if T != "s" else 768
                act.activation(PT[par][:, u, :, :].rearrange("k t n -> k (t n)")[:, 0:n], PST[r["bank"]][:, 0:n],
                               ACT.Exp).then_inc(st_free[r["bank"]], 1)

            def step_lnt(s, r, p):
                act.wait_ge(m_full[r["bank"]], r["full"])
                bank, free = PM[r["bank"]], m_free[r["bank"]]
                w = s[1]
                act.activation(nxT[w][:, :], bank[:, 0:LQ], ACT.Identity, bias=lnb[:, w:w + 1], scale=lng[:, w:w + 1]).then_inc(free, 1)

            def step_split(s, r, p):
                w = {"QK": "s", "K": "k", "Q": "q"}[s[0]]
                act.wait_ge(m_full[r["bank"]], r["full"])
                bank, free = PM[r["bank"]], m_free[r["bank"]]
                act.wait_ge(split_done[w], r["w"])
                per = 96 if w == "s" else 48
                act.wait_ge(scr_in[w], r["w"] * per)
                act.activation(full32[w][:, :], bank[:, 0:width[w]], ACT.Copy)
                act.activation(split[w][:, 0, :], bank[:, 0:width[w]], ACT.Copy).then_inc(free, 1)

            def step_v(s, r, p):
                act.wait_ge(m_full[r["bank"]], r["full"])
                bank, free = PM[r["bank"]], m_free[r["bank"]]
                T = s[1]
                n = KTS[T] * D
                act.activation(V1[T][:, 0:KTS[T], :, 0:DH], bank[:, 0:n].rearrange("k (t h d) -> k t h d", h=NH, d=DH), ACT.Copy).then_inc(free, 1)

            def step_outb(s, r, p):
                act.wait_ge(m_full[r["bank"]], r["full"])
                act.activation(cnT[:, :], PM[r["bank"]][:, 0:LQ], ACT.Copy).then_inc(m_free[r["bank"]], 1)

            def step_ct3(s, r, p):
                act.wait_ge(m_full[r["bank"]], r["full"])
                act.activation(ctxT3[:, :], PM[r["bank"]][:, 0:LK], ACT.Copy).then_inc(m_free[r["bank"]], 1)

            def step_xt(s, r, p):
                act.wait_ge(m_full[r["bank"]], r["full"])
                act.activation(xT1[:, :], PM[r["bank"]][:, 0:LQ], ACT.Copy).then_inc(m_free[r["bank"]], 1)

            def step_yt(s, r, p):
                act.wait_ge(m_full[r["bank"]], r["full"])
                act.activation(yT1[:, :], PM[r["bank"]][:, 0:LQ], ACT.Copy).then_inc(m_free[r["bank"]], 1)

            def step_y2t(s, r, p):
                act.wait_ge(m_full[r["bank"]], r["full"])
                act.activation(y2T[:, :], PM[r["bank"]][:, 0:LQ], ACT.Copy).then_inc(m_free[r["bank"]], 1)

            def step_l1a(s, r, p):
                act.wait_ge(m_full[r["bank"]], r["full"])
                act.activation(attT[:, :], PM[r["bank"]][:, 0:LQ], ACT.Copy).then_inc(m_free[r["bank"]], 1)

            def step_l3a(s, r, p):
                act.wait_ge(m_full[r["bank"]], r["full"])
                act.activation(tiT[:, :], PM[r["bank"]][:, 0:LQ], ACT.Copy).then_inc(m_free[r["bank"]], 1)

            def step_ct(s, r, p):
                dst = ctxT["c" if p == 1 else "cd"[s[2] % 2]]
                act.wait_ge(m_full[r["bank"]], r["full"])
                act.activation(dst[:, :], PM[r["bank"]][:, :], ACT.Copy).then_inc(m_free[r["bank"]], 1)

            def step_ff1(s, r, p):
                act.wait_ge(m_full[r["bank"]], r["full"])
                bank, free = PM[r["bank"]], m_free[r["bank"]]
                for k in range(2):
                    blk = 2 * s[3] + k
                    ins = act.activation(hT[:, blk, :], bank[:, k * LQ:(k + 1) * LQ], ACT.Relu, bias=b1[:, blk:blk + 1])
                ins.then_inc(free, 1)

            def step_g1(s, r, p):
                act.wait_ge(m_full[r["bank"]], r["full"])
                bank, free = PM[r["bank"]], m_free[r["bank"]]
                if s[3] == 0:
                    act.activation(q1T[:, :], bank[:, 0:LQ], ACT.Gelu, bias=l1b[:, 0:1]).then_inc(free, 1)
                elif s[3] == 1:
                    act.activation(k1T[:, :], bank[:, :], ACT.Gelu, bias=l1b[:, 1:2]).then_inc(free, 1)
                else:
                    act.activation(v1[:, :, :].rearrange("k t d -> k (t d)"), bank[:, :], ACT.Gelu).then_inc(free, 1)

            def step_l1s(s, r, p):
                act.wait_ge(m_full[r["bank"]], r["full"])
                bank, free = PM[r["bank"]], m_free[r["bank"]]
                qt = s[3]
                act.wait_ge(nm1_ok, r["n"] * QT + qt + 1)
                act.activation(P1[:, qt, :], bank[:, :], ACT.Exp, bias=nm1[:, qt:qt + 1], accum_out=rs1[:, qt:qt + 1]).then_inc(free, 1)

            def step_l3s(s, r, p):
                act.wait_ge(m_full[r["bank"]], r["full"])
                bank, free = PM[r["bank"]], m_free[r["bank"]]
                act.wait_ge(nm3_ok, r["n"] * 2 + s[3] + 1)
                qt = s[3]
                act.activation(P3[:, qt, :], bank[:, :], ACT.Exp, bias=nm3[:, qt:qt + 1], accum_out=rs3[:, qt:qt + 1]).then_inc(free, 1)

            def step_l3h(s, r, p):
                act.wait_ge(m_free[r["bank"]], r["free"] + 1)
                act.activation(hb[:, :, :], hb[:, :, :], ACT.Tanh).then_inc(th_ok, 1)

            walk(act, {"ST": step_st, "LNT": step_lnt, "QK": step_split, "K": step_split, "Q": step_split, "V": step_v,
                       "OUTB": step_outb, "CT": step_ct, "CT3": step_ct3, "XT": step_xt,
                       "YT": step_yt, "Y2T": step_y2t, "L1A": step_l1a, "L3A": step_l3a,
                       "FF1": step_ff1, "G1": step_g1, "L1S": step_l1s, "L3S": step_l3s, "L3H": step_l3h})

        @block.vector
        def _(dve):
            chain = Chain(dve, "dve")
            for T in "cd":
                chain(dve.memset(V1[T][:, :, :, :], 0.0))
                chain(dve.memset(QA[T][:, :, :, :], 0.0))
                chain(dve.memset(V1[T][:, :, :, DH:DH + 1], 1.0))
            chain(dve.memset(ones1[:, :], 1.0))
            dve.wait_ge(w_in, N_W)
            chain(dve.tensor_scalar(mk, mk, NEG, None, ALU.mult))
            chain(dve.tensor_copy(mkp[:, 0, :], mk))
            chain(dve.tensor_tensor(mkr, mk, mkp[:, 0, :], ALU.subtract))
            chain(dve.tensor_copy(mkp[:, 1, :], mkr))
            chain(dve.tensor_tensor(mkp[:, 2, :], mkr, mkp[:, 1, :], ALU.subtract))
            scale = float(np.float32(1.0) / np.sqrt(np.float32(DH)))

            def permuted(dst, src, by):
                view = src.rearrange("k (p j i) -> k j i p", p=NPAIR, j=2)
                for j in range(2):
                    chain(dve.tensor_scalar(dst[:, 64 * j:64 * j + 64].rearrange("k (i p) -> k i p", p=NPAIR), view[:, j], by, None, ALU.mult))

            permuted(wqp["s"], w_qkv[:, 0:D], scale)
            permuted(wkp["s"], w_qkv[:, D:2 * D], 1.0)
            permuted(wqp[1], w_q0[:, :], scale)
            permuted(wkp[1], w_kv0[:, 0:D], 1.0)
            dve.memset(junk[:, :, :], 0.0).then_inc(setup_v, 1)

            def step_wt(s, r, p):
                dve.wait_ge(m_full[r["bank"]], r["full"])
                bank, free = PM[r["bank"]], m_free[r["bank"]]
                permuted(wqp[2], bank[:, 0:128], scale)
                permuted(wkp[2], bank[:, 128:256], 1.0)
                chain(dve.tensor_copy(wv2[:, :], bank[:, 256:384]))
                dve.tensor_copy(wo2[:, :], bank[:, 384:512]).then_inc(free, 1)

            def step_s(s, r, p):
                T, q, u, par = s[1], s[3], s[4], s[3] % 2
                bank, free = PS[r["bank"]], s_free[r["bank"]]
                if u == 0:
                    dve.wait_ge(nm_split[par], r["mx"])
                dve.wait_ge(s_full[r["bank"]], r["free"] + 1)
                if T == "s":
                    dve.sem_inc(passed, 1)
                    pp, j = u // 2, u % 2
                    dve.tensor_tensor_reduce(out=junk[:, r["bank"], 0:128], in0=bank[:, 0:128], in1=causal[:, 128:256], scale=1.0, scalar=-3.0e38,
                                             op0=ALU.add, op1=ALU.max, accum_out=mx[par][:, 0, j, pp:pp + 1])
                    dve.tensor_tensor_reduce(out=junk[:, r["bank"], 128:384], in0=bank[:, 128:384], in1=causal[:, :], scale=1.0, scalar=-3.0e38,
                                             op0=ALU.add, op1=ALU.max, accum_out=mx[par][:, 1, j, pp:pp + 1]).then_inc(free, 1)
                else:
                    pp, j, qt = u // 4, u // 2 % 2, u % 2
                    dve.reduce_max(mx[par][:, qt, j, pp:pp + 1], bank[:, :], X).then_inc(free, 1)

            def step_nmt(s, r, p):
                dve.wait_ge(m_full[r["bank"]], r["full"])
                bank, free = PM[r["bank"]], m_free[r["bank"]]
                par = s[3] % 2
                dve.wait_ge(nm_in[par], 32 * r["mx"])
                dve.tensor_copy(nmt[par][:, :], bank[0:12, 0:128].bitcast(bf16)).then_inc(free, 1)

            def step_pv(s, r, p):
                dve.wait_ge(pv_done[s[3] % 2], r["pt"])
                dve.tensor_copy(CT[s[1]][:, s[3], :], PM[r["bank"]][:, 0:LQ]).then_inc(m_free[r["bank"]], 1)

            def step_lns(s, r, p):
                w = s[1]
                src = {0: xln, 1: x1, 2: x2, 3: xo1, 4: xo2}[w]
                if w == 0:
                    dve.wait_ge(x_in, 16 * (r["n"] + 1))
                else:
                    dve.wait_ge(m_free[r["in_b"]], r["in"])
                for t in range(QT):
                    chain(dve.bn_stats(bst[:, t, :], src[:, t, :]))
                for t in range(QT):
                    ins = dve.bn_aggr(mv[w][:, t, :], bst[:, t, :])
                ins.then_inc(stats[w], 1)

            def step_lnz(s, r, p):
                w = s[1]
                src = {0: xln, 1: x1, 2: x2, 3: xo1, 4: xo2}[w]
                dve.wait_ge(rstd_ok[w], r["n"] + 1)
                if w >= 3:
                    dve.wait_ge(y_ok[w], r["n"])
                for t in range(QT):
                    ins = dve.tensor_scalar(zt[w][:, t, :], src[:, t, :], mv[w][:, t, 0:1], rstd[w][:, t:t + 1], ALU.subtract, ALU.mult)
                ins.then_inc(z_ok[w], 1)

            def step_outa(s, r, p):
                dve.wait_ge(m_full[r["bank"]], r["full"])
                bank, free = PM[r["bank"]], m_free[r["bank"]]
                v = bank[:, :].rearrange("q (g c r) -> q g c r", g=NQUAD, c=4)
                chain(dve.reciprocal(rr[:, s[3], :, :], v[:, :, :, DH]))
                dve.tensor_tensor(cn[:, s[3], :].rearrange("q (g c r) -> q g c r", g=NQUAD, c=4), v[:, :, :, 0:DH],
                                  rr[:, s[3], :, :].rearrange("q g (c o) -> q g c o", o=1).to_broadcast([128, NQUAD, 4, DH]), ALU.mult).then_inc(free, 1)

            def step_outc(s, r, p):
                dve.wait_ge(m_full[r["bank"]], r["full"])
                bank, free = PM[r["bank"]], m_free[r["bank"]]
                T = s[1]
                if T == "s":
                    dve.wait_ge(xr_in, 16 * (r["n"] + 1))
                    dve.wait_ge(x1b_ok, r["n"])
                    dst, res = x1, xr
                elif p == 1:
                    dve.wait_ge(x1b_ok, r["n"] + 1)
                    dst, res = x2, x1b
                else:
                    dve.wait_ge(y1b_ok[T], r["t"] + 1 - (8 if T == "c" else 0))
                    dst, res = xo2, y1b[T]
                dve.tensor_tensor(dst[:, :, :], bank[:, 0:LQ].rearrange("q (t d) -> q t d", t=QT), res[:, :, :], ALU.add).then_inc(free, 1)

            def step_ff2(s, r, p):
                dve.wait_ge(m_full[r["bank"]], r["full"])
                bank, free = PM[r["bank"]], m_free[r["bank"]]
                dve.wait_ge(xs_out, 16 * r["n"])
                dve.tensor_tensor(x3[:, :, :], bank[:, 0:LQ].rearrange("q (t d) -> q t d", t=QT), x2[:, :, :], ALU.add).then_inc(free, 1)

            def step_l1s(s, r, p):
                dve.wait_ge(m_full[r["bank"]], r["full"])
                bank, free = PM[r["bank"]], m_free[r["bank"]]
                dve.tensor_reduce(nm1[:, s[3]:s[3] + 1], bank[:, :], X, ALU.max, negate=True).then_inc(nm1_ok, 1)

            def step_l1t(s, r, p):
                dve.wait_ge(m_full[r["bank"]], r["full"])
                bank, free = PM[r["bank"]], m_free[r["bank"]]
                qt = s[3]
                dve.tensor_copy(P1T[:, :, qt * 128:qt * 128 + 128], bank[:, :].rearrange("k (t q) -> k t q", t=KT)).then_inc(free, 1)

            def step_l1o(s, r, p):
                dve.wait_ge(m_full[r["bank"]], r["full"])
                bank, free = PM[r["bank"]], m_free[r["bank"]]
                dve.wait_ge(m_free[r["ex_b"]], r["ex"])
                chain(dve.reciprocal(rr1[:, :], rs1[:, :]))
                dve.wait_ge(xb_ok, r["n"] + 1)
                for t in range(QT):
                    ins = dve.scalar_tensor_tensor(xo1[:, t, :], bank[:, t * D:(t + 1) * D], rr1[:, t:t + 1], xb1[:, t, :], ALU.mult, ALU.add)
                ins.then_inc(free, 1)

            def step_l3s(s, r, p):
                dve.wait_ge(m_full[r["bank"]], r["full"])
                bank, free = PM[r["bank"]], m_free[r["bank"]]
                dve.tensor_reduce(nm3[:, s[3]:s[3] + 1], bank[:, :], X, ALU.max, negate=True).then_inc(nm3_ok, 1)

            def step_l3n(s, r, p):
                dve.wait_ge(m_free[r["in_b"]], r["in"])
                dve.wait_ge(m_free[r["in2_b"]], r["in2"])
                dve.wait_ge(p3_ok, r["n"])
                dve.reciprocal(rr3[:, :], rs3[:, :]).then_inc(rr3_ok, 1)

            def step_l3t(s, r, p):
                dve.wait_ge(m_full[r["bank"]], r["full"])
                bank, free = PM[r["bank"]], m_free[r["bank"]]
                dve.tensor_copy(P3T[:, :, s[3] * 128:s[3] * 128 + 128], bank[:, :].rearrange("k (t q) -> k t q", t=KT)).then_inc(free, 1)

            def step_l3h(s, r, p):
                dve.wait_ge(m_full[r["bank"]], r["full"])
                bank, free = PM[r["bank"]], m_free[r["bank"]]
                dve.wait_ge(ob_ok, r["n"])
                dve.tensor_tensor(hb[:, :, :], bank[:, 0:LQ].rearrange("q (t d) -> q t d", t=QT),
                                  tbb[:, :].rearrange("p (o n) -> p o n", o=1).to_broadcast([128, QT, D]), ALU.add).then_inc(free, 1)

            walk(dve, {"WT": step_wt, "S": step_s, "NMT": step_nmt, "PV": step_pv, "LNS": step_lns, "LNZ": step_lnz, "OUTA": step_outa,
                       "OUTC": step_outc, "FF2": step_ff2, "L1S": step_l1s, "L1T": step_l1t, "L1O": step_l1o, "L3S": step_l3s,
                       "L3N": step_l3n, "L3T": step_l3t, "L3H": step_l3h}, chain)

        @block.tensor
        def _(pe):
            pe.wait_ge(setup_p, 1)
            pe.wait_ge(w_in, N_W)
            pe.wait_ge(setup_v, 1)

            def transposed(bank, blocks):
                for k, src in enumerate(blocks):
                    ins = pe.transpose(bank[:, 128 * k:128 * k + 128], src, ident[:, :])
                return ins

            def mm(out_, l, m, first=True, last=True):
                return pe.matmul(out_, l, m, start=first, stop=True, skip_group_check=True)

            def step_wt(s, r, p):
                pe.wait_ge(m_free[r["bank"]], r["free"])
                transposed(PM[r["bank"]], [w2raw[:, k, :] for k in range(4)]).then_inc(m_full[r["bank"]], 1)

            def step_s(s, r, p):
                T, q, u = s[1], s[3], s[4]
                if q == 0 and u == 0:
                    pe.wait_ge(q_in[T], 32 * (r["t"] + 1))
                    pe.wait_ge(k_in[T], 32 * (r["t"] + 1))
                pe.wait_ge(s_free[r["bank"]], r["free"])
                bank = PS[r["bank"]]
                if T == "s":
                    pr, j = 2 * q + u // 2, u % 2
                    mm(bank[:, 0:128], QA[T][:, pr, j, 0:128], KA[T][:, pr, 0:128])
                    ins = mm(bank[:, 128:384], QA[T][:, pr, j, 128:256], KA[T][:, pr, 0:LQ])
                else:
                    pr, j, qt = 2 * q + u // 4, u // 2 % 2, u % 2
                    ins = mm(bank[:, :], QA[T][:, pr, j, 128 * qt:128 * qt + 128], KA[T][:, pr, :])
                ins.then_inc(s_full[r["bank"]], 1)

            def step_nmt(s, r, p):
                par = s[3] % 2
                pe.wait_ge(nm_split[par], r["mx"] + 1)
                pe.wait_ge(m_free[r["bank"]], r["free"])
                bank, fullsem = PM[r["bank"]], m_full[r["bank"]]
                o = bank[0:12, 0:128].bitcast(bf16)
                for qt in range(QT):
                    ins = pe.transpose(o[:, 128 * qt:128 * qt + 128], nms[par][:, qt, :, :, :].rearrange("q j t p -> q (j t p)"), identb[:, :])
                ins.then_inc(fullsem, 1)

            def step_st(s, r, p):
                T, q, u, par = s[1], s[3], s[4], s[3] % 2
                pe.wait_ge(nm_in[par], 32 * r["mx"])
                pe.wait_ge(st_free[r["bank"]], r["free"])
                bank = PST[r["bank"]]
                if T == "s":
                    pr = 2 * q + u
                    mm(bank[:, 0:512], KA[T][:, pr, 0:128], QA[T][:, pr, :, :].rearrange("k j n -> k (j n)"))
                    ins = mm(bank[:, 512:768].rearrange("k (j n) -> k j n", j=2), KA[T][:, pr, 128:256], QA[T][:, pr, :, 128:256])
                else:
                    pr = 2 * q + u // 2
                    for k in range(2):
                        kt = 2 * (u % 2) + k
                        ins = mm(bank[:, 512 * k:512 * k + 512], KA[T][:, pr, 128 * kt:128 * kt + 128],
                                 QA[T][:, pr, :, :].rearrange("k j n -> k (j n)"))
                ins.then_inc(st_full[r["bank"]], 1)

            def step_pv(s, r, p):
                T, q, par = s[1], s[3], s[3] % 2
                pe.wait_ge(st_free[0], r["st0"])
                pe.wait_ge(st_free[1], r["st1"])
                if T == "s":
                    pe.wait_ge(causal_cut, r["t"] * 16 + 4 * (q + 1))
                if q == 0 and r["v_b"] != r["bank"]:
                    pe.wait_ge(m_free[r["v_b"]], r["v"])
                pe.wait_ge(m_free[r["bank"]], r["free"])
                bank, fullsem = PM[r["bank"]], m_full[r["bank"]]
                nkt = KTS[T]
                for kt in range(nkt):
                    for c in range(4):
                        pp, j = c // 2, c % 2
                        lhs = V1[T][:, kt, 4 * q + c, :]
                        if T == "s" and kt == 1:
                            o, rhs = bank[32 * c:32 * c + 32, 128:256], PT[par][:, pp, 1, 128 * j:128 * j + 128]
                        elif T == "s":
                            o, rhs = bank[32 * c:32 * c + 32, 0:256], PT[par][:, pp, 0, 256 * j:256 * j + 256]
                        else:
                            o, rhs = bank[32 * c:32 * c + 32, 0:256], PT[par][:, 2 * pp + kt // 2, kt % 2, 256 * j:256 * j + 256]
                        ins = pe.matmul(o, lhs, rhs, start=kt == 0, stop=True, skip_group_check=True)
                ins.then_inc(pv_done[par], 1)

            def step_lnt(s, r, p):
                w = s[1]
                pe.wait_ge(z_ok[w], r["n"] + 1)
                pe.wait_ge(m_free[r["bank"]], r["free"])
                transposed(PM[r["bank"]], [zt[w][:, t, :] for t in range(QT)]).then_inc(m_full[r["bank"]], 1)

            def step_qk(s, r, p):
                if r["in_b"] != r["bank"]:
                    pe.wait_ge(m_free[r["in_b"]], r["in"])
                pe.wait_ge(m_free[r["bank"]], r["free"])
                bank, fullsem = PM[r["bank"]], m_full[r["bank"]]
                mm(bank[:, 0:LQ], wqp["s"][:, :], nxT[0][:, :])
                mm(bank[:, LQ:2 * LQ], wkp["s"][:, :], nxT[0][:, :]).then_inc(fullsem, 1)

            def step_q(s, r, p):
                if r["in_b"] != r["bank"]:
                    pe.wait_ge(m_free[r["in_b"]], r["in"])
                pe.wait_ge(m_free[r["bank"]], r["free"])
                bank, fullsem = PM[r["bank"]], m_full[r["bank"]]
                mm(bank[:, 0:LQ], wqp[p][:, :], (nxT[1] if p == 1 else yT1)[:, :]).then_inc(fullsem, 1)

            def step_k(s, r, p):
                if r["in_b"] != r["bank"]:
                    pe.wait_ge(m_free[r["in_b"]], r["in"])
                pe.wait_ge(m_free[r["bank"]], r["free"])
                bank, fullsem = PM[r["bank"]], m_full[r["bank"]]
                mm(bank[:, :], wkp[p][:, :], ctxT[s[1]][:, :]).then_inc(fullsem, 1)

            def step_v(s, r, p):
                if r["in_b"] != r["bank"]:
                    pe.wait_ge(m_free[r["in_b"]], r["in"])
                pe.wait_ge(m_free[r["bank"]], r["free"])
                bank, fullsem = PM[r["bank"]], m_full[r["bank"]]
                T = s[1]
                src = nxT[0] if T == "s" else ctxT[T]
                w = w_qkv[:, 2 * D:3 * D] if T == "s" else (w_kv0[:, D:2 * D] if p == 1 else wv2[:, :])
                for t in range(KTS[T]):
                    ins = mm(bank[:, D * t:D * t + D], src[:, 128 * t:128 * t + 128], w)
                ins.then_inc(fullsem, 1)

            def step_outa(s, r, p):
                if r["in_b"] != r["bank"]:
                    pe.wait_ge(m_free[r["in_b"]], r["in"])
                qt = s[3]
                pe.wait_ge(m_free[r["bank"]], r["free"])
                transposed(PM[r["bank"]], [CT[s[1]][:, g, 128 * qt:128 * qt + 128] for g in range(NQUAD)]).then_inc(m_full[r["bank"]], 1)

            def step_outb(s, r, p):
                if r["in_b"] != r["bank"]:
                    pe.wait_ge(m_free[r["in_b"]], r["in"])
                pe.wait_ge(m_free[r["bank"]], r["free"])
                transposed(PM[r["bank"]], [cn[:, t, :] for t in range(QT)]).then_inc(m_full[r["bank"]], 1)

            def step_outc(s, r, p):
                if r["in_b"] != r["bank"]:
                    pe.wait_ge(m_free[r["in_b"]], r["in"])
                pe.wait_ge(m_free[r["bank"]], r["free"])
                bank, fullsem = PM[r["bank"]], m_full[r["bank"]]
                w = w_so if s[1] == "s" else (w_co if p == 1 else wo2)
                for t in range(QT):
                    ins = mm(bank[:, D * t:D * t + D], cnT[:, 128 * t:128 * t + 128], w[:, :])
                ins.then_inc(fullsem, 1)

            def step_ct(s, r, p):
                pe.wait_ge(c_in, 16 * (r["n"] + 1 + (B if p == 2 else 0)))
                pe.wait_ge(m_free[r["bank"]], r["free"])
                transposed(PM[r["bank"]], [cin[:, t, :] for t in range(KT)]).then_inc(m_full[r["bank"]], 1)

            def step_ff1(s, r, p):
                if r["in_b"] != r["bank"]:
                    pe.wait_ge(m_free[r["in_b"]], r["in"])
                pe.wait_ge(m_free[r["bank"]], r["free"])
                bank, fullsem = PM[r["bank"]], m_full[r["bank"]]
                for k in range(2):
                    blk = 2 * s[3] + k
                    ins = mm(bank[:, LQ * k:LQ * k + LQ], w1[:, 128 * blk:128 * blk + 128], nxT[2][:, :])
                ins.then_inc(fullsem, 1)

            def step_ff2(s, r, p):
                if r["in_b"] != r["bank"]:
                    pe.wait_ge(m_free[r["in_b"]], r["in"])
                pe.wait_ge(m_free[r["bank"]], r["free"])
                bank, fullsem = PM[r["bank"]], m_full[r["bank"]]
                for t in range(QT):
                    o = bank[:, D * t:D * t + D]
                    mm(o, ones1[:, :], b2[:, :], True, False)
                    for blk in range(F // 128):
                        ins = mm(o, hT[:, blk, 128 * t:128 * t + 128], w2[:, blk, :], False, blk == F // 128 - 1)
                ins.then_inc(fullsem, 1)

            def step_xt(s, r, p):
                pe.wait_ge(xs_in, 16 * (r["n"] + 1))
                pe.wait_ge(m_free[r["bank"]], r["free"])
                transposed(PM[r["bank"]], [xl1[:, t, :] for t in range(QT)]).then_inc(m_full[r["bank"]], 1)

            def step_g1(s, r, p):
                if r["in_b"] != r["bank"]:
                    pe.wait_ge(m_free[r["in_b"]], r["in"])
                if r["in2_b"] != r["bank"]:
                    pe.wait_ge(m_free[r["in2_b"]], r["in2"])
                pe.wait_ge(m_free[r["bank"]], r["free"])
                bank, fullsem = PM[r["bank"]], m_full[r["bank"]]
                if s[3] == 0:
                    ins = mm(bank[:, 0:LQ], l1w[:, 0, :], xT1[:, :])
                elif s[3] == 1:
                    ins = mm(bank[:, :], l1w[:, 1, :], ctxT[s[1]][:, :])
                else:
                    mm(bank[:, :], ones1[:, :], bv4[:, :, :].rearrange("o t d -> o (t d)"), True, False)
                    for t in range(KT):
                        ins = pe.matmul(bank[:, D * t:D * t + D], ctxT[s[1]][:, 128 * t:128 * t + 128], l1w[:, 2, :], start=False, stop=True,
                                        skip_group_check=True)
                ins.then_inc(fullsem, 1)

            def step_l1s(s, r, p):
                if r["in_b"] != r["bank"]:
                    pe.wait_ge(m_free[r["in_b"]], r["in"])
                pe.wait_ge(m_free[r["bank"]], r["free"])
                bank, fullsem = PM[r["bank"]], m_full[r["bank"]]
                mm(bank[:, :], q1T[:, 128 * s[3]:128 * s[3] + 128], k1T[:, :]).then_inc(fullsem, 1)

            def step_l1t(s, r, p):
                if r["in_b"] != r["bank"]:
                    pe.wait_ge(m_free[r["in_b"]], r["in"])
                pe.wait_ge(m_free[r["bank"]], r["free"])
                transposed(PM[r["bank"]], [P1[:, s[3], 128 * t:128 * t + 128] for t in range(KT)]).then_inc(m_full[r["bank"]], 1)

            def step_l1a(s, r, p):
                if r["in_b"] != r["bank"]:
                    pe.wait_ge(m_free[r["in_b"]], r["in"])
                pe.wait_ge(m_free[r["bank"]], r["free"])
                bank, fullsem = PM[r["bank"]], m_full[r["bank"]]
                for t in range(KT):
                    ins = mm(bank[:, 0:LQ], v1[:, t, :], P1T[:, t, :], t == 0, t == KT - 1)
                ins.then_inc(fullsem, 1)

            def step_l1o(s, r, p):
                if r["in_b"] != r["bank"]:
                    pe.wait_ge(m_free[r["in_b"]], r["in"])
                pe.wait_ge(m_free[r["bank"]], r["free"])
                bank, fullsem = PM[r["bank"]], m_full[r["bank"]]
                for t in range(QT):
                    ins = mm(bank[:, D * t:D * t + D], attT[:, 128 * t:128 * t + 128], l1w[:, 3, :])
                ins.then_inc(fullsem, 1)

            def step_yt(s, r, p):
                pe.wait_ge(y_ok[3], r["n"] + 1)
                pe.wait_ge(m_free[r["bank"]], r["free"])
                transposed(PM[r["bank"]], [y1[s[1]][:, t, :] for t in range(QT)]).then_inc(m_full[r["bank"]], 1)

            def step_y2t(s, r, p):
                pe.wait_ge(y_ok[4], r["n"] + 1)
                pe.wait_ge(m_free[r["bank"]], r["free"])
                transposed(PM[r["bank"]], [y2[:, t, :] for t in range(QT)]).then_inc(m_full[r["bank"]], 1)

            def step_ct3(s, r, p):
                pe.wait_ge(c3_in, 16 * (r["n"] + 1))
                pe.wait_ge(m_free[r["bank"]], r["free"])
                transposed(PM[r["bank"]], [cin3[:, t, :] for t in range(KT)]).then_inc(m_full[r["bank"]], 1)

            def step_l3s(s, r, p):
                if r["in_b"] != r["bank"]:
                    pe.wait_ge(m_free[r["in_b"]], r["in"])
                if r["in2_b"] != r["bank"]:
                    pe.wait_ge(m_free[r["in2_b"]], r["in2"])
                pe.wait_ge(m_free[r["bank"]], r["free"])
                bank, fullsem = PM[r["bank"]], m_full[r["bank"]]
                mm(bank[:, :], y2T[:, 128 * s[3]:128 * s[3] + 128], ctxT3[:, :]).then_inc(fullsem, 1)

            def step_l3t(s, r, p):
                pe.wait_ge(p3_ok, r["n"] + 1)
                pe.wait_ge(m_free[r["bank"]], r["free"])
                transposed(PM[r["bank"]], [P3[:, s[3], 128 * t:128 * t + 128] for t in range(KT)]).then_inc(m_full[r["bank"]], 1)

            def step_l3a(s, r, p):
                if r["in_b"] != r["bank"]:
                    pe.wait_ge(m_free[r["in_b"]], r["in"])
                pe.wait_ge(m_free[r["bank"]], r["free"])
                bank, fullsem = PM[r["bank"]], m_full[r["bank"]]
                for t in range(KT):
                    ins = mm(bank[:, 0:LQ], cin3[:, t, :], P3T[:, t, :], t == 0, t == KT - 1)
                ins.then_inc(fullsem, 1)

            def step_l3h(s, r, p):
                if r["in_b"] != r["bank"]:
                    pe.wait_ge(m_free[r["in_b"]], r["in"])
                pe.wait_ge(m_free[r["bank"]], r["free"])
                bank, fullsem = PM[r["bank"]], m_full[r["bank"]]
                for t in range(QT):
                    mm(bank[:, D * t:D * t + D], y2T[:, 128 * t:128 * t + 128], tw[:, 0, :], True, False)
                    ins = mm(bank[:, D * t:D * t + D], tiT[:, 128 * t:128 * t + 128], tw[:, 1, :], False, True)
                ins.then_inc(fullsem, 1)

            walk(pe, {"WT": step_wt, "S": step_s, "NMT": step_nmt, "ST": step_st, "PV": step_pv, "LNT": step_lnt, "QK": step_qk,
                      "Q": step_q, "K": step_k, "V": step_v, "OUTA": step_outa, "OUTB": step_outb, "OUTC": step_outc, "CT": step_ct,
                      "FF1": step_ff1, "FF2": step_ff2, "XT": step_xt, "G1": step_g1, "L1S": step_l1s, "L1T": step_l1t,
                      "L1A": step_l1a, "L1O": step_l1o, "YT": step_yt, "Y2T": step_y2t, "CT3": step_ct3, "L3S": step_l3s,
                      "L3T": step_l3t, "L3A": step_l3a, "L3H": step_l3h})


_INS = ["x", "ctx_1024", "mask_Bx1x1xS2_ff0"] + [f"L0_xattn_{n}" for n in (
    "W_qkv", "W_self_out", "W_q", "W_kv", "W_cross_out", "W1", "b1", "W2", "b2", "ln1_scale", "ln1_bias", "ln2_scale",
    "ln2_bias", "ln3_scale", "ln3_bias")] + [f"L1_xattn_{n}" for n in (
        "Wq", "bq", "Wk", "bk", "Wv", "bv", "Wf", "bf", "ln_gamma", "ln_beta")] + [f"L2_xattn_{n}" for n in (
            "Wq", "Wk", "Wv", "Wo", "gamma", "beta")] + ["L3_xattn_trans_W", "L3_xattn_trans_b"]


def kernel(**inputs):
    import numpy as _np
    import concourse.bacc as _bacc
    from concourse import mybir as _mybir
    from concourse.bass_utils import run_bass_kernel_spmd as _run

    nc = _bacc.Bacc("TRN2", target_bir_lowering=False, num_devices=1)
    arrays, args = {}, {}
    for name in _INS:
        arr = _np.ascontiguousarray(inputs[name])
        arrays[f"in_{name}"] = arr
        args[name] = nc.dram_tensor(f"in_{name}", arr.shape, _mybir.dt.from_np(arr.dtype), kind="ExternalInput").ap()
    o = nc.dram_tensor("out_0", (B, LQ, D), _mybir.dt.float32, kind="ExternalOutput").ap()
    program(nc, args, o)
    r = _run(nc, [arrays], core_ids=[0])
    return r.results[0]["out_0"]
```

```python
from contextlib import ExitStack

import numpy as np
import concourse.bass as bass
from concourse import mybir
from concourse.alu_op_type import AluOpType as ALU

B, LQ, LK, D = 8, 256, 512, 128
NH, DH = 16, 8
NPAIR, NQUAD = NH // 2, NH // 4
QT, KT = LQ // 128, LK // 128
F = 512
GROUPS = 8
HB = 64
R_MAX, R_MASK = 48, 51
NEG = -1.0e9
Q_PARTS = (0, 0, 0, 1, 1, 2)
K_PARTS = (0, 1, 2, 0, 1, 0)
N_PS, N_PST, N_PM = 2, 3, 3
S_USES = {"s": 4, "c": 8, "d": 8}
ST_UNITS = {"s": 4, "c": 8, "d": 8}
KTS = {"s": 2, "c": 4, "d": 4}
TURN = "dc"
NMT_AT = (0.15, 0.15)



def all_slots():
    slots = {}

    def put(slot, p, *steps, span=(0.0, 1.0)):
        slots.setdefault(slot, []).append((span, [[(x, p) for x in (g if isinstance(g, list) else [g])] for g in steps]))

    def attention(base, p, T, n):
        for q in range(NQUAD):
            k = base + q
            put(k, p, *[("S", T, n, q, u) for u in range(S_USES[T])])
            put(k, p, ("NM", T, n, q, 0), span=(1.0, 1.0))
            put(k + 1, p, ("NMT", T, n, q, 0), span=NMT_AT)
            put(k + 2, p, *[("ST", T, n, q, u) for u in range(ST_UNITS[T])])
            put(k + 3, p, *[("PV", T, n, q, u) for u in range(KTS[T])])
            put(k + 3, p, ("PVC", T, n, q, 0), span=(1.0, 1.0))

    for n in range(B):
        s, c = 8 * n - 8, 8 * n
        put(s - 7, 1, ("XLN", 0, n, 0, 0))
        put(s - 5, 1, ("LNS", 0, n, 0, 0))
        put(s - 4, 1, ("LNZ", 0, n, 0, 0), ("LNT", 0, n, 0, 0), ("QK", "s", n, 0, 0), ("QKW", "s", n, 0, 0))
        put(s - 2, 1, ("QKL", "s", n, 0, 0))
        put(s - 1, 1, ("V", "s", n, 0, 0))
        attention(s, 1, "s", n)
        put(s + 1, 1, ("XR", 0, n, 0, 0))
        put(s + 4, 1, ("CL", 0, n, 0, 0))
        put(s + 7, 1, ("OUTA", "s", n, 0, 0), ("OUTA", "s", n, 1, 0), ("OUTB", "s", n, 0, 0), ("OUTC", "s", n, 0, 0))
        put(c, 1, ("LNS", 1, n, 0, 0), ("LNZ", 1, n, 0, 0))
        put(c, 1, ("CT", 0, n, 0, 0), ("K", "c", n, 0, 0))
        put(c + 1, 1, ("LNT", 1, n, 0, 0), ("KW", "c", n, 0, 0), ("Q", "c", n, 0, 0), ("QW", "c", n, 0, 0))
        put(c + 2, 1, ("KL", "c", n, 0, 0))
        put(c + 3, 1, ("QL", "c", n, 0, 0), ("V", "c", n, 0, 0))
        put(c + 4, 1, ("X1B", 0, n, 0, 0))
        attention(c + 4, 1, "c", n)
        put(c + 11, 1, ("OUTA", "c", n, 0, 0), ("OUTA", "c", n, 1, 0), ("OUTB", "c", n, 0, 0), ("OUTC", "c", n, 0, 0))
        put(c + 12, 1, ("LNS", 2, n, 0, 0), ("LNZ", 2, n, 0, 0), ("LNT", 2, n, 0, 0))
        put(c + 13, 1, ("FF1", 0, n, 0, 0), ("FF1", 0, n, 1, 0), ("FF2", 0, n, 0, 0))
    for m in range(B):
        k, T = 8 * B + 4 * m, TURN[m % 2]
        put(k - 7, 2, ("XS", T, m, 0, 0), ("CL", 0, m, 0, 0))
        put(k - 6, 2, ("XT", T, m, 0, 0), ("CT", 0, m, 0, 0), [("G1", T, m, u, 0) for u in range(3)])
        put(k - 5, 2, ("L1S", T, m, 0, 0), ("L1S", T, m, 1, 0), ("L1T", T, m, 0, 0), ("L1T", T, m, 1, 0), ("K", T, m, 0, 0))
        put(k - 4, 2, ("L1A", T, m, 0, 0), ("KW", T, m, 0, 0), ("L1O", T, m, 0, 0), ("LNS", 3, m, 0, 0), ("LNZ", 3, m, 0, 0), ("LNG", 3, m, 0, 0))
        put(k - 3, 2, ("YT", T, m, 0, 0), ("Q", T, m, 0, 0), ("QW", T, m, 0, 0))
        put(k - 2, 2, ("KL", T, m, 0, 0), ("QL", T, m, 0, 0))
        put(k - 1, 2, ("V", T, m, 0, 0))
        put(k, 2, ("Y1B", T, m, 0, 0))
        attention(k, 2, T, m)
        put(k + 7, 2, ("OUTA", T, m, 0, 0), ("OUTA", T, m, 1, 0), ("OUTB", T, m, 0, 0), ("OUTC", T, m, 0, 0))
        put(k + 8, 2, ("LNS", 4, m, 0, 0), ("CL3", T, m, 0, 0), ("LNZ", 4, m, 0, 0), ("LNG", 4, m, 0, 0))
        put(k + 9, 2, ("CT3", T, m, 0, 0), ("Y2T", T, m, 0, 0), ("L3S", T, m, 0, 0), ("L3S", T, m, 1, 0), ("L3N", T, m, 0, 0))
        put(k + 10, 2, ("L3T", T, m, 0, 0), ("L3T", T, m, 1, 0), ("L3A", T, m, 0, 0))
        put(k + 11, 2, ("L3H", T, m, 0, 0))
    put(-17, 1, ("WT", 0, 0, 0, 0))
    return slots


def in_order(lanes):
    marks = [(lo + (hi - lo) * (k + 0.5) / len(groups), n, k, g)
             for n, ((lo, hi), groups) in enumerate(lanes) for k, g in enumerate(groups)]
    return [x for *_, g in sorted(marks, key=lambda m: m[:3]) for x in g]


MISC = {"NMT", "PV", "LNT", "QK", "K", "Q", "V", "OUTA", "OUTB", "OUTC", "CT", "FF1", "FF2", "WT", "XT", "G1", "L1S",
        "L1T", "L1A", "L1O", "YT", "CT3", "Y2T", "L3S", "L3T", "L3A", "L3H"}


class Counts:

    def __init__(self):
        self.misc = self.s = self.st = 0
        self.misc_used, self.misc_full = [0] * N_PM, [0] * N_PM
        self.s_used, self.st_used = [0] * N_PS, [0] * N_PST
        self.pt_used, self.mx_used = [0, 0], [0, 0]
        self.quads = {"s": 0, "c": 0, "d": 0}
        self.writes = {"s": 0, "k": 0, "q": 0}
        self.st_mark, self.done = {}, {}
        self.nT = {}
        self.last_nmt, self.last_load = {}, {}

    def resolve(self, step, phase):
        kind, T, n, q, u = step
        r = {"n": n}
        if phase == 2:
            r["j"] = n // 2
        key = (phase, T, n)
        if T in ("s", "c", "d") and kind in ("S", "NM", "NMT", "ST", "PV", "QL", "KL", "QKL", "V", "OUTA", "OUTB", "OUTC"):
            if key not in self.nT:
                self.nT[key] = self.quads[T]
                self.quads[T] += 1
            r["t"] = self.nT[key]
        if kind == "PVC" or kind == "PV" and u:
            r["bank"], r["pt"] = N_PM - 1, self.pt_used[q % 2]
        elif kind in MISC:
            b = N_PM - 1 if kind == "PV" else self.misc % (N_PM - 1)
            self.misc += kind != "PV"
            r["bank"], r["free"] = b, self.misc_used[b]
            self.misc_used[b] += 1
            if kind != "PV":
                self.misc_full[b] += 1
                r["full"] = self.misc_full[b]
            self.done[(phase, kind, T, n, q)] = (b, self.misc_used[b])
        if kind == "S":
            b = self.s % N_PS
            self.s += 1
            r["bank"], r["free"] = b, self.s_used[b]
            self.s_used[b] += 1
            if u == 0:
                r["mx"] = self.mx_used[q % 2]
        if kind == "NM":
            r["s0"], r["s1"], r["mx"] = self.s_used[0], self.s_used[1], self.mx_used[q % 2]
            r["prev_b"], r["prev"] = self.last_nmt.get(q % 2, (0, 0))
        if kind == "NMT":
            r["mx"] = self.mx_used[q % 2]
            self.mx_used[q % 2] += 1
            self.last_nmt[q % 2] = self.done[(phase, "NMT", T, n, q)]
            self.done[(phase, "MX", T, n, q)] = (q % 2, self.mx_used[q % 2])
        if kind == "ST":
            b = self.st % N_PST
            self.st += 1
            r["bank"], r["free"] = b, self.st_used[b]
            self.st_used[b] += 1
            r["mx"] = self.done[(phase, "MX", T, n, q)][1]
            if u == 0:
                r["pt"] = self.pt_used[q % 2]
            if u == ST_UNITS[T] - 1:
                self.done[(phase, "EXP", T, n, q)] = tuple(self.st_used)
        if kind == "PV" and not u:
            self.pt_used[q % 2] += 1
            r["pt"] = self.pt_used[q % 2]
            r["st0"], r["st1"], r["st2"] = self.done[(phase, "EXP", T, n, q)]
        if kind in ("QK", "K", "Q"):
            w = {"QK": "s", "K": "k", "Q": "q"}[kind]
            r["w"] = self.writes[w]
            self.writes[w] += 1
            self.nT[(phase, "w", w, T, n)] = r["w"]
        if kind in ("QKW", "QKL", "KW", "KL", "QW", "QL"):
            r["w"] = self.nT[(phase, "w", {"QK": "s", "K": "k", "Q": "q"}[kind[:-1]], T, n)]
        if kind in ("QKW", "KW", "QW"):
            r["ldT_b"], r["ld"] = self.last_load.get(kind[:-1], (0, 0))
        if kind in ("QKL", "KL", "QL"):
            self.last_load[kind[:-1]] = ("scd".index(T), 32 * (r["t"] + 1))
            before = self.last_exp(T)
            r["e0"], r["e1"], r["e2"] = before
        ins = self.inputs(step, phase)
        for name, src in ins.items():
            r[name + "_b"], r[name] = self.done.get(src, (0, 0))
        return r

    def last_exp(self, T):
        best = (0,) * N_PST
        for k, v in self.done.items():
            if k[1] == "EXP" and (k[2] == "c") == (T == "c"):
                best = max(best, v)
        return best

    def inputs(self, step, phase):
        kind, T, n, q, u = step
        p = phase
        if kind == "QK":
            return {"in": (p, "LNT", 0, n, 0)}
        if kind == "Q":
            return {"in": (p, "LNT", 1, n, 0)} if p == 1 else {"in": (p, "YT", T, n, 0)}
        if kind == "V":
            return {"in": (p, "LNT", 0, n, 0)} if T == "s" else {"in": (p, "CT", 0, n, 0)}
        if kind == "K":
            return {"in": (p, "CT", 0, n, 0)}
        if kind == "PV" and not u:
            return {"v": (p, "V", T, n, 0)}
        if kind == "OUTA":
            return {"in": (p, "PV", T, n, 3)}
        if kind == "OUTB":
            return {"in": (p, "OUTA", T, n, 1)}
        if kind == "OUTC":
            return {"in": (p, "OUTB", T, n, 0)}
        if kind == "LNS":
            src = {1: (1, "OUTC", "s", n, 0), 2: (1, "OUTC", "c", n, 0), 3: (2, "L1O", TURN[n % 2], n, 0), 4: (2, "OUTC", TURN[n % 2], n, 0)}.get(T)
            return {"in": src} if src else {}
        if kind == "X1B":
            return {"in": (1, "OUTC", "s", n, 0), "prev": (1, "OUTC", "c", n - 1, 0)}
        if kind == "Y1B":
            return {"prev": (2, "OUTC", T, n - 2, 0)}
        if kind == "FF1":
            return {"in": (p, "LNT", 2, n, 0)}
        if kind == "FF2":
            return {"in": (p, "FF1", 0, n, 1)}
        if kind == "CL":
            return {"prev": (p, "CT", 0, n - 1, 0)} if p == 1 or n else {"prev": (1, "CT", 0, B - 1, 0)}
        if kind == "XR":
            return {"prev": (1, "OUTC", "s", n - 1, 0)}
        if kind == "XS":
            return {"prev": (p, "L1O", TURN[(n - 1) % 2], n - 1, 0)}
        if kind == "G1":
            return {"in": (p, "XT", T, n, 0), "in2": (p, "CT", 0, n, 0)}
        if kind == "L1S":
            return {"in": (p, "G1", T, n, 1)}
        if kind == "L1T":
            return {"in": (p, "L1S", T, n, q)}
        if kind == "L1A":
            return {"in": (p, "L1T", T, n, 1)}
        if kind == "L1O":
            return {"in": (p, "L1A", T, n, 0), "ex": (p, "L1S", T, n, 1)}
        if kind == "L3S":
            return {"in": (p, "Y2T", T, n, 0), "in2": (p, "CT3", T, n, 0)}
        if kind == "L3N":
            return {"in": (p, "L3S", T, n, 1), "in2": (p, "L3S", T, n, 0)}
        if kind == "L3A":
            return {"in": (p, "L3T", T, n, 1)}
        if kind == "L3H":
            return {"in": (p, "L3A", T, n, 0)}
        return {}


def build_schedule():
    counts = Counts()
    slots = all_slots()
    chunks = {}
    for slot in sorted(slots):
        chunks.setdefault(slot // 8, []).extend(in_order(slots[slot]))
    its = []
    for c in sorted(chunks):
        counts.misc = counts.s = counts.st = 0
        its.append([(s, counts.resolve(s, p), p) for s, p in chunks[c]])
    parts, k = [], 0
    while k < len(its):
        run = 1

        def shape(it):
            return [(s[0], s[1], s[3], s[4], sorted(r), p) for s, r, p in it]

        def diff(x, y):
            return [r1[v] - r0[v] for (_, r0, _), (_, r1, _) in zip(x, y) for v in sorted(r0)]

        while k + run < len(its) and shape(its[k + run]) == shape(its[k]):
            if run >= 2 and diff(its[k + run - 1], its[k + run]) != diff(its[k], its[k + 1]):
                break
            run += 1
        first = its[k]
        second = its[k + 1] if run > 1 else first
        banks = all(r0[x] == r1[x] for (_, r0, _), (_, r1, _) in zip(first, second) for x in r0 if x == "bank" or x.endswith("_b"))
        if run < 2 or not banks:
            run = 1
            second = first
        parts.append((run, [(s, {x: (r0[x], r1[x] - r0[x]) for x in r0}, p) for (s, r0, p), (_, r1, _) in zip(first, second)]))
        k += run
    return parts


def program(nc, a, out):
    f32, bf16 = mybir.dt.float32, mybir.dt.bfloat16
    ACT = mybir.ActivationFunctionType
    X = mybir.AxisListType.X
    parts = build_schedule()

    with ExitStack() as ctx:
        def sb(name, shape, dt=f32):
            return ctx.enter_context(nc.sbuf_tensor(name, shape, dt))

        def sem(name):
            return ctx.enter_context(nc.semaphore(name))

        def row(name, n):
            return a[name].rearrange("(o n) -> o n", o=1).to_broadcast([128, n])

        ident, identb = sb("ident", [128, 128]), sb("identb", [128, 128], bf16)
        causal = sb("causal", [128, 2 * 128])
        ones1 = sb("ones1", [1, 128])
        half = sb("half", [128, 2])
        w_qkv, w_kv0 = sb("w_qkv", [128, 3 * D]), sb("w_kv0", [128, 2 * D])
        w_q0 = sb("w_q0", [128, D])
        wqp = {"s": sb("wqp_s", [128, D]), 1: sb("wqp_1", [128, D]), 2: sb("wqp_2", [128, D])}
        wkp = {"s": sb("wkp_s", [128, D]), 1: sb("wkp_1", [128, D]), 2: sb("wkp_2", [128, D])}
        wv2, wo2 = sb("wv2", [128, D]), sb("wo2", [128, D])
        w_so, w_co = sb("w_so", [128, D]), sb("w_co", [128, D])
        w1, w2 = sb("w1", [128, F]), sb("w2", [128, F // 128, D])
        b1 = sb("b1", [128, F // 128])
        b2 = sb("b2", [1, D])
        lng, lnb = sb("lng", [128, 3]), sb("lnb", [128, 3])
        l1w = sb("l1w", [128, 4, D])
        l1b = sb("l1b", [128, 2])
        bv4 = sb("bv4", [1, KT, D])
        bfb = sb("bfb", [128, D])
        gb = {3: (sb("g3", [128, D]), sb("be3", [128, D])), 4: (sb("g4", [128, D]), sb("be4", [128, D]))}
        tw = sb("tw", [128, 2, D])
        tbb = sb("tbb", [128, D])

        QA = {T: sb(f"QA_{T}", [128, NPAIR, 2, LQ], bf16) for T in "cd"}
        KA = {T: sb(f"KA_{T}", [128, NPAIR, LK], bf16) for T in "cd"}
        V1 = {T: sb(f"V1_{T}", [128, KT, NH, 32]) for T in "cd"}
        CT = {T: sb(f"CT_{T}", [128, NQUAD, LQ]) for T in "cd"}
        for of in (QA, KA, V1, CT):
            of["s"] = of["d"]
        nk = {"s": LQ, "c": LK, "d": LK}
        PT = [sb(f"PT{k}", [128, 4, 2, 512]) for k in range(2)]
        first, second = PT[0][:, :, :, :].rearrange("k a b n -> k (a b n)"), PT[1][:, :, :, :].rearrange("k a b n -> k (a b n)")
        kone = first[0:16, 0:2048].bitcast(bf16).rearrange("r (p n) -> r p n", p=NPAIR)
        qone = first[0:16, 2048:3072].bitcast(bf16).rearrange("r (p n) -> r p n", p=NPAIR)
        mk, mkr = second[0:B, 0:LK], second[0:B, LK:2 * LK]
        mkp = second[0:B, 2 * LK:2 * LK + 3 * LK // 2].bitcast(bf16).rearrange("b (t n) -> b t n", t=3)
        w2raw = second[:, 2048:2048 + 4 * D].rearrange("k (t n) -> k t n", t=4)
        mx = [sb(f"mx{k}", [128, QT, 2, 2]) for k in range(2)]
        nr = [sb(f"nr{k}", [128, QT, 2, 2]) for k in range(2)]
        nms = [sb(f"nms{k}", [128, QT, 2, 3, 2], bf16) for k in range(2)]
        nmt = [sb(f"nmt{k}", [12, LQ], bf16) for k in range(2)]
        junk = sb("junk", [128, 2, 384], bf16)
        width = {"s": 2 * LQ, "k": LK, "q": LQ}
        full32 = {w: sb(f"f32_{w}", [128, width[w]]) for w in "skq"}
        rest32 = {w: sb(f"r32_{w}", [128, width[w]]) for w in "skq"}
        split = {w: sb(f"split_{w}", [128, 3, width[w]], bf16) for w in "skq"}
        rr = sb("rr", [128, QT, NQUAD, 4])
        cn, cnT = sb("cn", [128, QT, D]), sb("cnT", [128, LQ])

        xln, xr, x1, x1b, x2, x3 = (sb(n, [128, QT, D]) for n in ("xln", "xr", "x1", "x1b", "x2", "x3"))
        bst = sb("bst", [128, QT, 6])
        mv = [sb(f"mv{w}", [128, QT, 2]) for w in range(5)]
        ve = [sb(f"ve{w}", [128, QT]) for w in range(5)]
        rstd = [sb(f"rstd{w}", [128, QT]) for w in range(5)]
        zt = [sb(f"zt{w}", [128, QT, D]) for w in range(5)]
        nxT = [sb(f"nxT{w}", [128, LQ]) for w in range(3)]
        hT = sb("hT", [128, F // 128, LQ])
        cin, cin3 = sb("cin", [128, KT, D]), sb("cin3", [128, KT, D])
        ctxT = {T: sb(f"ctxT_{T}", [128, LK]) for T in "cd"}
        ctxT3 = sb("ctxT3", [128, LK])
        xl1, xb1, xo1 = (sb(n, [128, QT, D]) for n in ("xl1", "xb1", "xo1"))
        xT1, q1T, k1T, v1 = sb("xT1", [128, LQ]), sb("q1T", [128, LQ]), sb("k1T", [128, LK]), sb("v1", [128, KT, D])
        nm1, rs1, rr1 = sb("nm1", [128, QT]), sb("rs1", [128, QT]), sb("rr1", [128, QT])
        P1, P1T, attT = sb("P1", [128, QT, LK]), sb("P1T", [128, KT, LQ]), sb("attT", [128, LQ])
        y1 = {T: sb(f"y1_{T}", [128, QT, D]) for T in "cd"}
        yT1 = sb("yT1", [128, LQ])
        y1b = {T: sb(f"y1b_{T}", [128, QT, D]) for T in "cd"}
        xo2, y2, y2T = sb("xo2", [128, QT, D]), sb("y2", [128, QT, D]), sb("y2T", [128, LQ])
        nm3, rs3, rr3 = sb("nm3", [128, QT]), sb("rs3", [128, QT]), sb("rr3", [128, QT])
        P3, P3T, tiT = sb("P3", [128, QT, LK]), sb("P3T", [128, KT, LQ]), sb("tiT", [128, LQ])
        hb, ob = sb("hb", [128, QT, D]), sb("ob", [128, QT, D])

        PS, PST, PM = ([ctx.enter_context(nc.psum_tensor(f"{name}{k}", [128, 512], f32)) for k in range(n)]
                       for name, n in (("PS", N_PS), ("PST", N_PST), ("PM", N_PM)))

        scr = {w: nc.dram_tensor(f"scr_{w}", [GROUPS, 128, n], bf16).ap() for w, n in (("sq", LQ), ("sk", LQ), ("q", LQ), ("k", LK))}
        mscr = nc.dram_tensor("mscr", [B, 3, LK], bf16).ap()
        xs = nc.dram_tensor("xs", [B, 128, QT, D], f32).ap()

        s_full, s_free = [sem(f"s_full{k}") for k in range(2)], [sem(f"s_free{k}") for k in range(2)]
        st_full, st_free = [sem(f"st_full{k}") for k in range(N_PST)], [sem(f"st_free{k}") for k in range(N_PST)]
        m_full, m_free = [sem(f"m_full{k}") for k in range(N_PM)], [sem(f"m_free{k}") for k in range(N_PM)]
        pv_done = [sem(f"pv_done{k}") for k in range(2)]
        nm_split = [sem(f"nm_split{k}") for k in range(2)]
        nm_in = [sem(f"nm_in{k}") for k in range(2)]
        causal_cut = sem("causal_cut")
        q_in = {T: sem(f"q_in_{T}") for T in "scd"}
        k_in = {T: sem(f"k_in_{T}") for T in "scd"}
        split_done = {w: sem(f"split_done_{w}") for w in "skq"}
        scr_in = {w: sem(f"scr_in_{w}") for w in "skq"}
        stats = [sem(f"stats{w}") for w in range(5)]
        rstd_ok = [sem(f"rstd_ok{w}") for w in range(5)]
        z_ok = [sem(f"z_ok{w}") for w in range(5)]
        y_ok = {3: sem("y_ok3"), 4: sem("y_ok4")}
        x_in, xr_in, c_in, xs_in, c3_in = sem("x_in"), sem("xr_in"), sem("c_in"), sem("xs_in"), sem("c3_in")
        x1b_ok, xb_ok, y1b_ok = sem("x1b_ok"), sem("xb_ok"), {T: sem(f"y1b_ok_{T}") for T in "cd"}
        xs_out = sem("xs_out")
        nm1_ok, nm3_ok = sem("nm1_ok"), sem("nm3_ok")
        rr3_ok, p3_ok = sem("rr3_ok"), sem("p3_ok")
        th_ok, ob_ok, out_ok = sem("th_ok"), sem("ob_ok"), sem("out_ok")
        mask_in = sem("mask_in")
        w_in, id_ok, setup_v, setup_p, scr_const, mscr_ok = (sem(n) for n in ("w_in", "id_ok", "setup_v", "setup_p", "scr_const", "mscr_ok"))
        chains = {e: sem(f"chain_{e}") for e in ("dve", "pool", "act")}

        class Chain:

            def __init__(self, eng, name):
                self.eng, self.sem, self.at = eng, chains[name], 0

            def __call__(self, ins):
                self.at += 1
                ins.then_inc(self.sem, 1)
                self.eng.wait_ge(self.sem, self.at)

            def restart(self):
                if self.at:
                    self.eng.sem_clear(self.sem)
                self.at = 0

        passed = sem("passed")

        def apart(eng):
            eng.sem_inc(passed, 1)

        def walk(eng, table, chain=None):
            for times, steps in parts:
                mine = [x for x in steps if x[0][0] in table]
                if not mine:
                    continue
                if chain:
                    chain.restart()
                if times == 1:
                    for s, r, phase in mine:
                        table[s[0]](s, {x: v[0] for x, v in r.items()}, phase)
                    continue
                with eng.Fori(0, times) as i:
                    for s, r, phase in mine:
                        table[s[0]](s, {x: v[0] if v[1] == 0 else i * v[1] + v[0] for x, v in r.items()}, phase)
                    if chain:
                        chain.restart()

        W_LOADS = []

        def load(dst, src):
            W_LOADS.append((dst, src))

        load(w_qkv[:, :], a["L0_xattn_W_qkv"]); load(w_so[:, :], a["L0_xattn_W_self_out"])
        load(w_q0[:, :], a["L0_xattn_W_q"]); load(w_kv0[:, :], a["L0_xattn_W_kv"]); load(w_co[:, :], a["L0_xattn_W_cross_out"])
        load(w1[:, :], a["L0_xattn_W1"]); load(w2[:, :, :], a["L0_xattn_W2"].rearrange("(k p) n -> p k n", p=128))
        load(b1[:, :], a["L0_xattn_b1"].rearrange("(k p) -> p k", p=128)); load(b2[:, :], a["L0_xattn_b2"].rearrange("(o n) -> o n", o=1))
        for w in range(3):
            load(lng[:, w:w + 1], a[f"L0_xattn_ln{w + 1}_scale"].rearrange("(p o) -> p o", o=1))
            load(lnb[:, w:w + 1], a[f"L0_xattn_ln{w + 1}_bias"].rearrange("(p o) -> p o", o=1))
        for k, name in enumerate(("Wq", "Wk", "Wv", "Wf")):
            load(l1w[:, k, :], a[f"L1_xattn_{name}"])
        load(l1b[:, 0:1], a["L1_xattn_bq"].rearrange("(p o) -> p o", o=1))
        load(l1b[:, 1:2], a["L1_xattn_bk"].rearrange("(p o) -> p o", o=1))
        for kt in range(KT):
            load(bv4[:, kt, :], a["L1_xattn_bv"].rearrange("(o n) -> o n", o=1))
        load(bfb[:, :], row("L1_xattn_bf", D))
        load(gb[3][0][:, :], row("L1_xattn_ln_gamma", D)); load(gb[3][1][:, :], row("L1_xattn_ln_beta", D))
        load(gb[4][0][:, :], row("L2_xattn_gamma", D)); load(gb[4][1][:, :], row("L2_xattn_beta", D))
        for k, name in enumerate(("Wq", "Wk", "Wv", "Wo")):
            load(w2raw[:, k, :], a[f"L2_xattn_{name}"])
        load(tw[:, :, :], a["L3_xattn_trans_W"].rearrange("(k p) n -> p k n", p=128))
        load(tbb[:, :], row("L3_xattn_trans_b", D))
        load(mk, a["mask_Bx1x1xS2_ff0"].rearrange("b o c n -> b (o c n)"))
        N_W = 16 * len(W_LOADS)

        x_dram = a["x"].rearrange("b (t p) d -> b p t d", p=128)
        c_dram = a["ctx_1024"].rearrange("b (t p) d -> b p t d", p=128)
        o_dram = out.rearrange("b (t p) d -> b p t d", p=128)

        block = ctx.enter_context(nc.Block())

        @block.sync
        def _(sp):
            for dst, src in W_LOADS:
                sp.dma_start(dst, src, allow_slow_non_contiguous=dst.shape[0] == 128 and dst.shape[-1] == F // 128).then_inc(w_in, 16)
            sp.wait_ge(setup_p, 1)
            for name, src, n in (("sq", qone, LQ), ("q", qone, LQ), ("sk", kone, LQ), ("k", kone, LK)):
                for j in range(2):
                    dst = scr[name].rearrange("g (j i p) n -> j g i p n", j=2, p=8)[j, 6:8]
                    sp.dma_start(dst, src[:, :, 0:n]).then_inc(scr_const, 16)
            sp.wait_ge(setup_v, 1)
            sp.dma_start(mscr, mkp).then_inc(mscr_ok, 16)
            sp.wait_ge(scr_const, 16 * 8)
            sp.wait_ge(mscr_ok, 16)

            def put(w, name, src, groups, lo=0):
                g, k = groups[0], len(groups)
                sp.dma_start(scr[name][g:g + k].rearrange("g r n -> r g n"), src).then_inc(scr_in[w], 16)

            def put_q(w, name, n, off=0):
                put(w, name, split[w][:, 0:1, off:off + n].to_broadcast([128, 3, n]), (0, 1, 2))
                put(w, name, split[w][:, 1:2, off:off + n].to_broadcast([128, 2, n]), (3, 4))
                put(w, name, split[w][:, 2:3, off:off + n], (5,))

            def put_k(w, name, n, off=0):
                put(w, name, split[w][:, 0:3, off:off + n], (0, 1, 2))
                put(w, name, split[w][:, 0:2, off:off + n], (3, 4))
                put(w, name, split[w][:, 0:1, off:off + n], (5,))

            def get_q(T, name, w):
                for j in range(2):
                    sp.dma_start(QA[T][HB * j:HB * j + HB, :, j, :],
                                 scr[name].rearrange("g (j i p) n -> j g i p n", j=2, p=8)[j]).then_inc(q_in[T], 16)

            def get_k(T, name, w):
                for j in range(2):
                    sp.dma_start(KA[T][HB * j:HB * j + HB, :, 0:nk[T]],
                                 scr[name].rearrange("g (j i p) n -> j g i p n", j=2, p=8)[j]).then_inc(k_in[T], 16)

            def scratch_free(w, r):
                sp.wait_ge(split_done[w], r["w"] + 1)
                apart(sp)
                T = "scd"[r["ldT_b"]]
                sp.wait_ge((q_in if w == "q" else k_in)[T], r["ld"])
                apart(sp)
                if w == "s":
                    sp.wait_ge(q_in[T], r["ld"])
                    apart(sp)

            def step_xln(s, r, p):
                sp.wait_ge(z_ok[0], r["n"])
                apart(sp)
                sp.dma_start(xln[:, :, :], x_dram[r["n"]]).then_inc(x_in, 16)

            def step_xr(s, r, p):
                sp.wait_ge(m_free[r["prev_b"]], r["prev"])
                apart(sp)
                sp.dma_start(xr[:, :, :], x_dram[r["n"]]).then_inc(xr_in, 16)

            def step_cl(s, r, p):
                sp.wait_ge(m_free[r["prev_b"]], r["prev"])
                apart(sp)
                sp.dma_start(cin[:, :, :], c_dram[r["n"]]).then_inc(c_in, 16)

            def step_cl3(s, r, p):
                sp.wait_ge(ob_ok, r["n"])
                apart(sp)
                sp.dma_start(cin3[:, :, :], c_dram[r["n"]]).then_inc(c3_in, 16)

            def step_xs(s, r, p):
                sp.wait_ge(xs_out, 16 * (r["n"] + 1))
                apart(sp)
                sp.wait_ge(m_free[r["prev_b"]], r["prev"])
                apart(sp)
                sp.dma_start(xl1[:, :, :], xs[r["n"]]).then_inc(xs_in, 16)

            def step_qkw(s, r, p):
                scratch_free("s", r)
                put_q("s", "sq", LQ)
                put_k("s", "sk", LQ, off=LQ)

            def step_qkl(s, r, p):
                sp.wait_ge(scr_in["s"], (r["w"] + 1) * 96)
                apart(sp)
                sp.wait_ge(st_free[0], r["e0"])
                apart(sp)
                sp.wait_ge(st_free[1], r["e1"])
                apart(sp)
                sp.wait_ge(st_free[2], r["e2"])
                apart(sp)
                get_q("s", "sq", "s")
                get_k("s", "sk", "s")

            def step_kw(s, r, p):
                scratch_free("k", r)
                put_k("k", "k", LK)
                if p == 2:
                    for j in range(2):
                        dst = scr["k"].rearrange("g (j i p) n -> g j i p n", j=2, p=8)[6, j, 3:6]
                        sp.dma_start(dst, mscr[r["n"]].rearrange("t (o n) -> t o n", o=1).to_broadcast([3, 8, LK])).then_inc(mask_in, 16)

            def step_kl(s, r, p):
                sp.wait_ge(scr_in["k"], (r["w"] + 1) * 48)
                apart(sp)
                if p == 2:
                    sp.wait_ge(mask_in, (r["n"] + 1) * 32)
                    apart(sp)
                sp.wait_ge(st_free[0], r["e0"])
                apart(sp)
                sp.wait_ge(st_free[1], r["e1"])
                apart(sp)
                sp.wait_ge(st_free[2], r["e2"])
                apart(sp)
                get_k(s[1], "k", "k")

            def step_qw(s, r, p):
                scratch_free("q", r)
                put_q("q", "q", LQ)

            def step_ql(s, r, p):
                sp.wait_ge(scr_in["q"], (r["w"] + 1) * 48)
                apart(sp)
                sp.wait_ge(st_free[0], r["e0"])
                apart(sp)
                sp.wait_ge(st_free[1], r["e1"])
                apart(sp)
                sp.wait_ge(st_free[2], r["e2"])
                apart(sp)
                get_q(s[1], "q", "q")

            def step_nmt(s, r, p):
                T, q, par = s[1], s[3], s[3] % 2
                sp.wait_ge(m_free[r["bank"]], r["free"] + 1)
                apart(sp)
                for j in range(2):
                    sp.dma_start(QA[T][HB * j + R_MAX:HB * j + R_MAX + 3, 2 * q:2 * q + 2, j, :],
                                 nmt[par][6 * j:6 * j + 6, :]).then_inc(nm_in[par], 16)

            def step_ff2(s, r, p):
                sp.wait_ge(m_free[r["bank"]], r["free"] + 1)
                apart(sp)
                sp.dma_start(xs[r["n"]], x3[:, :, :]).then_inc(xs_out, 16)

            def step_l3h(s, r, p):
                sp.wait_ge(ob_ok, r["n"] + 1)
                apart(sp)
                sp.dma_start(o_dram[r["n"]], ob[:, :, :]).then_inc(out_ok, 16)

            walk(sp, {"XLN": step_xln, "XR": step_xr, "CL": step_cl, "CL3": step_cl3, "XS": step_xs, "QKW": step_qkw,
                      "QKL": step_qkl, "KW": step_kw, "KL": step_kl, "QW": step_qw, "QL": step_ql, "NMT": step_nmt,
                      "FF2": step_ff2, "L3H": step_l3h})
            sp.wait_ge(out_ok, 16 * B)

        @block.gpsimd
        def _(pool):
            chain = Chain(pool, "pool")
            pool.memset(kone, 0.0).then_inc(id_ok, 1)
            pool.memset(qone, 0.0).then_inc(id_ok, 1)
            pool.memset(ident[:, :], 0.0).then_inc(id_ok, 1)
            pool.memset(identb[:, :], 0.0).then_inc(id_ok, 1)
            pool.memset(causal[:, :], 0.0).then_inc(id_ok, 1)
            pool.memset(half[:, :], -0.5).then_inc(id_ok, 1)
            pool.wait_ge(id_ok, 6)
            for m in (ident, identb):
                chain(pool.affine_select(out=m[:, :], in_=m[:, :], compare_op=ALU.not_equal, fill=1.0, base=0,
                                         pattern=[[-1, 128]], channel_multiplier=1))
            chain(pool.affine_select(out=causal[:, 128:256], in_=causal[:, 128:256], compare_op=ALU.is_ge, fill=NEG, base=0,
                                     pattern=[[-1, 128]], channel_multiplier=1))
            chain(pool.affine_select(out=kone, in_=kone, compare_op=ALU.is_ge, fill=1.0, base=-3,
                                     pattern=[[0, NPAIR], [0, LK]], channel_multiplier=1))
            chain(pool.affine_select(out=qone, in_=qone, compare_op=ALU.is_ge, fill=1.0, base=-6,
                                     pattern=[[0, NPAIR], [0, LQ]], channel_multiplier=1))
            pool.affine_select(out=qone, in_=qone, compare_op=ALU.is_ge, fill=0.0, base=-3,
                               pattern=[[0, NPAIR], [0, LQ]], channel_multiplier=1).then_inc(setup_p, 1)
            pool.wait_ge(setup_p, 1)
            pool.wait_ge(w_in, N_W)

            def parts_of(w, r):
                chain(pool.tensor_tensor(rest32[w][:, :], full32[w][:, :], split[w][:, 0, :], ALU.subtract))
                chain(pool.tensor_copy(split[w][:, 1, :], rest32[w][:, :]))
                pool.tensor_tensor(split[w][:, 2, :], rest32[w][:, :], split[w][:, 1, :], ALU.subtract).then_inc(split_done[w], 1)

            def step_split(s, r, p):
                w = {"QK": "s", "K": "k", "Q": "q"}[s[0]]
                pool.wait_ge(m_free[r["bank"]], r["free"] + 1)
                apart(pool)
                parts_of(w, r)

            def step_st(s, r, p):
                if s[1] != "s":
                    return
                par, u = s[3] % 2, s[4]
                pool.wait_ge(st_free[r["bank"]], r["free"] + 1)
                apart(pool)
                d = PT[par][:, u // 2, u % 2, 0:256 if u % 2 else 512].rearrange("k (j n) -> k j n", j=2)[:, :, 0:128]
                pool.affine_select(out=d, in_=d, compare_op=ALU.is_ge, fill=0.0, base=0,
                                   pattern=[[0, 2], [1, 128]], channel_multiplier=-1).then_inc(causal_cut, 1)

            def step_lns(s, r, p):
                w = s[1]
                pool.wait_ge(stats[w], r["n"] + 1)
                apart(pool)
                chain(pool.tensor_scalar(ve[w][:, :], mv[w][:, :, 1], 1e-6 if w < 3 else 1e-5, None, ALU.add))
                pool.tensor_tensor(rstd[w][:, :], ve[w][:, :], half[:, :], ALU.pow).then_inc(rstd_ok[w], 1)

            def step_x1b(s, r, p):
                pool.wait_ge(m_free[r["in_b"]], r["in"])
                apart(pool)
                pool.wait_ge(m_free[r["prev_b"]], r["prev"])
                apart(pool)
                pool.tensor_copy(x1b[:, :, :], x1[:, :, :]).then_inc(x1b_ok, 1)

            def step_y1b(s, r, p):
                pool.wait_ge(m_free[r["prev_b"]], r["prev"])
                apart(pool)
                pool.wait_ge(y_ok[3], r["n"] + 1)
                apart(pool)
                pool.tensor_copy(y1b[s[1]][:, :, :], y1[s[1]][:, :, :]).then_inc(y1b_ok[s[1]], 1)

            def step_xs(s, r, p):
                pool.wait_ge(xs_in, 16 * (r["n"] + 1))
                apart(pool)
                pool.wait_ge(m_free[r["prev_b"]], r["prev"])
                apart(pool)
                pool.tensor_tensor(xb1[:, :, :], xl1[:, :, :], bfb[:, :].rearrange("p (o n) -> p o n", o=1).to_broadcast([128, QT, D]),
                                   ALU.add).then_inc(xb_ok, 1)

            def step_lng(s, r, p):
                w = s[1]
                pool.wait_ge(z_ok[w], r["n"] + 1)
                apart(pool)
                if w == 3:
                    pool.wait_ge(y1b_ok[TURN[s[2] % 2]], r["j"])
                    apart(pool)
                T = TURN[s[2] % 2]
                y = y1[T] if w == 3 else y2
                g, be = (t[:, :].rearrange("p (o n) -> p o n", o=1).to_broadcast([128, QT, D]) for t in gb[w])
                chain(pool.tensor_tensor(zt[w][:, :, :], zt[w][:, :, :], g, ALU.mult))
                pool.tensor_tensor(y[:, :, :], zt[w][:, :, :], be, ALU.add).then_inc(y_ok[w], 1)

            def step_l3h(s, r, p):
                pool.wait_ge(th_ok, r["n"] + 1)
                apart(pool)
                pool.wait_ge(out_ok, 16 * r["n"])
                apart(pool)
                pool.tensor_tensor(ob[:, :, :], hb[:, :, :], y2[:, :, :], ALU.add).then_inc(ob_ok, 1)

            walk(pool, {"QK": step_split, "K": step_split, "Q": step_split, "ST": step_st, "LNS": step_lns,
                        "X1B": step_x1b, "Y1B": step_y1b, "XS": step_xs, "LNG": step_lng, "L3H": step_l3h}, chain)

        @block.scalar
        def _(act):
            act.wait_ge(w_in, N_W)
            act.wait_ge(setup_v, 1)

            def step_st(s, r, p):
                T, q, u, par = s[1], s[3], s[4], s[3] % 2
                act.wait_ge(st_full[r["bank"]], r["free"] + 1)
                if u == 0:
                    act.wait_ge(pv_done[par], r["pt"])
                n = 256 if T == "s" and u % 2 else 512
                act.activation(PT[par][:, u // 2, u % 2, 0:n], PST[r["bank"]][:, 0:n], ACT.Exp).then_inc(st_free[r["bank"]], 1)

            def step_lnt(s, r, p):
                act.wait_ge(m_full[r["bank"]], r["full"])
                bank, free = PM[r["bank"]], m_free[r["bank"]]
                w = s[1]
                act.activation(nxT[w][:, :], bank[:, 0:LQ], ACT.Identity, bias=lnb[:, w:w + 1], scale=lng[:, w:w + 1]).then_inc(free, 1)

            def step_split(s, r, p):
                w = {"QK": "s", "K": "k", "Q": "q"}[s[0]]
                act.wait_ge(m_full[r["bank"]], r["full"])
                bank, free = PM[r["bank"]], m_free[r["bank"]]
                act.wait_ge(split_done[w], r["w"])
                per = 96 if w == "s" else 48
                act.wait_ge(scr_in[w], r["w"] * per)
                act.activation(full32[w][:, :], bank[:, 0:width[w]], ACT.Copy)
                act.activation(split[w][:, 0, :], bank[:, 0:width[w]], ACT.Copy).then_inc(free, 1)

            def step_v(s, r, p):
                act.wait_ge(m_full[r["bank"]], r["full"])
                bank, free = PM[r["bank"]], m_free[r["bank"]]
                T = s[1]
                n = KTS[T] * D
                act.activation(V1[T][:, 0:KTS[T], :, 0:DH], bank[:, 0:n].rearrange("k (t h d) -> k t h d", h=NH, d=DH), ACT.Copy).then_inc(free, 1)

            def step_outb(s, r, p):
                act.wait_ge(m_full[r["bank"]], r["full"])
                act.activation(cnT[:, :], PM[r["bank"]][:, 0:LQ], ACT.Copy).then_inc(m_free[r["bank"]], 1)

            def step_ct3(s, r, p):
                act.wait_ge(m_full[r["bank"]], r["full"])
                act.activation(ctxT3[:, :], PM[r["bank"]][:, 0:LK], ACT.Copy).then_inc(m_free[r["bank"]], 1)

            def step_xt(s, r, p):
                act.wait_ge(m_full[r["bank"]], r["full"])
                act.activation(xT1[:, :], PM[r["bank"]][:, 0:LQ], ACT.Copy).then_inc(m_free[r["bank"]], 1)

            def step_yt(s, r, p):
                act.wait_ge(m_full[r["bank"]], r["full"])
                act.activation(yT1[:, :], PM[r["bank"]][:, 0:LQ], ACT.Copy).then_inc(m_free[r["bank"]], 1)

            def step_y2t(s, r, p):
                act.wait_ge(m_full[r["bank"]], r["full"])
                act.activation(y2T[:, :], PM[r["bank"]][:, 0:LQ], ACT.Copy).then_inc(m_free[r["bank"]], 1)

            def step_l1a(s, r, p):
                act.wait_ge(m_full[r["bank"]], r["full"])
                act.activation(attT[:, :], PM[r["bank"]][:, 0:LQ], ACT.Copy).then_inc(m_free[r["bank"]], 1)

            def step_l3a(s, r, p):
                act.wait_ge(m_full[r["bank"]], r["full"])
                act.activation(tiT[:, :], PM[r["bank"]][:, 0:LQ], ACT.Copy).then_inc(m_free[r["bank"]], 1)

            def step_ct(s, r, p):
                dst = ctxT["c" if p == 1 else TURN[s[2] % 2]]
                act.wait_ge(m_full[r["bank"]], r["full"])
                act.activation(dst[:, :], PM[r["bank"]][:, :], ACT.Copy).then_inc(m_free[r["bank"]], 1)

            def step_ff1(s, r, p):
                act.wait_ge(m_full[r["bank"]], r["full"])
                bank, free = PM[r["bank"]], m_free[r["bank"]]
                for k in range(2):
                    blk = 2 * s[3] + k
                    ins = act.activation(hT[:, blk, :], bank[:, k * LQ:(k + 1) * LQ], ACT.Relu, bias=b1[:, blk:blk + 1])
                ins.then_inc(free, 1)

            def step_g1(s, r, p):
                act.wait_ge(m_full[r["bank"]], r["full"])
                bank, free = PM[r["bank"]], m_free[r["bank"]]
                if s[3] == 0:
                    act.activation(q1T[:, :], bank[:, 0:LQ], ACT.Gelu, bias=l1b[:, 0:1]).then_inc(free, 1)
                elif s[3] == 1:
                    act.activation(k1T[:, :], bank[:, :], ACT.Gelu, bias=l1b[:, 1:2]).then_inc(free, 1)
                else:
                    act.activation(v1[:, :, :].rearrange("k t d -> k (t d)"), bank[:, :], ACT.Gelu).then_inc(free, 1)

            def step_l1s(s, r, p):
                act.wait_ge(m_full[r["bank"]], r["full"])
                bank, free = PM[r["bank"]], m_free[r["bank"]]
                qt = s[3]
                act.wait_ge(nm1_ok, r["n"] * QT + qt + 1)
                act.activation(P1[:, qt, :], bank[:, :], ACT.Exp, bias=nm1[:, qt:qt + 1], accum_out=rs1[:, qt:qt + 1]).then_inc(free, 1)

            def step_l3s(s, r, p):
                act.wait_ge(m_full[r["bank"]], r["full"])
                bank, free = PM[r["bank"]], m_free[r["bank"]]
                act.wait_ge(nm3_ok, r["n"] * 2 + s[3] + 1)
                qt = s[3]
                act.activation(P3[:, qt, :], bank[:, :], ACT.Exp, bias=nm3[:, qt:qt + 1], accum_out=rs3[:, qt:qt + 1]).then_inc(free, 1)

            def step_l3n(s, r, p):
                act.wait_ge(rr3_ok, r["n"] + 1)
                for qt in range(QT):
                    ins = act.activation(P3[:, qt, :], P3[:, qt, :], ACT.Copy, scale=rr3[:, qt:qt + 1])
                ins.then_inc(p3_ok, 1)

            def step_l3h(s, r, p):
                act.wait_ge(m_free[r["bank"]], r["free"] + 1)
                act.activation(hb[:, :, :], hb[:, :, :], ACT.Tanh).then_inc(th_ok, 1)

            walk(act, {"ST": step_st, "LNT": step_lnt, "QK": step_split, "K": step_split, "Q": step_split, "V": step_v,
                       "OUTB": step_outb, "CT": step_ct, "CT3": step_ct3, "XT": step_xt,
                       "YT": step_yt, "Y2T": step_y2t, "L1A": step_l1a, "L3A": step_l3a,
                       "FF1": step_ff1, "G1": step_g1, "L1S": step_l1s, "L3S": step_l3s, "L3N": step_l3n, "L3H": step_l3h})

        @block.vector
        def _(dve):
            chain = Chain(dve, "dve")
            for T in "cd":
                chain(dve.memset(V1[T][:, :, :, :], 0.0))
                chain(dve.memset(QA[T][:, :, :, :], 0.0))
                chain(dve.memset(V1[T][:, :, :, DH:DH + 1], 1.0))
            chain(dve.memset(ones1[:, :], 1.0))
            dve.wait_ge(w_in, N_W)
            chain(dve.tensor_scalar(mk, mk, NEG, None, ALU.mult))
            chain(dve.tensor_copy(mkp[:, 0, :], mk))
            chain(dve.tensor_tensor(mkr, mk, mkp[:, 0, :], ALU.subtract))
            chain(dve.tensor_copy(mkp[:, 1, :], mkr))
            chain(dve.tensor_tensor(mkp[:, 2, :], mkr, mkp[:, 1, :], ALU.subtract))
            scale = float(np.float32(1.0) / np.sqrt(np.float32(DH)))

            def permuted(dst, src, by):
                view = src.rearrange("k (p j i) -> k j i p", p=NPAIR, j=2)
                for j in range(2):
                    chain(dve.tensor_scalar(dst[:, 64 * j:64 * j + 64].rearrange("k (i p) -> k i p", p=NPAIR), view[:, j], by, None, ALU.mult))

            permuted(wqp["s"], w_qkv[:, 0:D], scale)
            permuted(wkp["s"], w_qkv[:, D:2 * D], 1.0)
            permuted(wqp[1], w_q0[:, :], scale)
            permuted(wkp[1], w_kv0[:, 0:D], 1.0)
            dve.memset(junk[:, :, :], 0.0).then_inc(setup_v, 1)

            def step_wt(s, r, p):
                dve.wait_ge(m_full[r["bank"]], r["full"])
                bank, free = PM[r["bank"]], m_free[r["bank"]]
                permuted(wqp[2], bank[:, 0:128], scale)
                permuted(wkp[2], bank[:, 128:256], 1.0)
                chain(dve.tensor_copy(wv2[:, :], bank[:, 256:384]))
                dve.tensor_copy(wo2[:, :], bank[:, 384:512]).then_inc(free, 1)

            def step_s(s, r, p):
                T, q, u, par = s[1], s[3], s[4], s[3] % 2
                bank, free = PS[r["bank"]], s_free[r["bank"]]
                if u == 0:
                    dve.wait_ge(nm_split[par], r["mx"])
                dve.wait_ge(s_full[r["bank"]], r["free"] + 1)
                if T == "s":
                    dve.sem_inc(passed, 1)
                    pp, j = u // 2, u % 2
                    dve.tensor_tensor_reduce(out=junk[:, r["bank"], 0:128], in0=bank[:, 0:128], in1=causal[:, 128:256], scale=1.0, scalar=-3.0e38,
                                             op0=ALU.add, op1=ALU.max, accum_out=mx[par][:, 0, j, pp:pp + 1])
                    dve.tensor_tensor_reduce(out=junk[:, r["bank"], 128:384], in0=bank[:, 128:384], in1=causal[:, :], scale=1.0, scalar=-3.0e38,
                                             op0=ALU.add, op1=ALU.max, accum_out=mx[par][:, 1, j, pp:pp + 1]).then_inc(free, 1)
                else:
                    pp, j, qt = u // 4, u // 2 % 2, u % 2
                    dve.reduce_max(mx[par][:, qt, j, pp:pp + 1], bank[:, :], X).then_inc(free, 1)

            def step_nm(s, r, p):
                par = s[3] % 2
                dve.wait_ge(s_free[0], r["s0"])
                dve.wait_ge(s_free[1], r["s1"])
                dve.sem_inc(passed, 1)
                chain(dve.tensor_scalar(nms[par][:, :, :, 0, :], mx[par][:, :, :, :], -1.0, None, ALU.mult))
                chain(dve.scalar_tensor_tensor(nr[par][:, :, :, :], mx[par][:, :, :, :], -1.0, nms[par][:, :, :, 0, :], ALU.mult, ALU.subtract))
                chain(dve.tensor_copy(nms[par][:, :, :, 1, :], nr[par][:, :, :, :]))
                dve.tensor_tensor(nms[par][:, :, :, 2, :], nr[par][:, :, :, :], nms[par][:, :, :, 1, :],
                                  ALU.subtract).then_inc(nm_split[par], 1)

            def step_nmt(s, r, p):
                dve.wait_ge(m_full[r["bank"]], r["full"])
                bank, free = PM[r["bank"]], m_free[r["bank"]]
                par = s[3] % 2
                dve.wait_ge(nm_in[par], 32 * r["mx"])
                dve.tensor_copy(nmt[par][:, :], bank[0:12, 0:128].bitcast(bf16)).then_inc(free, 1)

            def step_pvc(s, r, p):
                dve.wait_ge(pv_done[s[3] % 2], r["pt"])
                dve.tensor_copy(CT[s[1]][:, s[3], :], PM[r["bank"]][:, 0:LQ]).then_inc(m_free[r["bank"]], 1)

            def step_lns(s, r, p):
                w = s[1]
                src = {0: xln, 1: x1, 2: x2, 3: xo1, 4: xo2}[w]
                if w == 0:
                    dve.wait_ge(x_in, 16 * (r["n"] + 1))
                else:
                    dve.wait_ge(m_free[r["in_b"]], r["in"])
                for t in range(QT):
                    chain(dve.bn_stats(bst[:, t, :], src[:, t, :]))
                for t in range(QT):
                    ins = dve.bn_aggr(mv[w][:, t, :], bst[:, t, :])
                ins.then_inc(stats[w], 1)

            def step_lnz(s, r, p):
                w = s[1]
                src = {0: xln, 1: x1, 2: x2, 3: xo1, 4: xo2}[w]
                dve.wait_ge(rstd_ok[w], r["n"] + 1)
                if w >= 3:
                    dve.wait_ge(y_ok[w], r["n"])
                for t in range(QT):
                    ins = dve.tensor_scalar(zt[w][:, t, :], src[:, t, :], mv[w][:, t, 0:1], rstd[w][:, t:t + 1], ALU.subtract, ALU.mult)
                ins.then_inc(z_ok[w], 1)

            def step_outa(s, r, p):
                dve.wait_ge(m_full[r["bank"]], r["full"])
                bank, free = PM[r["bank"]], m_free[r["bank"]]
                v = bank[:, :].rearrange("q (g c r) -> q g c r", g=NQUAD, c=4)
                chain(dve.reciprocal(rr[:, s[3], :, :], v[:, :, :, DH]))
                dve.tensor_tensor(cn[:, s[3], :].rearrange("q (g c r) -> q g c r", g=NQUAD, c=4), v[:, :, :, 0:DH],
                                  rr[:, s[3], :, :].rearrange("q g (c o) -> q g c o", o=1).to_broadcast([128, NQUAD, 4, DH]), ALU.mult).then_inc(free, 1)

            def step_outc(s, r, p):
                dve.wait_ge(m_full[r["bank"]], r["full"])
                bank, free = PM[r["bank"]], m_free[r["bank"]]
                T = s[1]
                if T == "s":
                    dve.wait_ge(xr_in, 16 * (r["n"] + 1))
                    dve.wait_ge(x1b_ok, r["n"])
                    dst, res = x1, xr
                elif p == 1:
                    dve.wait_ge(x1b_ok, r["n"] + 1)
                    dst, res = x2, x1b
                else:
                    dve.wait_ge(y1b_ok[T], r["t"] + 1 - (8 if T == "c" else 0))
                    dst, res = xo2, y1b[T]
                dve.tensor_tensor(dst[:, :, :], bank[:, 0:LQ].rearrange("q (t d) -> q t d", t=QT), res[:, :, :], ALU.add).then_inc(free, 1)

            def step_ff2(s, r, p):
                dve.wait_ge(m_full[r["bank"]], r["full"])
                bank, free = PM[r["bank"]], m_free[r["bank"]]
                dve.wait_ge(xs_out, 16 * r["n"])
                dve.tensor_tensor(x3[:, :, :], bank[:, 0:LQ].rearrange("q (t d) -> q t d", t=QT), x2[:, :, :], ALU.add).then_inc(free, 1)

            def step_l1s(s, r, p):
                dve.wait_ge(m_full[r["bank"]], r["full"])
                bank, free = PM[r["bank"]], m_free[r["bank"]]
                dve.tensor_reduce(nm1[:, s[3]:s[3] + 1], bank[:, :], X, ALU.max, negate=True).then_inc(nm1_ok, 1)

            def step_l1t(s, r, p):
                dve.wait_ge(m_full[r["bank"]], r["full"])
                bank, free = PM[r["bank"]], m_free[r["bank"]]
                qt = s[3]
                dve.tensor_copy(P1T[:, :, qt * 128:qt * 128 + 128], bank[:, :].rearrange("k (t q) -> k t q", t=KT)).then_inc(free, 1)

            def step_l1o(s, r, p):
                dve.wait_ge(m_full[r["bank"]], r["full"])
                bank, free = PM[r["bank"]], m_free[r["bank"]]
                dve.wait_ge(m_free[r["ex_b"]], r["ex"])
                chain(dve.reciprocal(rr1[:, :], rs1[:, :]))
                dve.wait_ge(xb_ok, r["n"] + 1)
                for t in range(QT):
                    ins = dve.scalar_tensor_tensor(xo1[:, t, :], bank[:, t * D:(t + 1) * D], rr1[:, t:t + 1], xb1[:, t, :], ALU.mult, ALU.add)
                ins.then_inc(free, 1)

            def step_l3s(s, r, p):
                dve.wait_ge(m_full[r["bank"]], r["full"])
                bank, free = PM[r["bank"]], m_free[r["bank"]]
                dve.tensor_reduce(nm3[:, s[3]:s[3] + 1], bank[:, :], X, ALU.max, negate=True).then_inc(nm3_ok, 1)

            def step_l3n(s, r, p):
                dve.wait_ge(m_free[r["in_b"]], r["in"])
                dve.wait_ge(m_free[r["in2_b"]], r["in2"])
                dve.wait_ge(p3_ok, r["n"])
                dve.reciprocal(rr3[:, :], rs3[:, :]).then_inc(rr3_ok, 1)

            def step_l3t(s, r, p):
                dve.wait_ge(m_full[r["bank"]], r["full"])
                bank, free = PM[r["bank"]], m_free[r["bank"]]
                dve.tensor_copy(P3T[:, :, s[3] * 128:s[3] * 128 + 128], bank[:, :].rearrange("k (t q) -> k t q", t=KT)).then_inc(free, 1)

            def step_l3h(s, r, p):
                dve.wait_ge(m_full[r["bank"]], r["full"])
                bank, free = PM[r["bank"]], m_free[r["bank"]]
                dve.wait_ge(ob_ok, r["n"])
                dve.tensor_tensor(hb[:, :, :], bank[:, 0:LQ].rearrange("q (t d) -> q t d", t=QT),
                                  tbb[:, :].rearrange("p (o n) -> p o n", o=1).to_broadcast([128, QT, D]), ALU.add).then_inc(free, 1)

            walk(dve, {"WT": step_wt, "S": step_s, "NM": step_nm, "NMT": step_nmt, "PVC": step_pvc, "LNS": step_lns, "LNZ": step_lnz, "OUTA": step_outa,
                       "OUTC": step_outc, "FF2": step_ff2, "L1S": step_l1s, "L1T": step_l1t, "L1O": step_l1o, "L3S": step_l3s,
                       "L3N": step_l3n, "L3T": step_l3t, "L3H": step_l3h}, chain)

        @block.tensor
        def _(pe):
            pe.wait_ge(setup_p, 1)
            pe.wait_ge(w_in, N_W)
            pe.wait_ge(setup_v, 1)

            def transposed(bank, blocks):
                for k, src in enumerate(blocks):
                    ins = pe.transpose(bank[:, 128 * k:128 * k + 128], src, ident[:, :])
                return ins

            def mm(out_, l, m, first=True, last=True):
                return pe.matmul(out_, l, m, start=first, stop=True, skip_group_check=True)

            def step_wt(s, r, p):
                pe.wait_ge(m_free[r["bank"]], r["free"])
                transposed(PM[r["bank"]], [w2raw[:, k, :] for k in range(4)]).then_inc(m_full[r["bank"]], 1)

            def step_s(s, r, p):
                T, q, u = s[1], s[3], s[4]
                if q == 0 and u == 0:
                    pe.wait_ge(q_in[T], 32 * (r["t"] + 1))
                    pe.wait_ge(k_in[T], 32 * (r["t"] + 1))
                pe.wait_ge(s_free[r["bank"]], r["free"])
                bank = PS[r["bank"]]
                if T == "s":
                    pr, j = 2 * q + u // 2, u % 2
                    mm(bank[:, 0:128], QA[T][:, pr, j, 0:128], KA[T][:, pr, 0:128])
                    ins = mm(bank[:, 128:384], QA[T][:, pr, j, 128:256], KA[T][:, pr, 0:LQ])
                else:
                    pr, j, qt = 2 * q + u // 4, u // 2 % 2, u % 2
                    ins = mm(bank[:, :], QA[T][:, pr, j, 128 * qt:128 * qt + 128], KA[T][:, pr, :])
                ins.then_inc(s_full[r["bank"]], 1)

            def step_nmt(s, r, p):
                par = s[3] % 2
                pe.wait_ge(nm_split[par], r["mx"] + 1)
                pe.wait_ge(m_free[r["bank"]], r["free"])
                bank, fullsem = PM[r["bank"]], m_full[r["bank"]]
                o = bank[0:12, 0:128].bitcast(bf16)
                for qt in range(QT):
                    ins = pe.transpose(o[:, 128 * qt:128 * qt + 128], nms[par][:, qt, :, :, :].rearrange("q j t p -> q (j t p)"), identb[:, :])
                ins.then_inc(fullsem, 1)

            def step_st(s, r, p):
                T, q, u, par = s[1], s[3], s[4], s[3] % 2
                pe.wait_ge(nm_in[par], 32 * r["mx"])
                pe.wait_ge(st_free[r["bank"]], r["free"])
                bank = PST[r["bank"]]
                if T == "s":
                    pr = 2 * q + u // 2
                    if u % 2 == 0:
                        ins = mm(bank[:, :], KA[T][:, pr, 0:128], QA[T][:, pr, :, :].rearrange("k j n -> k (j n)"))
                    else:
                        ins = mm(bank[:, 0:256].rearrange("k (j n) -> k j n", j=2), KA[T][:, pr, 128:256], QA[T][:, pr, :, 128:256])
                else:
                    pr, kt = 2 * q + u // 4, u % 4
                    ins = mm(bank[:, :], KA[T][:, pr, 128 * kt:128 * kt + 128], QA[T][:, pr, :, :].rearrange("k j n -> k (j n)"))
                ins.then_inc(st_full[r["bank"]], 1)

            def step_pv(s, r, p):
                T, q, kt, par = s[1], s[3], s[4], s[3] % 2
                if kt == 0:
                    pe.wait_ge(st_free[0], r["st0"])
                    pe.wait_ge(st_free[1], r["st1"])
                    pe.wait_ge(st_free[2], r["st2"])
                    if T == "s":
                        pe.wait_ge(causal_cut, r["t"] * 16 + 4 * (q + 1))
                    if q == 0:
                        pe.wait_ge(m_free[r["v_b"]], r["v"])
                    pe.wait_ge(m_free[r["bank"]], r["free"])
                bank = PM[r["bank"]]
                for c in range(4):
                    pp, j = c // 2, c % 2
                    lhs = V1[T][:, kt, 4 * q + c, :]
                    if T == "s" and kt == 1:
                        o, rhs = bank[32 * c:32 * c + 32, 128:256], PT[par][:, pp, 1, 128 * j:128 * j + 128]
                    elif T == "s":
                        o, rhs = bank[32 * c:32 * c + 32, 0:256], PT[par][:, pp, 0, 256 * j:256 * j + 256]
                    else:
                        o, rhs = bank[32 * c:32 * c + 32, 0:256], PT[par][:, 2 * pp + kt // 2, kt % 2, 256 * j:256 * j + 256]
                    ins = pe.matmul(o, lhs, rhs, start=kt == 0, stop=True, skip_group_check=True)
                if kt == KTS[T] - 1:
                    ins.then_inc(pv_done[par], 1)

            def step_lnt(s, r, p):
                w = s[1]
                pe.wait_ge(z_ok[w], r["n"] + 1)
                pe.wait_ge(m_free[r["bank"]], r["free"])
                transposed(PM[r["bank"]], [zt[w][:, t, :] for t in range(QT)]).then_inc(m_full[r["bank"]], 1)

            def step_qk(s, r, p):
                if r["in_b"] != r["bank"]:
                    pe.wait_ge(m_free[r["in_b"]], r["in"])
                pe.wait_ge(m_free[r["bank"]], r["free"])
                bank, fullsem = PM[r["bank"]], m_full[r["bank"]]
                mm(bank[:, 0:LQ], wqp["s"][:, :], nxT[0][:, :])
                mm(bank[:, LQ:2 * LQ], wkp["s"][:, :], nxT[0][:, :]).then_inc(fullsem, 1)

            def step_q(s, r, p):
                if r["in_b"] != r["bank"]:
                    pe.wait_ge(m_free[r["in_b"]], r["in"])
                pe.wait_ge(m_free[r["bank"]], r["free"])
                bank, fullsem = PM[r["bank"]], m_full[r["bank"]]
                mm(bank[:, 0:LQ], wqp[p][:, :], (nxT[1] if p == 1 else yT1)[:, :]).then_inc(fullsem, 1)

            def step_k(s, r, p):
                if r["in_b"] != r["bank"]:
                    pe.wait_ge(m_free[r["in_b"]], r["in"])
                pe.wait_ge(m_free[r["bank"]], r["free"])
                bank, fullsem = PM[r["bank"]], m_full[r["bank"]]
                mm(bank[:, :], wkp[p][:, :], ctxT[s[1]][:, :]).then_inc(fullsem, 1)

            def step_v(s, r, p):
                if r["in_b"] != r["bank"]:
                    pe.wait_ge(m_free[r["in_b"]], r["in"])
                pe.wait_ge(m_free[r["bank"]], r["free"])
                bank, fullsem = PM[r["bank"]], m_full[r["bank"]]
                T = s[1]
                src = nxT[0] if T == "s" else ctxT[T]
                w = w_qkv[:, 2 * D:3 * D] if T == "s" else (w_kv0[:, D:2 * D] if p == 1 else wv2[:, :])
                for t in range(KTS[T]):
                    ins = mm(bank[:, D * t:D * t + D], src[:, 128 * t:128 * t + 128], w)
                ins.then_inc(fullsem, 1)

            def step_outa(s, r, p):
                if r["in_b"] != r["bank"]:
                    pe.wait_ge(m_free[r["in_b"]], r["in"])
                qt = s[3]
                pe.wait_ge(m_free[r["bank"]], r["free"])
                transposed(PM[r["bank"]], [CT[s[1]][:, g, 128 * qt:128 * qt + 128] for g in range(NQUAD)]).then_inc(m_full[r["bank"]], 1)

            def step_outb(s, r, p):
                if r["in_b"] != r["bank"]:
                    pe.wait_ge(m_free[r["in_b"]], r["in"])
                pe.wait_ge(m_free[r["bank"]], r["free"])
                transposed(PM[r["bank"]], [cn[:, t, :] for t in range(QT)]).then_inc(m_full[r["bank"]], 1)

            def step_outc(s, r, p):
                if r["in_b"] != r["bank"]:
                    pe.wait_ge(m_free[r["in_b"]], r["in"])
                pe.wait_ge(m_free[r["bank"]], r["free"])
                bank, fullsem = PM[r["bank"]], m_full[r["bank"]]
                w = w_so if s[1] == "s" else (w_co if p == 1 else wo2)
                for t in range(QT):
                    ins = mm(bank[:, D * t:D * t + D], cnT[:, 128 * t:128 * t + 128], w[:, :])
                ins.then_inc(fullsem, 1)

            def step_ct(s, r, p):
                pe.wait_ge(c_in, 16 * (r["n"] + 1 + (B if p == 2 else 0)))
                pe.wait_ge(m_free[r["bank"]], r["free"])
                transposed(PM[r["bank"]], [cin[:, t, :] for t in range(KT)]).then_inc(m_full[r["bank"]], 1)

            def step_ff1(s, r, p):
                if r["in_b"] != r["bank"]:
                    pe.wait_ge(m_free[r["in_b"]], r["in"])
                pe.wait_ge(m_free[r["bank"]], r["free"])
                bank, fullsem = PM[r["bank"]], m_full[r["bank"]]
                for k in range(2):
                    blk = 2 * s[3] + k
                    ins = mm(bank[:, LQ * k:LQ * k + LQ], w1[:, 128 * blk:128 * blk + 128], nxT[2][:, :])
                ins.then_inc(fullsem, 1)

            def step_ff2(s, r, p):
                if r["in_b"] != r["bank"]:
                    pe.wait_ge(m_free[r["in_b"]], r["in"])
                pe.wait_ge(m_free[r["bank"]], r["free"])
                bank, fullsem = PM[r["bank"]], m_full[r["bank"]]
                for t in range(QT):
                    o = bank[:, D * t:D * t + D]
                    mm(o, ones1[:, :], b2[:, :], True, False)
                    for blk in range(F // 128):
                        ins = mm(o, hT[:, blk, 128 * t:128 * t + 128], w2[:, blk, :], False, blk == F // 128 - 1)
                ins.then_inc(fullsem, 1)

            def step_xt(s, r, p):
                pe.wait_ge(xs_in, 16 * (r["n"] + 1))
                pe.wait_ge(m_free[r["bank"]], r["free"])
                transposed(PM[r["bank"]], [xl1[:, t, :] for t in range(QT)]).then_inc(m_full[r["bank"]], 1)

            def step_g1(s, r, p):
                if r["in_b"] != r["bank"]:
                    pe.wait_ge(m_free[r["in_b"]], r["in"])
                if r["in2_b"] != r["bank"]:
                    pe.wait_ge(m_free[r["in2_b"]], r["in2"])
                pe.wait_ge(m_free[r["bank"]], r["free"])
                bank, fullsem = PM[r["bank"]], m_full[r["bank"]]
                if s[3] == 0:
                    ins = mm(bank[:, 0:LQ], l1w[:, 0, :], xT1[:, :])
                elif s[3] == 1:
                    ins = mm(bank[:, :], l1w[:, 1, :], ctxT[s[1]][:, :])
                else:
                    mm(bank[:, :], ones1[:, :], bv4[:, :, :].rearrange("o t d -> o (t d)"), True, False)
                    for t in range(KT):
                        ins = pe.matmul(bank[:, D * t:D * t + D], ctxT[s[1]][:, 128 * t:128 * t + 128], l1w[:, 2, :], start=False, stop=True,
                                        skip_group_check=True)
                ins.then_inc(fullsem, 1)

            def step_l1s(s, r, p):
                if r["in_b"] != r["bank"]:
                    pe.wait_ge(m_free[r["in_b"]], r["in"])
                pe.wait_ge(m_free[r["bank"]], r["free"])
                bank, fullsem = PM[r["bank"]], m_full[r["bank"]]
                mm(bank[:, :], q1T[:, 128 * s[3]:128 * s[3] + 128], k1T[:, :]).then_inc(fullsem, 1)

            def step_l1t(s, r, p):
                if r["in_b"] != r["bank"]:
                    pe.wait_ge(m_free[r["in_b"]], r["in"])
                pe.wait_ge(m_free[r["bank"]], r["free"])
                transposed(PM[r["bank"]], [P1[:, s[3], 128 * t:128 * t + 128] for t in range(KT)]).then_inc(m_full[r["bank"]], 1)

            def step_l1a(s, r, p):
                if r["in_b"] != r["bank"]:
                    pe.wait_ge(m_free[r["in_b"]], r["in"])
                pe.wait_ge(m_free[r["bank"]], r["free"])
                bank, fullsem = PM[r["bank"]], m_full[r["bank"]]
                for t in range(KT):
                    ins = mm(bank[:, 0:LQ], v1[:, t, :], P1T[:, t, :], t == 0, t == KT - 1)
                ins.then_inc(fullsem, 1)

            def step_l1o(s, r, p):
                if r["in_b"] != r["bank"]:
                    pe.wait_ge(m_free[r["in_b"]], r["in"])
                pe.wait_ge(m_free[r["bank"]], r["free"])
                bank, fullsem = PM[r["bank"]], m_full[r["bank"]]
                for t in range(QT):
                    ins = mm(bank[:, D * t:D * t + D], attT[:, 128 * t:128 * t + 128], l1w[:, 3, :])
                ins.then_inc(fullsem, 1)

            def step_yt(s, r, p):
                pe.wait_ge(y_ok[3], r["n"] + 1)
                pe.wait_ge(m_free[r["bank"]], r["free"])
                transposed(PM[r["bank"]], [y1[s[1]][:, t, :] for t in range(QT)]).then_inc(m_full[r["bank"]], 1)

            def step_y2t(s, r, p):
                pe.wait_ge(y_ok[4], r["n"] + 1)
                pe.wait_ge(m_free[r["bank"]], r["free"])
                transposed(PM[r["bank"]], [y2[:, t, :] for t in range(QT)]).then_inc(m_full[r["bank"]], 1)

            def step_ct3(s, r, p):
                pe.wait_ge(c3_in, 16 * (r["n"] + 1))
                pe.wait_ge(m_free[r["bank"]], r["free"])
                transposed(PM[r["bank"]], [cin3[:, t, :] for t in range(KT)]).then_inc(m_full[r["bank"]], 1)

            def step_l3s(s, r, p):
                if r["in_b"] != r["bank"]:
                    pe.wait_ge(m_free[r["in_b"]], r["in"])
                if r["in2_b"] != r["bank"]:
                    pe.wait_ge(m_free[r["in2_b"]], r["in2"])
                pe.wait_ge(m_free[r["bank"]], r["free"])
                bank, fullsem = PM[r["bank"]], m_full[r["bank"]]
                mm(bank[:, :], y2T[:, 128 * s[3]:128 * s[3] + 128], ctxT3[:, :]).then_inc(fullsem, 1)

            def step_l3t(s, r, p):
                pe.wait_ge(p3_ok, r["n"] + 1)
                pe.wait_ge(m_free[r["bank"]], r["free"])
                transposed(PM[r["bank"]], [P3[:, s[3], 128 * t:128 * t + 128] for t in range(KT)]).then_inc(m_full[r["bank"]], 1)

            def step_l3a(s, r, p):
                if r["in_b"] != r["bank"]:
                    pe.wait_ge(m_free[r["in_b"]], r["in"])
                pe.wait_ge(m_free[r["bank"]], r["free"])
                bank, fullsem = PM[r["bank"]], m_full[r["bank"]]
                for t in range(KT):
                    ins = mm(bank[:, 0:LQ], cin3[:, t, :], P3T[:, t, :], t == 0, t == KT - 1)
                ins.then_inc(fullsem, 1)

            def step_l3h(s, r, p):
                if r["in_b"] != r["bank"]:
                    pe.wait_ge(m_free[r["in_b"]], r["in"])
                pe.wait_ge(m_free[r["bank"]], r["free"])
                bank, fullsem = PM[r["bank"]], m_full[r["bank"]]
                for t in range(QT):
                    mm(bank[:, D * t:D * t + D], y2T[:, 128 * t:128 * t + 128], tw[:, 0, :], True, False)
                    ins = mm(bank[:, D * t:D * t + D], tiT[:, 128 * t:128 * t + 128], tw[:, 1, :], False, True)
                ins.then_inc(fullsem, 1)

            walk(pe, {"WT": step_wt, "S": step_s, "NMT": step_nmt, "ST": step_st, "PV": step_pv, "LNT": step_lnt, "QK": step_qk,
                      "Q": step_q, "K": step_k, "V": step_v, "OUTA": step_outa, "OUTB": step_outb, "OUTC": step_outc, "CT": step_ct,
                      "FF1": step_ff1, "FF2": step_ff2, "XT": step_xt, "G1": step_g1, "L1S": step_l1s, "L1T": step_l1t,
                      "L1A": step_l1a, "L1O": step_l1o, "YT": step_yt, "Y2T": step_y2t, "CT3": step_ct3, "L3S": step_l3s,
                      "L3T": step_l3t, "L3A": step_l3a, "L3H": step_l3h})


_INS = ["x", "ctx_1024", "mask_Bx1x1xS2_ff0"] + [f"L0_xattn_{n}" for n in (
    "W_qkv", "W_self_out", "W_q", "W_kv", "W_cross_out", "W1", "b1", "W2", "b2", "ln1_scale", "ln1_bias", "ln2_scale",
    "ln2_bias", "ln3_scale", "ln3_bias")] + [f"L1_xattn_{n}" for n in (
        "Wq", "bq", "Wk", "bk", "Wv", "bv", "Wf", "bf", "ln_gamma", "ln_beta")] + [f"L2_xattn_{n}" for n in (
            "Wq", "Wk", "Wv", "Wo", "gamma", "beta")] + ["L3_xattn_trans_W", "L3_xattn_trans_b"]


def kernel(**inputs):
    import numpy as _np
    import concourse.bacc as _bacc
    from concourse import mybir as _mybir
    from concourse.bass_utils import run_bass_kernel_spmd as _run

    nc = _bacc.Bacc("TRN2", target_bir_lowering=False, num_devices=1)
    arrays, args = {}, {}
    for name in _INS:
        arr = _np.ascontiguousarray(inputs[name])
        arrays[f"in_{name}"] = arr
        args[name] = nc.dram_tensor(f"in_{name}", arr.shape, _mybir.dt.from_np(arr.dtype), kind="ExternalInput").ap()
    o = nc.dram_tensor("out_0", (B, LQ, D), _mybir.dt.float32, kind="ExternalOutput").ap()
    program(nc, args, o)
    r = _run(nc, [arrays], core_ids=[0])
    return r.results[0]["out_0"]
```

```python
from contextlib import ExitStack

import numpy as np
import concourse.bass as bass
from concourse import mybir
from concourse.alu_op_type import AluOpType as ALU

B, LQ, LK, D = 8, 256, 512, 128
NH, DH = 16, 8
NPAIR, NQUAD = NH // 2, NH // 4
QT, KT = LQ // 128, LK // 128
F = 512
GROUPS = 8
HB = 64
R_MAX, R_MASK = 48, 51
NEG = -1.0e9
Q_PARTS = (0, 0, 0, 1, 1, 2)
K_PARTS = (0, 1, 2, 0, 1, 0)
N_PS, N_PST, N_PM = 3, 2, 3
S_USES = {"s": 4, "c": 8, "d": 8}
ST_UNITS = {"s": 4, "c": 8, "d": 8}
KTS = {"s": 2, "c": 4, "d": 4}
LATER_LOADS = (-12, -9, -8, -7, -5, -3, 1, 2)
TURN = "dc"
SPAN = {
    ("S", "c"): (-0.1, 0.9), ("S", "d"): (-0.05, 0.8),
    ("NM", "s"): (1.0, 1.0), ("NM", "c"): (1.0, 1.0), ("NM", "d"): (1.0, 1.0),
    ("NMT", "s"): (0.1, 0.1), ("NMT", "c"): (0.3, 0.3), ("NMT", "d"): (0.4, 0.4),
    ("ST", "s"): (0.05, 1.0),
    ("PV", "s"): (0.3, 1.2), ("PV", "c"): (0.3, 1.3), ("PV", "d"): (0.4, 1.3),
    ("PVC", "s"): (0.1, 0.1), ("PVC", "c"): (0.0, 0.0), ("PVC", "d"): (0.0, 0.0),
    ("OUTA", "s"): (0.15, 1.2), ("OUTA", "c"): (0.15, 1.0), ("OUTA", "d"): (0.05, 1.0),
    ("CT", 0): (-0.1, 1.2),
    ("FF1", 0): (0.0, 0.95),
    ("L1A", "c"): (-0.2, 1.0),
    ("L3H", "c"): (0.2, 1.0),
    ("L3T", "d"): (0.05, 1.0),
    ("LNZ", 0): (-0.2, 1.0),
    ("QL", "c"): (0.0, 0.9),
    ("XLN", 0): (0.2, 1.0),
    ("XT", "c"): (0.1, 1.0), ("XT", "d"): (0.0, 1.1),
    ("Y1B", "c"): (0.1, 1.0),
}



def all_slots():
    slots = {}

    def put(slot, p, *steps):
        first = steps[0]
        slots.setdefault(slot, []).append((SPAN.get(first[:2], (0.0, 1.0)), [[(x, p) for x in (g if isinstance(g, list) else [g])] for g in steps]))

    def attention(base, p, T, n):
        for q in range(NQUAD):
            k = base + q
            put(k, p, *[("S", T, n, q, u) for u in range(S_USES[T])])
            put(k, p, ("NM", T, n, q, 0))
            put(k + 1, p, ("NMT", T, n, q, 0))
            put(k + 2, p, *[("ST", T, n, q, u) for u in range(ST_UNITS[T])])
            put(k + 3, p, *[("PV", T, n, q, u) for u in range(KTS[T])])
            put(k + 4, p, ("PVC", T, n, q, 0))

    for n in range(B):
        s, c = 8 * n - 8, 8 * n
        put(s - 7, 1, ("XLN", 0, n, 0, 0))
        put(s - 5, 1, ("LNS", 0, n, 0, 0))
        put(s - 4, 1, ("LNZ", 0, n, 0, 0), ("LNT", 0, n, 0, 0), ("QK", "s", n, 0, 0), ("QKW", "s", n, 0, 0))
        put(s - 2, 1, ("QKL", "s", n, 0, 0))
        put(s, 1, ("V", "s", n, 0, 0))
        attention(s, 1, "s", n)
        put(s + 1, 1, ("XR", 0, n, 0, 0))
        put(c - 5, 1, ("CL", 0, n, 0, 0))
        put(s + 7, 1, ("OUTA", "s", n, 0, 0), ("OUTA", "s", n, 1, 0), ("OUTB", "s", n, 0, 0), ("OUTC", "s", n, 0, 0))
        put(c, 1, ("LNS", 1, n, 0, 0), ("LNZ", 1, n, 0, 0))
        put(c - 3, 1, ("CT", 0, n, 0, 0))
        put(c - 2, 1, ("K", "c", n, 0, 0), ("KW", "c", n, 0, 0))
        put(c + 1, 1, ("LNT", 1, n, 0, 0), ("Q", "c", n, 0, 0), ("QW", "c", n, 0, 0))
        put(c + 2, 1, ("KL", "c", n, 0, 0))
        put(c + 3, 1, ("QL", "c", n, 0, 0), ("V", "c", n, 0, 0))
        put(c + 5, 1, ("X1B", 0, n, 0, 0))
        attention(c + 4, 1, "c", n)
        put(c + 11, 1, ("OUTA", "c", n, 0, 0), ("OUTA", "c", n, 1, 0), ("OUTB", "c", n, 0, 0), ("OUTC", "c", n, 0, 0))
        put(c + 12, 1, ("LNS", 2, n, 0, 0), ("LNZ", 2, n, 0, 0), ("LNT", 2, n, 0, 0))
        put(c + 13, 1, ("FF1", 0, n, 0, 0), ("FF1", 0, n, 1, 0), ("FF2", 0, n, 0, 0))
    for m in range(-2, B):
        k, T = 8 * B + 4 * m, TURN[m % 2]
        put(k - 7, 2, ("XS", T, m, 0, 0), ("CL", 0, m, 0, 0))
        put(k - 6, 2, ("XT", T, m, 0, 0), ("CT", 0, m, 0, 0), [("G1", T, m, u, 0) for u in range(3)])
        put(k - 5, 2, ("L1S", T, m, 0, 0), ("L1S", T, m, 1, 0), ("L1T", T, m, 0, 0), ("L1T", T, m, 1, 0), ("K", T, m, 0, 0))
        put(k - 4, 2, ("L1A", T, m, 0, 0), ("KW", T, m, 0, 0), ("L1O", T, m, 0, 0), ("LNS", 3, m, 0, 0), ("LNZ", 3, m, 0, 0), ("LNG", 3, m, 0, 0))
        put(k - 3, 2, ("YT", T, m, 0, 0), ("Q", T, m, 0, 0), ("QW", T, m, 0, 0))
        put(k - 2, 2, ("KL", T, m, 0, 0), ("QL", T, m, 0, 0))
        put(k, 2, ("V", T, m, 0, 0))
        put(k, 2, ("Y1B", T, m, 0, 0))
        if m >= 0:
            attention(k, 2, T, m)
        if m >= 0:
            put(k + 7, 2, ("OUTA", T, m, 0, 0), ("OUTA", T, m, 1, 0), ("OUTB", T, m, 0, 0), ("OUTC", T, m, 0, 0))
        put(k + 8, 2, ("LNS", 4, m, 0, 0), ("CL3", T, m, 0, 0), ("LNZ", 4, m, 0, 0), ("LNG", 4, m, 0, 0))
        put(k + 9, 2, ("CT3", T, m, 0, 0), ("Y2T", T, m, 0, 0), ("L3S", T, m, 0, 0), ("L3S", T, m, 1, 0), ("L3N", T, m, 0, 0))
        put(k + 10, 2, ("L3T", T, m, 0, 0), ("L3T", T, m, 1, 0), ("L3A", T, m, 0, 0))
        put(k + 11, 2, ("L3H", T, m, 0, 0))
    for g, slot in enumerate(LATER_LOADS):
        put(slot, 1, ("LD", 0, 0, g, 0))
    put(-4, 1, ("WB", 0, 0, 0, 0))
    put(4, 1, ("WT", 0, 0, 0, 0))
    return slots


def in_order(lanes):
    marks = [(lo + (hi - lo) * (k + 0.5) / len(groups), n, k, g)
             for n, ((lo, hi), groups) in enumerate(lanes) for k, g in enumerate(groups)]
    return [x for *_, g in sorted(marks, key=lambda m: m[:3]) for x in g]


MISC = {"NMT", "PV", "LNT", "QK", "K", "Q", "V", "OUTA", "OUTB", "OUTC", "CT", "FF1", "FF2", "WT", "XT", "G1", "L1S",
        "L1T", "L1A", "L1O", "YT", "CT3", "Y2T", "L3S", "L3T", "L3A", "L3H"}


class Counts:

    def __init__(self):
        self.misc = self.s = self.st = 0
        self.misc_used, self.misc_full = [0] * N_PM, [0] * N_PM
        self.s_used, self.st_used = [0] * N_PS, [0] * N_PST
        self.pt_used, self.mx_used = [0, 0], [0, 0]
        self.quads = {"s": 0, "c": 0, "d": 0}
        self.writes = {"s": 0, "k": 0, "q": 0}
        self.st_mark, self.done = {}, {}
        self.nT, self.scored = {}, {}
        self.last_load = {}

    def resolve(self, step, phase, beside=False):
        kind, T, n, q, u = step
        r = {"n": n}
        if phase == 2:
            r["j"] = n // 2
        key = (phase, T, n)
        if T in ("s", "c", "d") and kind in ("S", "NM", "NMT", "ST", "PV", "QL", "KL", "QKL", "V", "OUTA", "OUTB", "OUTC"):
            if key not in self.nT:
                self.nT[key] = self.quads[T]
                self.quads[T] += 1
            r["t"] = self.nT[key]
        if kind == "PVC":
            r["bank"], r["pt"] = N_PM - 1, self.nT[(phase, "pt", T, n, q)]
        elif kind == "PV" and u:
            r["bank"] = N_PM - 1
        elif kind in MISC:
            b = N_PM - 1 if kind == "PV" else self.misc % (N_PM - 1)
            self.misc += kind != "PV" and not beside
            r["bank"], r["free"] = b, self.misc_used[b]
            self.misc_used[b] += 1
            if kind != "PV":
                self.misc_full[b] += 1
                r["full"] = self.misc_full[b]
            self.done[(phase, kind, T, n, q)] = (b, self.misc_used[b])
        if kind == "S":
            b = self.s % N_PS
            self.s += 1
            r["bank"], r["free"] = b, self.s_used[b]
            self.s_used[b] += 1
            if u == 0:
                r["mx"] = self.mx_used[q % 2]
        if kind == "S":
            self.scored[T, n, q] = u + 1
        if kind == "NM":
            assert self.scored[T, n, q] == S_USES[T], step
            r["s0"], r["s1"], r["s2"] = self.s_used
        if kind == "NMT":
            r["mx"] = self.mx_used[q % 2]
            self.mx_used[q % 2] += 1
            self.done[(phase, "MX", T, n, q)] = (q % 2, self.mx_used[q % 2])
        if kind == "ST":
            b = self.st % N_PST
            self.st += 1
            r["bank"], r["free"] = b, self.st_used[b]
            self.st_used[b] += 1
            r["mx"] = self.done[(phase, "MX", T, n, q)][1]
            if u == 0:
                r["pt"] = self.pt_used[q % 2]
            if u == ST_UNITS[T] - 1:
                self.done[(phase, "EXP", T, n, q)] = tuple(self.st_used)
        if kind == "PV" and not u:
            self.pt_used[q % 2] += 1
            r["pt"] = self.nT[(phase, "pt", T, n, q)] = self.pt_used[q % 2]
            r["st0"], r["st1"] = self.done[(phase, "EXP", T, n, q)]
        if kind in ("QK", "K", "Q"):
            w = {"QK": "s", "K": "k", "Q": "q"}[kind]
            r["w"] = self.writes[w]
            self.writes[w] += 1
            self.nT[(phase, "w", w, T, n)] = r["w"]
        if kind in ("QKW", "QKL", "KW", "KL", "QW", "QL"):
            r["w"] = self.nT[(phase, "w", {"QK": "s", "K": "k", "Q": "q"}[kind[:-1]], T, n)]
        if kind in ("QKW", "KW", "QW"):
            r["ldT_b"], r["ld"] = self.last_load.get(kind[:-1], (0, 0))
        if kind in ("QKL", "KL", "QL"):
            self.last_load[kind[:-1]] = ("scd".index(T), 32 * (r["t"] + 1))
            before = self.last_exp(T)
            r["e0"], r["e1"] = before
        ins = self.inputs(step, phase)
        for name, src in ins.items():
            assert src in self.done or src[3] < 0, (step, src)
            r[name + "_b"], r[name] = self.done.get(src, (0, 0))
        return r

    def last_exp(self, T):
        best = (0,) * N_PST
        for k, v in self.done.items():
            if k[1] == "EXP" and (k[2] == "c") == (T == "c"):
                best = max(best, v)
        return best

    def inputs(self, step, phase):
        kind, T, n, q, u = step
        p = phase
        if kind == "QK":
            return {"in": (p, "LNT", 0, n, 0)}
        if kind == "Q":
            return {"in": (p, "LNT", 1, n, 0)} if p == 1 else {"in": (p, "YT", T, n, 0)}
        if kind == "V":
            return {"in": (p, "LNT", 0, n, 0)} if T == "s" else {"in": (p, "CT", 0, n, 0)}
        if kind == "K":
            return {"in": (p, "CT", 0, n, 0)}
        if kind == "PV" and not u:
            return {"v": (p, "V", T, n, 0)}
        if kind == "OUTA":
            return {"in": (p, "PV", T, n, 3)}
        if kind == "OUTB":
            return {"in": (p, "OUTA", T, n, 1)}
        if kind == "OUTC":
            return {"in": (p, "OUTB", T, n, 0)}
        if kind == "LNS":
            src = {1: (1, "OUTC", "s", n, 0), 2: (1, "OUTC", "c", n, 0), 3: (2, "L1O", TURN[n % 2], n, 0), 4: (2, "OUTC", TURN[n % 2], n, 0)}.get(T)
            return {"in": src} if src else {}
        if kind == "X1B":
            return {"in": (1, "OUTC", "s", n, 0), "prev": (1, "OUTC", "c", n - 1, 0)}
        if kind == "Y1B":
            return {"prev": (2, "OUTC", T, n - 2, 0)}
        if kind == "FF1":
            return {"in": (p, "LNT", 2, n, 0)}
        if kind == "FF2":
            return {"in": (p, "FF1", 0, n, 1)}
        if kind == "CL":
            return {"prev": (p, "CT", 0, n - 1, 0)} if p == 1 or n else {"prev": (1, "CT", 0, B - 1, 0)}
        if kind == "XR":
            return {"prev": (1, "OUTC", "s", n - 1, 0)}
        if kind == "XS":
            return {"prev": (p, "L1O", TURN[(n - 1) % 2], n - 1, 0)}
        if kind == "G1":
            return {"in": (p, "XT", T, n, 0), "in2": (p, "CT", 0, n, 0)}
        if kind == "L1S":
            return {"in": (p, "G1", T, n, 1)}
        if kind == "L1T":
            return {"in": (p, "L1S", T, n, q)}
        if kind == "L1A":
            return {"in": (p, "L1T", T, n, 1)}
        if kind == "L1O":
            return {"in": (p, "L1A", T, n, 0)}
        if kind == "L3S":
            return {"in": (p, "Y2T", T, n, 0), "in2": (p, "CT3", T, n, 0)}
        if kind == "L3N":
            return {"in": (p, "L3S", T, n, 1), "in2": (p, "L3S", T, n, 0)}
        if kind == "L3A":
            return {"in": (p, "L3T", T, n, 1)}
        if kind == "L3H":
            return {"in": (p, "L3A", T, n, 0)}
        return {}


def build_schedule():
    counts = Counts()
    slots = all_slots()
    chunks = {}
    for slot in sorted(slots):
        chunks.setdefault(slot // 8, []).extend(in_order(slots[slot]))
    its = []
    for c in sorted(chunks):
        counts.misc = counts.s = counts.st = 0
        its.append([])
        for s, p in chunks[c]:
            if s[2] < 0:
                counts.misc += s[0] in MISC
            else:
                its[-1].append((s, counts.resolve(s, p, c >= B and p == 1 and s[0] in ("LNT", "FF1", "FF2")), p))
    parts, k = [], 0
    while k < len(its):
        run = 1

        def shape(it):
            return [(s[0], s[1], s[3], s[4], sorted(r), p) for s, r, p in it]

        def diff(x, y):
            return [r1[v] - r0[v] for (_, r0, _), (_, r1, _) in zip(x, y) for v in sorted(r0)]

        while k + run < len(its) and shape(its[k + run]) == shape(its[k]):
            if run >= 2 and diff(its[k + run - 1], its[k + run]) != diff(its[k], its[k + 1]):
                break
            run += 1
        first = its[k]
        second = its[k + 1] if run > 1 else first
        banks = all(r0[x] == r1[x] for (_, r0, _), (_, r1, _) in zip(first, second) for x in r0 if x == "bank" or x.endswith("_b"))
        if run < 2 or not banks:
            run = 1
            second = first
        parts.append((run, [(s, {x: (r0[x], r1[x] - r0[x]) for x in r0}, p) for (s, r0, p), (_, r1, _) in zip(first, second)]))
        k += run
    return parts


def program(nc, a, out):
    f32, bf16 = mybir.dt.float32, mybir.dt.bfloat16
    ACT = mybir.ActivationFunctionType
    X = mybir.AxisListType.X
    parts = build_schedule()

    with ExitStack() as ctx:
        def sb(name, shape, dt=f32):
            return ctx.enter_context(nc.sbuf_tensor(name, shape, dt))

        def sem(name):
            return ctx.enter_context(nc.semaphore(name))

        def row(name, n):
            return a[name].rearrange("(o n) -> o n", o=1).to_broadcast([128, n])

        ident, identb = sb("ident", [128, 128]), sb("identb", [128, 128], bf16)
        causal = sb("causal", [128, 2 * 128])
        ones1 = sb("ones1", [1, 128])
        half = sb("half", [128, 2])
        w_qkv, w_kv0 = sb("w_qkv", [128, 3 * D]), sb("w_kv0", [128, 2 * D])
        w_q0 = sb("w_q0", [128, D])
        wqp = {"s": sb("wqp_s", [128, D]), 1: sb("wqp_1", [128, D]), 2: sb("wqp_2", [128, D])}
        wkp = {"s": sb("wkp_s", [128, D]), 1: sb("wkp_1", [128, D]), 2: sb("wkp_2", [128, D])}
        wv2, wo2 = sb("wv2", [128, D]), sb("wo2", [128, D])
        w_so, w_co = sb("w_so", [128, D]), sb("w_co", [128, D])
        w1, w2 = sb("w1", [128, F]), sb("w2", [128, F // 128, D])
        b1 = sb("b1", [128, F // 128])
        b2 = sb("b2", [1, D])
        lng, lnb = sb("lng", [128, 3]), sb("lnb", [128, 3])
        l1w = sb("l1w", [128, 4, D])
        l1b = sb("l1b", [128, 2])
        bv4 = sb("bv4", [1, KT, D])
        bfb = sb("bfb", [128, D])
        gb = {3: (sb("g3", [128, D]), sb("be3", [128, D])), 4: (sb("g4", [128, D]), sb("be4", [128, D]))}
        tw = sb("tw", [128, 2, D])
        tbb = sb("tbb", [128, D])

        QA = {T: sb(f"QA_{T}", [128, NPAIR, 2, LQ], bf16) for T in "cd"}
        KA = {T: sb(f"KA_{T}", [128, NPAIR, LK], bf16) for T in "cd"}
        V1 = {T: sb(f"V1_{T}", [128, KT, NH, 32]) for T in "cd"}
        CT = {T: sb(f"CT_{T}", [128, NQUAD, LQ]) for T in "cd"}
        for of in (QA, KA, V1, CT):
            of["s"] = of["d"]
        nk = {"s": LQ, "c": LK, "d": LK}
        PT = [sb(f"PT{k}", [128, 4, 2, 512]) for k in range(2)]
        first = PT[0][:, :, :, :].rearrange("k a b n -> k (a b n)")
        kone = first[0:16, 0:LK // 2].bitcast(bf16)
        qone = first[0:16, LK // 2:LK // 2 + LQ // 2].bitcast(bf16)
        mx = [sb(f"mx{k}", [128, QT, 2, 2]) for k in range(2)]
        nr = [sb(f"nr{k}", [128, QT, 2, 2]) for k in range(2)]
        nms = [sb(f"nms{k}", [128, QT, 2, 3, 2], bf16) for k in range(2)]
        nmt = [sb(f"nmt{k}", [12, LQ], bf16) for k in range(2)]
        junk = sb("junk", [128, N_PS, 384], bf16)
        width = {"s": 2 * LQ, "k": LK, "q": LQ}
        full32 = {w: sb(f"f32_{w}", [128, width[w]]) for w in "skq"}
        rest32 = {w: sb(f"r32_{w}", [128, width[w]]) for w in "skq"}
        split = {w: sb(f"split_{w}", [128, 3, width[w]], bf16) for w in "skq"}
        rr = sb("rr", [128, QT, NQUAD, 4])
        cn, cnT = sb("cn", [128, QT, D]), sb("cnT", [128, LQ])

        xln, xr, x1, x1b, x2, x3 = (sb(n, [128, QT, D]) for n in ("xln", "xr", "x1", "x1b", "x2", "x3"))
        bst = sb("bst", [128, QT, 6])
        mv = [sb(f"mv{w}", [128, QT, 2]) for w in range(5)]
        ve = [sb(f"ve{w}", [128, QT]) for w in range(5)]
        rstd = [sb(f"rstd{w}", [128, QT]) for w in range(5)]
        zt = [sb(f"zt{w}", [128, QT, D]) for w in range(5)]
        nxT = [sb(f"nxT{w}", [128, LQ]) for w in range(3)]
        hT = sb("hT", [128, F // 128, LQ])
        cin, cin3 = sb("cin", [128, KT, D]), sb("cin3", [128, KT, D])
        ctxT = {T: sb(f"ctxT_{T}", [128, LK]) for T in "cd"}
        ctxT3 = sb("ctxT3", [128, LK])
        xl1, xb1, xo1 = (sb(n, [128, QT, D]) for n in ("xl1", "xb1", "xo1"))
        xT1, q1T, k1T, v1 = sb("xT1", [128, LQ]), sb("q1T", [128, LQ]), sb("k1T", [128, LK]), sb("v1", [128, KT, D])
        nm1, rs1, rr1 = sb("nm1", [128, QT]), sb("rs1", [128, QT]), sb("rr1", [128, QT])
        P1, P1T, attT = sb("P1", [128, QT, LK]), sb("P1T", [128, KT, LQ]), sb("attT", [128, LQ])
        y1 = {T: sb(f"y1_{T}", [128, QT, D]) for T in "cd"}
        yT1 = sb("yT1", [128, LQ])
        y1b = {T: sb(f"y1b_{T}", [128, QT, D]) for T in "cd"}
        xo2, y2, y2T = sb("xo2", [128, QT, D]), sb("y2", [128, QT, D]), sb("y2T", [128, LQ])
        nm3, rs3, rr3 = sb("nm3", [128, QT]), sb("rs3", [128, QT]), sb("rr3", [128, QT])
        P3, P3T, tiT = sb("P3", [128, QT, LK]), sb("P3T", [128, KT, LQ]), sb("tiT", [128, LQ])
        hb, ob = sb("hb", [128, QT, D]), sb("ob", [128, QT, D])
        mk, mkr = P1[0:B, 0, :], P1[0:B, 1, :]
        mkp = P3T[0:B, :, :].rearrange("b t n -> b (t n)")[:, 0:3 * LK // 2].bitcast(bf16).rearrange("b (t n) -> b t n", t=3)
        w2raw = P3[:, 0, :].rearrange("k (t n) -> k t n", t=4)

        PS, PST, PM = ([ctx.enter_context(nc.psum_tensor(f"{name}{k}", [128, 512], f32)) for k in range(n)]
                       for name, n in (("PS", N_PS), ("PST", N_PST), ("PM", N_PM)))

        scr = {w: nc.dram_tensor(f"scr_{w}", [GROUPS, 128, n], bf16).ap() for w, n in (("sq", LQ), ("sk", LQ), ("q", LQ), ("k", LK))}
        mscr = nc.dram_tensor("mscr", [B, 3, LK], bf16).ap()
        xs = nc.dram_tensor("xs", [B, 128, QT, D], f32).ap()

        s_full, s_free = [sem(f"s_full{k}") for k in range(N_PS)], [sem(f"s_free{k}") for k in range(N_PS)]
        st_full, st_free = [sem(f"st_full{k}") for k in range(N_PST)], [sem(f"st_free{k}") for k in range(N_PST)]
        m_full, m_free = [sem(f"m_full{k}") for k in range(N_PM)], [sem(f"m_free{k}") for k in range(N_PM)]
        pv_done = [sem(f"pv_done{k}") for k in range(2)]
        nm_split = [sem(f"nm_split{k}") for k in range(2)]
        nm_in = [sem(f"nm_in{k}") for k in range(2)]
        causal_cut = sem("causal_cut")
        q_in = {T: sem(f"q_in_{T}") for T in "scd"}
        k_in = {T: sem(f"k_in_{T}") for T in "scd"}
        split_done = {w: sem(f"split_done_{w}") for w in "skq"}
        scr_in = {w: sem(f"scr_in_{w}") for w in "skq"}
        stats = [sem(f"stats{w}") for w in range(5)]
        rstd_ok = [sem(f"rstd_ok{w}") for w in range(5)]
        z_ok = [sem(f"z_ok{w}") for w in range(5)]
        y_ok = {3: sem("y_ok3"), 4: sem("y_ok4")}
        x_in, xr_in, c_in, xs_in, c3_in = sem("x_in"), sem("xr_in"), sem("c_in"), sem("xs_in"), sem("c3_in")
        x1b_ok, xb_ok, y1b_ok = sem("x1b_ok"), sem("xb_ok"), {T: sem(f"y1b_ok_{T}") for T in "cd"}
        xs_out = sem("xs_out")
        nm1_ok, nm3_ok = sem("nm1_ok"), sem("nm3_ok")
        rr3_ok, th_ok = sem("rr3_ok"), sem("th_ok")
        p3_ok, ob_ok, out_ok = sem("p3_ok"), sem("ob_ok"), sem("out_ok")
        mask_in = sem("mask_in")
        w_in = [sem(f"w_in{k}") for k in range(3)]
        mask_split, zero_c, wqk_c = sem("mask_split"), sem("zero_c"), sem("wqk_c")
        id_ok, setup_v, setup_p, scr_const, mscr_ok = (sem(n) for n in ("id_ok", "setup_v", "setup_p", "scr_const", "mscr_ok"))
        chains = {e: sem(f"chain_{e}") for e in ("dve", "pool", "act")}

        class Chain:

            def __init__(self, eng, name):
                self.eng, self.sem, self.at = eng, chains[name], 0

            def __call__(self, ins):
                self.at += 1
                ins.then_inc(self.sem, 1)
                self.eng.wait_ge(self.sem, self.at)

            def restart(self):
                if self.at:
                    self.eng.sem_clear(self.sem)
                self.at = 0

        passed = sem("passed")

        def apart(eng):
            eng.sem_inc(passed, 1)

        def walk(eng, table, chain=None):
            for times, steps in parts:
                mine = [x for x in steps if x[0][0] in table]
                if not mine:
                    continue
                if chain:
                    chain.restart()
                if times == 1:
                    for s, r, phase in mine:
                        table[s[0]](s, {x: v[0] for x, v in r.items()}, phase)
                    continue
                with eng.Fori(0, times) as i:
                    for s, r, phase in mine:
                        table[s[0]](s, {x: v[0] if v[1] == 0 else i * v[1] + v[0] for x, v in r.items()}, phase)
                    if chain:
                        chain.restart()

        loads = ([], [], [])

        def load(dst, src, group=1):
            loads[group].append((dst, src))

        load(w_qkv[:, :], a["L0_xattn_W_qkv"], 0)
        load(w_so[:, :], a["L0_xattn_W_self_out"])
        load(w_q0[:, :], a["L0_xattn_W_q"]); load(w_kv0[:, :], a["L0_xattn_W_kv"]); load(w_co[:, :], a["L0_xattn_W_cross_out"])
        load(w1[:, :], a["L0_xattn_W1"]); load(w2[:, :, :], a["L0_xattn_W2"].rearrange("(k p) n -> p k n", p=128))
        load(b1[:, :], a["L0_xattn_b1"].rearrange("(k p) -> p k", p=128)); load(b2[:, :], a["L0_xattn_b2"].rearrange("(o n) -> o n", o=1))
        for w in range(3):
            load(lng[:, w:w + 1], a[f"L0_xattn_ln{w + 1}_scale"].rearrange("(p o) -> p o", o=1), min(w, 1))
            load(lnb[:, w:w + 1], a[f"L0_xattn_ln{w + 1}_bias"].rearrange("(p o) -> p o", o=1), min(w, 1))
        for k, name in enumerate(("Wq", "Wk", "Wv", "Wf")):
            load(l1w[:, k, :], a[f"L1_xattn_{name}"], 2)
        load(l1b[:, 0:1], a["L1_xattn_bq"].rearrange("(p o) -> p o", o=1), 2)
        load(l1b[:, 1:2], a["L1_xattn_bk"].rearrange("(p o) -> p o", o=1), 2)
        for kt in range(KT):
            load(bv4[:, kt, :], a["L1_xattn_bv"].rearrange("(o n) -> o n", o=1), 2)
        load(bfb[:, :], row("L1_xattn_bf", D), 2)
        load(gb[3][0][:, :], row("L1_xattn_ln_gamma", D), 2); load(gb[3][1][:, :], row("L1_xattn_ln_beta", D), 2)
        load(gb[4][0][:, :], row("L2_xattn_gamma", D), 2); load(gb[4][1][:, :], row("L2_xattn_beta", D), 2)
        for k, name in enumerate(("Wq", "Wk", "Wv", "Wo")):
            load(w2raw[:, k, :], a[f"L2_xattn_{name}"], 2)
        load(tw[:, :, :], a["L3_xattn_trans_W"].rearrange("(k p) n -> p k n", p=128), 2)
        load(tbb[:, :], row("L3_xattn_trans_b", D), 2)
        load(mk, a["mask_Bx1x1xS2_ff0"].rearrange("b o c n -> b (o c n)"), 2)
        n_w = [16 * len(g) for g in loads]
        later = [(1, x) for x in loads[1]] + [(2, x) for x in loads[2]]
        per_step = -(-len(later) // (len(LATER_LOADS) - 1))

        x_dram = a["x"].rearrange("b (t p) d -> b p t d", p=128)
        c_dram = a["ctx_1024"].rearrange("b (t p) d -> b p t d", p=128)
        o_dram = out.rearrange("b (t p) d -> b p t d", p=128)

        block = ctx.enter_context(nc.Block())

        @block.sync
        def _(sp):
            sp.sem_inc(out_ok, 16)
            for dst, src in loads[0]:
                sp.dma_start(dst, src).then_inc(w_in[0], 16)

            def step_ld(s, r, p):
                if s[3] == 0:
                    sp.wait_ge(setup_p, 1)
                    for name, src, n in (("sq", qone, LQ), ("sk", kone, LQ), ("q", qone, LQ), ("k", kone, LK)):
                        for j in range(2):
                            dst = scr[name].rearrange("g (j i p) n -> j g i p n", j=2, p=8)[j, 6:8]
                            sp.dma_start(dst, src[:, 0:n].rearrange("r (o n) -> r o n", o=1).to_broadcast([16, NPAIR, n])).then_inc(scr_const, 16)
                    return
                for group, (dst, src) in later[per_step * (s[3] - 1):per_step * s[3]]:
                    sp.dma_start(dst, src, allow_slow_non_contiguous=dst.shape[0] == 128 and dst.shape[-1] == F // 128).then_inc(w_in[group], 16)

            def step_wb(s, r, p):
                sp.wait_ge(zero_c, 4)

            def step_wt(s, r, p):
                sp.wait_ge(mask_split, 1)
                sp.dma_start(mscr, mkp).then_inc(mscr_ok, 16)

            def put(w, name, src, groups, lo=0):
                g, k = groups[0], len(groups)
                sp.dma_start(scr[name][g:g + k].rearrange("g r n -> r g n"), src).then_inc(scr_in[w], 16)

            def put_q(w, name, n, off=0):
                put(w, name, split[w][:, 0:1, off:off + n].to_broadcast([128, 3, n]), (0, 1, 2))
                put(w, name, split[w][:, 1:2, off:off + n].to_broadcast([128, 2, n]), (3, 4))
                put(w, name, split[w][:, 2:3, off:off + n], (5,))

            def put_k(w, name, n, off=0):
                put(w, name, split[w][:, 0:3, off:off + n], (0, 1, 2))
                put(w, name, split[w][:, 0:2, off:off + n], (3, 4))
                put(w, name, split[w][:, 0:1, off:off + n], (5,))

            def get_q(T, name, w):
                for j in range(2):
                    sp.dma_start(QA[T][HB * j:HB * j + HB, :, j, :],
                                 scr[name].rearrange("g (j i p) n -> j g i p n", j=2, p=8)[j]).then_inc(q_in[T], 16)

            def get_k(T, name, w):
                for j in range(2):
                    sp.dma_start(KA[T][HB * j:HB * j + HB, :, 0:nk[T]],
                                 scr[name].rearrange("g (j i p) n -> j g i p n", j=2, p=8)[j]).then_inc(k_in[T], 16)

            def scratch_free(w, r):
                sp.wait_ge(split_done[w], r["w"] + 1)
                apart(sp)
                T = "scd"[r["ldT_b"]]
                sp.wait_ge((q_in if w == "q" else k_in)[T], r["ld"])
                apart(sp)
                if w == "s":
                    sp.wait_ge(q_in[T], r["ld"])
                    apart(sp)

            def step_xln(s, r, p):
                sp.wait_ge(z_ok[0], r["n"])
                apart(sp)
                sp.dma_start(xln[:, :, :], x_dram[r["n"]]).then_inc(x_in, 16)

            def step_xr(s, r, p):
                sp.wait_ge(m_free[r["prev_b"]], r["prev"])
                apart(sp)
                sp.dma_start(xr[:, :, :], x_dram[r["n"]]).then_inc(xr_in, 16)

            def step_cl(s, r, p):
                sp.wait_ge(m_free[r["prev_b"]], r["prev"])
                apart(sp)
                sp.dma_start(cin[:, :, :], c_dram[r["n"]]).then_inc(c_in, 16)

            def step_cl3(s, r, p):
                sp.wait_ge(ob_ok, r["n"] + 1)
                apart(sp)
                sp.dma_start(cin3[:, :, :], c_dram[r["n"]]).then_inc(c3_in, 16)

            def step_xs(s, r, p):
                sp.wait_ge(xs_out, 16 * (r["n"] + 1))
                apart(sp)
                sp.wait_ge(m_free[r["prev_b"]], r["prev"])
                apart(sp)
                sp.dma_start(xl1[:, :, :], xs[r["n"]]).then_inc(xs_in, 16)

            def step_qkw(s, r, p):
                scratch_free("s", r)
                put_q("s", "sq", LQ)
                put_k("s", "sk", LQ, off=LQ)

            def step_qkl(s, r, p):
                if s[2] == 0:
                    sp.wait_ge(scr_const, 16 * 8)
                sp.wait_ge(scr_in["s"], (r["w"] + 1) * 96)
                apart(sp)
                sp.wait_ge(st_free[0], r["e0"])
                apart(sp)
                sp.wait_ge(st_free[1], r["e1"])
                apart(sp)
                get_q("s", "sq", "s")
                get_k("s", "sk", "s")

            def step_kw(s, r, p):
                scratch_free("k", r)
                put_k("k", "k", LK)
                if p == 2:
                    if s[2] == 0:
                        sp.wait_ge(mscr_ok, 16)
                    for j in range(2):
                        dst = scr["k"].rearrange("g (j i p) n -> g j i p n", j=2, p=8)[6, j, 3:6]
                        sp.dma_start(dst, mscr[r["n"]].rearrange("t (o n) -> t o n", o=1).to_broadcast([3, 8, LK])).then_inc(mask_in, 16)

            def step_kl(s, r, p):
                sp.wait_ge(scr_in["k"], (r["w"] + 1) * 48)
                apart(sp)
                if p == 2:
                    sp.wait_ge(mask_in, (r["n"] + 1) * 32)
                    apart(sp)
                sp.wait_ge(st_free[0], r["e0"])
                apart(sp)
                sp.wait_ge(st_free[1], r["e1"])
                apart(sp)
                get_k(s[1], "k", "k")

            def step_qw(s, r, p):
                scratch_free("q", r)
                put_q("q", "q", LQ)

            def step_ql(s, r, p):
                sp.wait_ge(scr_in["q"], (r["w"] + 1) * 48)
                apart(sp)
                sp.wait_ge(st_free[0], r["e0"])
                apart(sp)
                sp.wait_ge(st_free[1], r["e1"])
                apart(sp)
                get_q(s[1], "q", "q")

            def step_nmt(s, r, p):
                T, q, par = s[1], s[3], s[3] % 2
                sp.wait_ge(m_free[r["bank"]], r["free"] + 1)
                apart(sp)
                for j in range(2):
                    sp.dma_start(QA[T][HB * j + R_MAX:HB * j + R_MAX + 3, 2 * q:2 * q + 2, j, :],
                                 nmt[par][6 * j:6 * j + 6, :]).then_inc(nm_in[par], 16)

            def step_ff2(s, r, p):
                sp.wait_ge(m_free[r["bank"]], r["free"] + 1)
                apart(sp)
                sp.dma_start(xs[r["n"]], x3[:, :, :]).then_inc(xs_out, 16)

            def step_l3h(s, r, p):
                sp.wait_ge(ob_ok, r["n"] + 2)
                apart(sp)
                sp.dma_start(o_dram[r["n"]], ob[:, :, :]).then_inc(out_ok, 16)

            walk(sp, {"LD": step_ld, "WB": step_wb, "WT": step_wt, "XLN": step_xln, "XR": step_xr, "CL": step_cl, "CL3": step_cl3, "XS": step_xs, "QKW": step_qkw,
                      "QKL": step_qkl, "KW": step_kw, "KL": step_kl, "QW": step_qw, "QL": step_ql, "NMT": step_nmt,
                      "FF2": step_ff2, "L3H": step_l3h})
            sp.wait_ge(out_ok, 16 * (B + 1))

        @block.gpsimd
        def _(pool):
            chain = Chain(pool, "pool")
            for ahead in (ob_ok, y_ok[3], y_ok[4]):
                pool.sem_inc(ahead, 1)
            pool.memset(kone, 0.0).then_inc(id_ok, 1)
            pool.memset(qone, 0.0).then_inc(id_ok, 1)
            pool.memset(ident[:, :], 0.0).then_inc(id_ok, 1)
            pool.memset(identb[:, :], 0.0).then_inc(id_ok, 1)
            pool.memset(causal[:, :], 0.0).then_inc(id_ok, 1)
            pool.memset(half[:, :], -0.5).then_inc(id_ok, 1)
            pool.wait_ge(id_ok, 6)
            for m in (ident, identb):
                chain(pool.affine_select(out=m[:, :], in_=m[:, :], compare_op=ALU.not_equal, fill=1.0, base=0,
                                         pattern=[[-1, 128]], channel_multiplier=1))
            chain(pool.affine_select(out=causal[:, 128:256], in_=causal[:, 128:256], compare_op=ALU.is_ge, fill=NEG, base=0,
                                     pattern=[[-1, 128]], channel_multiplier=1))
            chain(pool.affine_select(out=kone, in_=kone, compare_op=ALU.is_ge, fill=1.0, base=-3,
                                     pattern=[[0, LK]], channel_multiplier=1))
            chain(pool.affine_select(out=qone, in_=qone, compare_op=ALU.is_ge, fill=1.0, base=-6,
                                     pattern=[[0, LQ]], channel_multiplier=1))
            pool.affine_select(out=qone, in_=qone, compare_op=ALU.is_ge, fill=0.0, base=-3,
                               pattern=[[0, LQ]], channel_multiplier=1).then_inc(setup_p, 1)
            pool.wait_ge(setup_p, 1)

            def step_ld(s, r, p):
                if s[3] == 1:
                    pool.memset(QA["c"][:, :, :, :], 0.0).then_inc(zero_c, 1)
                    pool.memset(V1["c"][:, :, :, 0:DH], 0.0).then_inc(zero_c, 1)
                    pool.memset(V1["c"][:, :, :, DH:DH + 1], 1.0).then_inc(zero_c, 1)
                    pool.memset(V1["c"][:, :, :, DH + 1:32], 0.0).then_inc(zero_c, 1)

            def step_wt(s, r, p):
                pool.wait_ge(w_in[2], n_w[2])

            def parts_of(w, r):
                chain(pool.tensor_tensor(rest32[w][:, :], full32[w][:, :], split[w][:, 0, :], ALU.subtract))
                chain(pool.tensor_copy(split[w][:, 1, :], rest32[w][:, :]))
                pool.tensor_tensor(split[w][:, 2, :], rest32[w][:, :], split[w][:, 1, :], ALU.subtract).then_inc(split_done[w], 1)

            def step_split(s, r, p):
                w = {"QK": "s", "K": "k", "Q": "q"}[s[0]]
                pool.wait_ge(m_free[r["bank"]], r["free"] + 1)
                apart(pool)
                parts_of(w, r)

            def step_st(s, r, p):
                if s[1] != "s":
                    return
                par, u = s[3] % 2, s[4]
                pool.wait_ge(st_free[r["bank"]], r["free"] + 1)
                apart(pool)
                d = PT[par][:, u // 2, u % 2, 0:256 if u % 2 else 512].rearrange("k (j n) -> k j n", j=2)[:, :, 0:128]
                pool.affine_select(out=d, in_=d, compare_op=ALU.is_ge, fill=0.0, base=0,
                                   pattern=[[0, 2], [1, 128]], channel_multiplier=-1).then_inc(causal_cut, 1)

            def step_lns(s, r, p):
                w = s[1]
                pool.wait_ge(stats[w], r["n"] + 1)
                apart(pool)
                chain(pool.tensor_scalar(ve[w][:, :], mv[w][:, :, 1], 1e-6 if w < 3 else 1e-5, None, ALU.add))
                pool.tensor_tensor(rstd[w][:, :], ve[w][:, :], half[:, :], ALU.pow).then_inc(rstd_ok[w], 1)

            def step_x1b(s, r, p):
                pool.wait_ge(m_free[r["in_b"]], r["in"])
                apart(pool)
                pool.wait_ge(m_free[r["prev_b"]], r["prev"])
                apart(pool)
                pool.tensor_copy(x1b[:, :, :], x1[:, :, :]).then_inc(x1b_ok, 1)

            def step_y1b(s, r, p):
                pool.wait_ge(m_free[r["prev_b"]], r["prev"])
                apart(pool)
                pool.wait_ge(y_ok[3], r["n"] + 2)
                apart(pool)
                pool.tensor_copy(y1b[s[1]][:, :, :], y1[s[1]][:, :, :]).then_inc(y1b_ok[s[1]], 1)

            def step_xs(s, r, p):
                pool.wait_ge(xs_in, 16 * (r["n"] + 1))
                apart(pool)
                pool.wait_ge(m_free[r["prev_b"]], r["prev"])
                apart(pool)
                pool.tensor_tensor(xb1[:, :, :], xl1[:, :, :], bfb[:, :].rearrange("p (o n) -> p o n", o=1).to_broadcast([128, QT, D]),
                                   ALU.add).then_inc(xb_ok, 1)

            def step_lng(s, r, p):
                w = s[1]
                pool.wait_ge(z_ok[w], r["n"] + 1)
                apart(pool)
                if w == 3:
                    pool.wait_ge(y1b_ok[TURN[s[2] % 2]], r["j"])
                    apart(pool)
                T = TURN[s[2] % 2]
                y = y1[T] if w == 3 else y2
                g, be = (t[:, :].rearrange("p (o n) -> p o n", o=1).to_broadcast([128, QT, D]) for t in gb[w])
                chain(pool.tensor_tensor(zt[w][:, :, :], zt[w][:, :, :], g, ALU.mult))
                pool.tensor_tensor(y[:, :, :], zt[w][:, :, :], be, ALU.add).then_inc(y_ok[w], 1)

            def step_l3h(s, r, p):
                pool.wait_ge(th_ok, r["n"] + 1)
                apart(pool)
                pool.wait_ge(out_ok, 16 * (r["n"] + 1))
                apart(pool)
                pool.tensor_tensor(ob[:, :, :], hb[:, :, :], y2[:, :, :], ALU.add).then_inc(ob_ok, 1)

            walk(pool, {"LD": step_ld, "WT": step_wt, "QK": step_split, "K": step_split, "Q": step_split, "ST": step_st, "LNS": step_lns,
                        "X1B": step_x1b, "Y1B": step_y1b, "XS": step_xs, "LNG": step_lng, "L3H": step_l3h}, chain)

        @block.scalar
        def _(act):
            act.sem_inc(p3_ok, 1)
            act.wait_ge(w_in[0], n_w[0])
            act.wait_ge(setup_v, 1)

            def step_wb(s, r, p):
                act.wait_ge(w_in[1], n_w[1])
                act.wait_ge(zero_c, 4)

            def step_wt(s, r, p):
                act.wait_ge(w_in[2], n_w[2])

            def step_st(s, r, p):
                T, q, u, par = s[1], s[3], s[4], s[3] % 2
                act.wait_ge(st_full[r["bank"]], r["free"] + 1)
                if u == 0:
                    act.wait_ge(pv_done[par], r["pt"])
                n = 256 if T == "s" and u % 2 else 512
                act.activation(PT[par][:, u // 2, u % 2, 0:n], PST[r["bank"]][:, 0:n], ACT.Exp).then_inc(st_free[r["bank"]], 1)

            def step_lnt(s, r, p):
                act.wait_ge(m_full[r["bank"]], r["full"])
                bank, free = PM[r["bank"]], m_free[r["bank"]]
                w = s[1]
                act.activation(nxT[w][:, :], bank[:, 0:LQ], ACT.Identity, bias=lnb[:, w:w + 1], scale=lng[:, w:w + 1]).then_inc(free, 1)

            def step_split(s, r, p):
                w = {"QK": "s", "K": "k", "Q": "q"}[s[0]]
                act.wait_ge(m_full[r["bank"]], r["full"])
                bank, free = PM[r["bank"]], m_free[r["bank"]]
                act.wait_ge(split_done[w], r["w"])
                per = 96 if w == "s" else 48
                act.wait_ge(scr_in[w], r["w"] * per)
                act.activation(full32[w][:, :], bank[:, 0:width[w]], ACT.Copy)
                act.activation(split[w][:, 0, :], bank[:, 0:width[w]], ACT.Copy).then_inc(free, 1)

            def step_pvc(s, r, p):
                act.wait_ge(pv_done[s[3] % 2], r["pt"])
                act.activation(CT[s[1]][:, s[3], :], PM[r["bank"]][:, 0:LQ], ACT.Copy).then_inc(m_free[r["bank"]], 1)

            def step_v(s, r, p):
                act.wait_ge(m_full[r["bank"]], r["full"])
                bank, free = PM[r["bank"]], m_free[r["bank"]]
                T = s[1]
                n = KTS[T] * D
                act.activation(V1[T][:, 0:KTS[T], :, 0:DH], bank[:, 0:n].rearrange("k (t h d) -> k t h d", h=NH, d=DH), ACT.Copy).then_inc(free, 1)

            def step_outb(s, r, p):
                act.wait_ge(m_full[r["bank"]], r["full"])
                act.activation(cnT[:, :], PM[r["bank"]][:, 0:LQ], ACT.Copy).then_inc(m_free[r["bank"]], 1)

            def step_ct3(s, r, p):
                act.wait_ge(m_full[r["bank"]], r["full"])
                act.activation(ctxT3[:, :], PM[r["bank"]][:, 0:LK], ACT.Copy).then_inc(m_free[r["bank"]], 1)

            def step_xt(s, r, p):
                act.wait_ge(m_full[r["bank"]], r["full"])
                act.activation(xT1[:, :], PM[r["bank"]][:, 0:LQ], ACT.Copy).then_inc(m_free[r["bank"]], 1)

            def step_yt(s, r, p):
                act.wait_ge(m_full[r["bank"]], r["full"])
                act.activation(yT1[:, :], PM[r["bank"]][:, 0:LQ], ACT.Copy).then_inc(m_free[r["bank"]], 1)

            def step_y2t(s, r, p):
                act.wait_ge(m_full[r["bank"]], r["full"])
                act.activation(y2T[:, :], PM[r["bank"]][:, 0:LQ], ACT.Copy).then_inc(m_free[r["bank"]], 1)

            def step_l1a(s, r, p):
                act.wait_ge(m_full[r["bank"]], r["full"])
                act.activation(attT[:, :], PM[r["bank"]][:, 0:LQ], ACT.Copy).then_inc(m_free[r["bank"]], 1)

            def step_l3a(s, r, p):
                act.wait_ge(m_full[r["bank"]], r["full"])
                act.activation(tiT[:, :], PM[r["bank"]][:, 0:LQ], ACT.Copy).then_inc(m_free[r["bank"]], 1)

            def step_ct(s, r, p):
                dst = ctxT["c" if p == 1 else TURN[s[2] % 2]]
                act.wait_ge(m_full[r["bank"]], r["full"])
                act.activation(dst[:, :], PM[r["bank"]][:, :], ACT.Copy).then_inc(m_free[r["bank"]], 1)

            def step_ff1(s, r, p):
                act.wait_ge(m_full[r["bank"]], r["full"])
                bank, free = PM[r["bank"]], m_free[r["bank"]]
                for k in range(2):
                    blk = 2 * s[3] + k
                    ins = act.activation(hT[:, blk, :], bank[:, k * LQ:(k + 1) * LQ], ACT.Relu, bias=b1[:, blk:blk + 1])
                ins.then_inc(free, 1)

            def step_g1(s, r, p):
                act.wait_ge(m_full[r["bank"]], r["full"])
                bank, free = PM[r["bank"]], m_free[r["bank"]]
                if s[3] == 0:
                    act.activation(q1T[:, :], bank[:, 0:LQ], ACT.Gelu, bias=l1b[:, 0:1]).then_inc(free, 1)
                elif s[3] == 1:
                    act.activation(k1T[:, :], bank[:, :], ACT.Gelu, bias=l1b[:, 1:2]).then_inc(free, 1)
                else:
                    act.activation(v1[:, :, :].rearrange("k t d -> k (t d)"), bank[:, :], ACT.Gelu).then_inc(free, 1)

            def step_l1s(s, r, p):
                act.wait_ge(m_full[r["bank"]], r["full"])
                bank, free = PM[r["bank"]], m_free[r["bank"]]
                qt = s[3]
                act.wait_ge(nm1_ok, r["n"] * QT + qt + 1)
                act.activation(P1[:, qt, :], bank[:, :], ACT.Exp, bias=nm1[:, qt:qt + 1], accum_out=rs1[:, qt:qt + 1]).then_inc(free, 1)

            def step_l3s(s, r, p):
                act.wait_ge(m_full[r["bank"]], r["full"])
                bank, free = PM[r["bank"]], m_free[r["bank"]]
                act.wait_ge(nm3_ok, r["n"] * 2 + s[3] + 1)
                qt = s[3]
                act.activation(P3[:, qt, :], bank[:, :], ACT.Exp, bias=nm3[:, qt:qt + 1], accum_out=rs3[:, qt:qt + 1]).then_inc(free, 1)

            def step_l3n(s, r, p):
                act.wait_ge(rr3_ok, r["n"] + 1)
                for qt in range(QT):
                    ins = act.activation(P3[:, qt, :], P3[:, qt, :], ACT.Copy, scale=rr3[:, qt:qt + 1])
                ins.then_inc(p3_ok, 1)

            def step_l3h(s, r, p):
                act.wait_ge(m_free[r["bank"]], r["free"] + 1)
                act.activation(hb[:, :, :], hb[:, :, :], ACT.Tanh).then_inc(th_ok, 1)

            walk(act, {"WB": step_wb, "WT": step_wt, "ST": step_st, "LNT": step_lnt, "QK": step_split, "K": step_split, "Q": step_split, "V": step_v, "PVC": step_pvc,
                       "OUTB": step_outb, "CT": step_ct, "CT3": step_ct3, "XT": step_xt,
                       "YT": step_yt, "Y2T": step_y2t, "L1A": step_l1a, "L3A": step_l3a,
                       "FF1": step_ff1, "G1": step_g1, "L1S": step_l1s, "L3S": step_l3s, "L3N": step_l3n, "L3H": step_l3h})

        @block.vector
        def _(dve):
            chain = Chain(dve, "dve")
            chain(dve.memset(V1["d"][:, :, :, :], 0.0))
            chain(dve.memset(V1["d"][:, :, :, DH:DH + 1], 1.0))
            chain(dve.memset(QA["d"][:, :, :, :], 0.0))
            chain(dve.memset(ones1[:, :], 1.0))
            dve.wait_ge(w_in[0], n_w[0])
            scale = float(np.float32(1.0) / np.sqrt(np.float32(DH)))

            def permuted(dst, src, by):
                view = src.rearrange("k (p j i) -> k j i p", p=NPAIR, j=2)
                for j in range(2):
                    chain(dve.tensor_scalar(dst[:, 64 * j:64 * j + 64].rearrange("k (i p) -> k i p", p=NPAIR), view[:, j], by, None, ALU.mult))

            permuted(wqp["s"], w_qkv[:, 0:D], scale)
            permuted(wkp["s"], w_qkv[:, D:2 * D], 1.0)
            dve.memset(junk[:, :, :], 0.0).then_inc(setup_v, 1)

            def step_wb(s, r, p):
                dve.wait_ge(w_in[1], n_w[1])
                permuted(wqp[1], w_q0[:, :], scale)
                permuted(wkp[1], w_kv0[:, 0:D], 1.0)
                dve.sem_inc(wqk_c, 1)

            def step_wt(s, r, p):
                dve.wait_ge(w_in[2], n_w[2])
                chain(dve.tensor_scalar(mk, mk, NEG, None, ALU.mult))
                chain(dve.tensor_copy(mkp[:, 0, :], mk))
                chain(dve.tensor_tensor(mkr, mk, mkp[:, 0, :], ALU.subtract))
                chain(dve.tensor_copy(mkp[:, 1, :], mkr))
                dve.tensor_tensor(mkp[:, 2, :], mkr, mkp[:, 1, :], ALU.subtract).then_inc(mask_split, 1)
                dve.wait_ge(m_full[r["bank"]], r["full"])
                bank, free = PM[r["bank"]], m_free[r["bank"]]
                permuted(wqp[2], bank[:, 0:128], scale)
                permuted(wkp[2], bank[:, 128:256], 1.0)
                chain(dve.tensor_copy(wv2[:, :], bank[:, 256:384]))
                dve.tensor_copy(wo2[:, :], bank[:, 384:512]).then_inc(free, 1)

            def step_s(s, r, p):
                T, q, u, par = s[1], s[3], s[4], s[3] % 2
                bank, free = PS[r["bank"]], s_free[r["bank"]]
                if u == 0:
                    dve.wait_ge(nm_split[par], r["mx"])
                dve.wait_ge(s_full[r["bank"]], r["free"] + 1)
                if T == "s":
                    dve.sem_inc(passed, 1)
                    pp, j = u // 2, u % 2
                    dve.tensor_tensor_reduce(out=junk[:, r["bank"], 0:128], in0=bank[:, 0:128], in1=causal[:, 128:256], scale=1.0, scalar=-3.0e38,
                                             op0=ALU.add, op1=ALU.max, accum_out=mx[par][:, 0, j, pp:pp + 1])
                    dve.tensor_tensor_reduce(out=junk[:, r["bank"], 128:384], in0=bank[:, 128:384], in1=causal[:, :], scale=1.0, scalar=-3.0e38,
                                             op0=ALU.add, op1=ALU.max, accum_out=mx[par][:, 1, j, pp:pp + 1]).then_inc(free, 1)
                else:
                    pp, j, qt = u // 4, u // 2 % 2, u % 2
                    dve.reduce_max(mx[par][:, qt, j, pp:pp + 1], bank[:, :], X).then_inc(free, 1)

            def step_nm(s, r, p):
                par = s[3] % 2
                dve.wait_ge(s_free[0], r["s0"])
                dve.wait_ge(s_free[1], r["s1"])
                dve.wait_ge(s_free[2], r["s2"])
                dve.sem_inc(passed, 1)
                chain(dve.tensor_scalar(nms[par][:, :, :, 0, :], mx[par][:, :, :, :], -1.0, None, ALU.mult))
                chain(dve.scalar_tensor_tensor(nr[par][:, :, :, :], mx[par][:, :, :, :], -1.0, nms[par][:, :, :, 0, :], ALU.mult, ALU.subtract))
                chain(dve.tensor_copy(nms[par][:, :, :, 1, :], nr[par][:, :, :, :]))
                dve.tensor_tensor(nms[par][:, :, :, 2, :], nr[par][:, :, :, :], nms[par][:, :, :, 1, :],
                                  ALU.subtract).then_inc(nm_split[par], 1)

            def step_nmt(s, r, p):
                dve.wait_ge(m_full[r["bank"]], r["full"])
                bank, free = PM[r["bank"]], m_free[r["bank"]]
                par = s[3] % 2
                dve.wait_ge(nm_in[par], 32 * r["mx"])
                dve.tensor_copy(nmt[par][:, :], bank[0:12, 0:128].bitcast(bf16)).then_inc(free, 1)

            def step_lns(s, r, p):
                w = s[1]
                src = {0: xln, 1: x1, 2: x2, 3: xo1, 4: xo2}[w]
                if w == 0:
                    dve.wait_ge(x_in, 16 * (r["n"] + 1))
                else:
                    dve.wait_ge(m_free[r["in_b"]], r["in"])
                for t in range(QT):
                    chain(dve.bn_stats(bst[:, t, :], src[:, t, :]))
                for t in range(QT):
                    ins = dve.bn_aggr(mv[w][:, t, :], bst[:, t, :])
                ins.then_inc(stats[w], 1)

            def step_lnz(s, r, p):
                w = s[1]
                src = {0: xln, 1: x1, 2: x2, 3: xo1, 4: xo2}[w]
                dve.wait_ge(rstd_ok[w], r["n"] + 1)
                if w >= 3:
                    dve.wait_ge(y_ok[w], r["n"] + 1)
                for t in range(QT):
                    ins = dve.tensor_scalar(zt[w][:, t, :], src[:, t, :], mv[w][:, t, 0:1], rstd[w][:, t:t + 1], ALU.subtract, ALU.mult)
                ins.then_inc(z_ok[w], 1)

            def step_outa(s, r, p):
                dve.wait_ge(m_full[r["bank"]], r["full"])
                bank, free = PM[r["bank"]], m_free[r["bank"]]
                v = bank[:, :].rearrange("q (g c r) -> q g c r", g=NQUAD, c=4)
                chain(dve.reciprocal(rr[:, s[3], :, :], v[:, :, :, DH]))
                dve.tensor_tensor(cn[:, s[3], :].rearrange("q (g c r) -> q g c r", g=NQUAD, c=4), v[:, :, :, 0:DH],
                                  rr[:, s[3], :, :].rearrange("q g (c o) -> q g c o", o=1).to_broadcast([128, NQUAD, 4, DH]), ALU.mult).then_inc(free, 1)

            def step_outc(s, r, p):
                dve.wait_ge(m_full[r["bank"]], r["full"])
                bank, free = PM[r["bank"]], m_free[r["bank"]]
                T = s[1]
                if T == "s":
                    dve.wait_ge(xr_in, 16 * (r["n"] + 1))
                    dve.wait_ge(x1b_ok, r["n"])
                    dst, res = x1, xr
                elif p == 1:
                    dve.wait_ge(x1b_ok, r["n"] + 1)
                    dst, res = x2, x1b
                else:
                    dve.wait_ge(y1b_ok[T], r["t"] + 1 - (8 if T == "c" else 0))
                    dst, res = xo2, y1b[T]
                dve.tensor_tensor(dst[:, :, :], bank[:, 0:LQ].rearrange("q (t d) -> q t d", t=QT), res[:, :, :], ALU.add).then_inc(free, 1)

            def step_ff2(s, r, p):
                dve.wait_ge(m_full[r["bank"]], r["full"])
                bank, free = PM[r["bank"]], m_free[r["bank"]]
                dve.wait_ge(xs_out, 16 * r["n"])
                dve.tensor_tensor(x3[:, :, :], bank[:, 0:LQ].rearrange("q (t d) -> q t d", t=QT), x2[:, :, :], ALU.add).then_inc(free, 1)

            def step_l1s(s, r, p):
                dve.wait_ge(m_full[r["bank"]], r["full"])
                bank, free = PM[r["bank"]], m_free[r["bank"]]
                dve.tensor_reduce(nm1[:, s[3]:s[3] + 1], bank[:, :], X, ALU.max, negate=True).then_inc(nm1_ok, 1)

            def step_l1t(s, r, p):
                dve.wait_ge(m_full[r["bank"]], r["full"])
                bank, free = PM[r["bank"]], m_free[r["bank"]]
                qt = s[3]
                dve.tensor_copy(P1T[:, :, qt * 128:qt * 128 + 128], bank[:, :].rearrange("k (t q) -> k t q", t=KT)).then_inc(free, 1)

            def step_l1o(s, r, p):
                dve.wait_ge(m_full[r["bank"]], r["full"])
                bank, free = PM[r["bank"]], m_free[r["bank"]]
                chain(dve.reciprocal(rr1[:, :], rs1[:, :]))
                dve.wait_ge(xb_ok, r["n"] + 1)
                for t in range(QT):
                    ins = dve.scalar_tensor_tensor(xo1[:, t, :], bank[:, t * D:(t + 1) * D], rr1[:, t:t + 1], xb1[:, t, :], ALU.mult, ALU.add)
                ins.then_inc(free, 1)

            def step_l3s(s, r, p):
                dve.wait_ge(m_full[r["bank"]], r["full"])
                bank, free = PM[r["bank"]], m_free[r["bank"]]
                dve.tensor_reduce(nm3[:, s[3]:s[3] + 1], bank[:, :], X, ALU.max, negate=True).then_inc(nm3_ok, 1)

            def step_l3n(s, r, p):
                dve.wait_ge(m_free[r["in_b"]], r["in"])
                dve.wait_ge(m_free[r["in2_b"]], r["in2"])
                dve.wait_ge(p3_ok, r["n"] + 1)
                dve.reciprocal(rr3[:, :], rs3[:, :]).then_inc(rr3_ok, 1)

            def step_l3t(s, r, p):
                dve.wait_ge(m_full[r["bank"]], r["full"])
                bank, free = PM[r["bank"]], m_free[r["bank"]]
                dve.tensor_copy(P3T[:, :, s[3] * 128:s[3] * 128 + 128], bank[:, :].rearrange("k (t q) -> k t q", t=KT)).then_inc(free, 1)

            def step_l3h(s, r, p):
                dve.wait_ge(m_full[r["bank"]], r["full"])
                bank, free = PM[r["bank"]], m_free[r["bank"]]
                dve.wait_ge(ob_ok, r["n"] + 1)
                dve.tensor_tensor(hb[:, :, :], bank[:, 0:LQ].rearrange("q (t d) -> q t d", t=QT),
                                  tbb[:, :].rearrange("p (o n) -> p o n", o=1).to_broadcast([128, QT, D]), ALU.add).then_inc(free, 1)

            walk(dve, {"WB": step_wb, "WT": step_wt, "S": step_s, "NM": step_nm, "NMT": step_nmt, "LNS": step_lns, "LNZ": step_lnz, "OUTA": step_outa,
                       "OUTC": step_outc, "FF2": step_ff2, "L1S": step_l1s, "L1T": step_l1t, "L1O": step_l1o, "L3S": step_l3s,
                       "L3N": step_l3n, "L3T": step_l3t, "L3H": step_l3h}, chain)

        @block.tensor
        def _(pe):
            pe.wait_ge(setup_p, 1)
            pe.wait_ge(w_in[0], n_w[0])
            pe.wait_ge(setup_v, 1)

            def transposed(bank, blocks):
                for k, src in enumerate(blocks):
                    ins = pe.transpose(bank[:, 128 * k:128 * k + 128], src, ident[:, :])
                return ins

            def mm(out_, l, m, first=True, last=True):
                return pe.matmul(out_, l, m, start=first, stop=True, skip_group_check=True)

            def step_wb(s, r, p):
                pe.wait_ge(w_in[1], n_w[1])
                pe.wait_ge(wqk_c, 1)
                pe.wait_ge(zero_c, 4)

            def step_wt(s, r, p):
                pe.wait_ge(w_in[2], n_w[2])
                pe.wait_ge(m_free[r["bank"]], r["free"])
                transposed(PM[r["bank"]], [w2raw[:, k, :] for k in range(4)]).then_inc(m_full[r["bank"]], 1)

            def step_s(s, r, p):
                T, q, u = s[1], s[3], s[4]
                if q == 0 and u == 0:
                    pe.wait_ge(q_in[T], 32 * (r["t"] + 1))
                    pe.wait_ge(k_in[T], 32 * (r["t"] + 1))
                pe.wait_ge(s_free[r["bank"]], r["free"])
                bank = PS[r["bank"]]
                if T == "s":
                    pr, j = 2 * q + u // 2, u % 2
                    mm(bank[:, 0:128], QA[T][:, pr, j, 0:128], KA[T][:, pr, 0:128])
                    ins = mm(bank[:, 128:384], QA[T][:, pr, j, 128:256], KA[T][:, pr, 0:LQ])
                else:
                    pr, j, qt = 2 * q + u // 4, u // 2 % 2, u % 2
                    ins = mm(bank[:, :], QA[T][:, pr, j, 128 * qt:128 * qt + 128], KA[T][:, pr, :])
                ins.then_inc(s_full[r["bank"]], 1)

            def step_nmt(s, r, p):
                par = s[3] % 2
                pe.wait_ge(nm_split[par], r["mx"] + 1)
                pe.wait_ge(m_free[r["bank"]], r["free"])
                bank, fullsem = PM[r["bank"]], m_full[r["bank"]]
                o = bank[0:12, 0:128].bitcast(bf16)
                for qt in range(QT):
                    ins = pe.transpose(o[:, 128 * qt:128 * qt + 128], nms[par][:, qt, :, :, :].rearrange("q j t p -> q (j t p)"), identb[:, :])
                ins.then_inc(fullsem, 1)

            def step_st(s, r, p):
                T, q, u, par = s[1], s[3], s[4], s[3] % 2
                pe.wait_ge(nm_in[par], 32 * r["mx"])
                pe.wait_ge(st_free[r["bank"]], r["free"])
                bank = PST[r["bank"]]
                if T == "s":
                    pr = 2 * q + u // 2
                    if u % 2 == 0:
                        ins = mm(bank[:, :], KA[T][:, pr, 0:128], QA[T][:, pr, :, :].rearrange("k j n -> k (j n)"))
                    else:
                        ins = mm(bank[:, 0:256].rearrange("k (j n) -> k j n", j=2), KA[T][:, pr, 128:256], QA[T][:, pr, :, 128:256])
                else:
                    pr, kt = 2 * q + u // 4, u % 4
                    ins = mm(bank[:, :], KA[T][:, pr, 128 * kt:128 * kt + 128], QA[T][:, pr, :, :].rearrange("k j n -> k (j n)"))
                ins.then_inc(st_full[r["bank"]], 1)

            def step_pv(s, r, p):
                T, q, kt, par = s[1], s[3], s[4], s[3] % 2
                if kt == 0:
                    pe.wait_ge(st_free[0], r["st0"])
                    pe.wait_ge(st_free[1], r["st1"])
                    if T == "s":
                        pe.wait_ge(causal_cut, r["t"] * 16 + 4 * (q + 1))
                    if q == 0:
                        pe.wait_ge(m_free[r["v_b"]], r["v"])
                    pe.wait_ge(m_free[r["bank"]], r["free"])
                bank = PM[r["bank"]]
                for c in range(4):
                    pp, j = c // 2, c % 2
                    lhs = V1[T][:, kt, 4 * q + c, :]
                    if T == "s" and kt == 1:
                        o, rhs = bank[32 * c:32 * c + 32, 128:256], PT[par][:, pp, 1, 128 * j:128 * j + 128]
                    elif T == "s":
                        o, rhs = bank[32 * c:32 * c + 32, 0:256], PT[par][:, pp, 0, 256 * j:256 * j + 256]
                    else:
                        o, rhs = bank[32 * c:32 * c + 32, 0:256], PT[par][:, 2 * pp + kt // 2, kt % 2, 256 * j:256 * j + 256]
                    ins = pe.matmul(o, lhs, rhs, start=kt == 0, stop=True, skip_group_check=True)
                if kt == KTS[T] - 1:
                    ins.then_inc(pv_done[par], 1)

            def step_lnt(s, r, p):
                w = s[1]
                pe.wait_ge(z_ok[w], r["n"] + 1)
                pe.wait_ge(m_free[r["bank"]], r["free"])
                transposed(PM[r["bank"]], [zt[w][:, t, :] for t in range(QT)]).then_inc(m_full[r["bank"]], 1)

            def step_qk(s, r, p):
                if r["in_b"] != r["bank"]:
                    pe.wait_ge(m_free[r["in_b"]], r["in"])
                pe.wait_ge(m_free[r["bank"]], r["free"])
                bank, fullsem = PM[r["bank"]], m_full[r["bank"]]
                mm(bank[:, 0:LQ], wqp["s"][:, :], nxT[0][:, :])
                mm(bank[:, LQ:2 * LQ], wkp["s"][:, :], nxT[0][:, :]).then_inc(fullsem, 1)

            def step_q(s, r, p):
                if r["in_b"] != r["bank"]:
                    pe.wait_ge(m_free[r["in_b"]], r["in"])
                pe.wait_ge(m_free[r["bank"]], r["free"])
                bank, fullsem = PM[r["bank"]], m_full[r["bank"]]
                mm(bank[:, 0:LQ], wqp[p][:, :], (nxT[1] if p == 1 else yT1)[:, :]).then_inc(fullsem, 1)

            def step_k(s, r, p):
                if r["in_b"] != r["bank"]:
                    pe.wait_ge(m_free[r["in_b"]], r["in"])
                pe.wait_ge(m_free[r["bank"]], r["free"])
                bank, fullsem = PM[r["bank"]], m_full[r["bank"]]
                mm(bank[:, :], wkp[p][:, :], ctxT[s[1]][:, :]).then_inc(fullsem, 1)

            def step_v(s, r, p):
                if r["in_b"] != r["bank"]:
                    pe.wait_ge(m_free[r["in_b"]], r["in"])
                pe.wait_ge(m_free[r["bank"]], r["free"])
                bank, fullsem = PM[r["bank"]], m_full[r["bank"]]
                T = s[1]
                src = nxT[0] if T == "s" else ctxT[T]
                w = w_qkv[:, 2 * D:3 * D] if T == "s" else (w_kv0[:, D:2 * D] if p == 1 else wv2[:, :])
                for t in range(KTS[T]):
                    ins = mm(bank[:, D * t:D * t + D], src[:, 128 * t:128 * t + 128], w)
                ins.then_inc(fullsem, 1)

            def step_outa(s, r, p):
                if r["in_b"] != r["bank"]:
                    pe.wait_ge(m_free[r["in_b"]], r["in"])
                qt = s[3]
                pe.wait_ge(m_free[r["bank"]], r["free"])
                transposed(PM[r["bank"]], [CT[s[1]][:, g, 128 * qt:128 * qt + 128] for g in range(NQUAD)]).then_inc(m_full[r["bank"]], 1)

            def step_outb(s, r, p):
                if r["in_b"] != r["bank"]:
                    pe.wait_ge(m_free[r["in_b"]], r["in"])
                pe.wait_ge(m_free[r["bank"]], r["free"])
                transposed(PM[r["bank"]], [cn[:, t, :] for t in range(QT)]).then_inc(m_full[r["bank"]], 1)

            def step_outc(s, r, p):
                if r["in_b"] != r["bank"]:
                    pe.wait_ge(m_free[r["in_b"]], r["in"])
                pe.wait_ge(m_free[r["bank"]], r["free"])
                bank, fullsem = PM[r["bank"]], m_full[r["bank"]]
                w = w_so if s[1] == "s" else (w_co if p == 1 else wo2)
                for t in range(QT):
                    ins = mm(bank[:, D * t:D * t + D], cnT[:, 128 * t:128 * t + 128], w[:, :])
                ins.then_inc(fullsem, 1)

            def step_ct(s, r, p):
                pe.wait_ge(c_in, 16 * (r["n"] + 1 + (B if p == 2 else 0)))
                pe.wait_ge(m_free[r["bank"]], r["free"])
                transposed(PM[r["bank"]], [cin[:, t, :] for t in range(KT)]).then_inc(m_full[r["bank"]], 1)

            def step_ff1(s, r, p):
                if r["in_b"] != r["bank"]:
                    pe.wait_ge(m_free[r["in_b"]], r["in"])
                pe.wait_ge(m_free[r["bank"]], r["free"])
                bank, fullsem = PM[r["bank"]], m_full[r["bank"]]
                for k in range(2):
                    blk = 2 * s[3] + k
                    ins = mm(bank[:, LQ * k:LQ * k + LQ], w1[:, 128 * blk:128 * blk + 128], nxT[2][:, :])
                ins.then_inc(fullsem, 1)

            def step_ff2(s, r, p):
                if r["in_b"] != r["bank"]:
                    pe.wait_ge(m_free[r["in_b"]], r["in"])
                pe.wait_ge(m_free[r["bank"]], r["free"])
                bank, fullsem = PM[r["bank"]], m_full[r["bank"]]
                for t in range(QT):
                    o = bank[:, D * t:D * t + D]
                    mm(o, ones1[:, :], b2[:, :], True, False)
                    for blk in range(F // 128):
                        ins = mm(o, hT[:, blk, 128 * t:128 * t + 128], w2[:, blk, :], False, blk == F // 128 - 1)
                ins.then_inc(fullsem, 1)

            def step_xt(s, r, p):
                pe.wait_ge(xs_in, 16 * (r["n"] + 1))
                pe.wait_ge(m_free[r["bank"]], r["free"])
                transposed(PM[r["bank"]], [xl1[:, t, :] for t in range(QT)]).then_inc(m_full[r["bank"]], 1)

            def step_g1(s, r, p):
                if r["in_b"] != r["bank"]:
                    pe.wait_ge(m_free[r["in_b"]], r["in"])
                if r["in2_b"] != r["bank"]:
                    pe.wait_ge(m_free[r["in2_b"]], r["in2"])
                pe.wait_ge(m_free[r["bank"]], r["free"])
                bank, fullsem = PM[r["bank"]], m_full[r["bank"]]
                if s[3] == 0:
                    ins = mm(bank[:, 0:LQ], l1w[:, 0, :], xT1[:, :])
                elif s[3] == 1:
                    ins = mm(bank[:, :], l1w[:, 1, :], ctxT[s[1]][:, :])
                else:
                    mm(bank[:, :], ones1[:, :], bv4[:, :, :].rearrange("o t d -> o (t d)"), True, False)
                    for t in range(KT):
                        ins = pe.matmul(bank[:, D * t:D * t + D], ctxT[s[1]][:, 128 * t:128 * t + 128], l1w[:, 2, :], start=False, stop=True,
                                        skip_group_check=True)
                ins.then_inc(fullsem, 1)

            def step_l1s(s, r, p):
                if r["in_b"] != r["bank"]:
                    pe.wait_ge(m_free[r["in_b"]], r["in"])
                pe.wait_ge(m_free[r["bank"]], r["free"])
                bank, fullsem = PM[r["bank"]], m_full[r["bank"]]
                mm(bank[:, :], q1T[:, 128 * s[3]:128 * s[3] + 128], k1T[:, :]).then_inc(fullsem, 1)

            def step_l1t(s, r, p):
                if r["in_b"] != r["bank"]:
                    pe.wait_ge(m_free[r["in_b"]], r["in"])
                pe.wait_ge(m_free[r["bank"]], r["free"])
                transposed(PM[r["bank"]], [P1[:, s[3], 128 * t:128 * t + 128] for t in range(KT)]).then_inc(m_full[r["bank"]], 1)

            def step_l1a(s, r, p):
                if r["in_b"] != r["bank"]:
                    pe.wait_ge(m_free[r["in_b"]], r["in"])
                pe.wait_ge(m_free[r["bank"]], r["free"])
                bank, fullsem = PM[r["bank"]], m_full[r["bank"]]
                for t in range(KT):
                    ins = mm(bank[:, 0:LQ], v1[:, t, :], P1T[:, t, :], t == 0, t == KT - 1)
                ins.then_inc(fullsem, 1)

            def step_l1o(s, r, p):
                if r["in_b"] != r["bank"]:
                    pe.wait_ge(m_free[r["in_b"]], r["in"])
                pe.wait_ge(m_free[r["bank"]], r["free"])
                bank, fullsem = PM[r["bank"]], m_full[r["bank"]]
                for t in range(QT):
                    ins = mm(bank[:, D * t:D * t + D], attT[:, 128 * t:128 * t + 128], l1w[:, 3, :])
                ins.then_inc(fullsem, 1)

            def step_yt(s, r, p):
                pe.wait_ge(y_ok[3], r["n"] + 2)
                pe.wait_ge(m_free[r["bank"]], r["free"])
                transposed(PM[r["bank"]], [y1[s[1]][:, t, :] for t in range(QT)]).then_inc(m_full[r["bank"]], 1)

            def step_y2t(s, r, p):
                pe.wait_ge(y_ok[4], r["n"] + 2)
                pe.wait_ge(m_free[r["bank"]], r["free"])
                transposed(PM[r["bank"]], [y2[:, t, :] for t in range(QT)]).then_inc(m_full[r["bank"]], 1)

            def step_ct3(s, r, p):
                pe.wait_ge(c3_in, 16 * (r["n"] + 1))
                pe.wait_ge(m_free[r["bank"]], r["free"])
                transposed(PM[r["bank"]], [cin3[:, t, :] for t in range(KT)]).then_inc(m_full[r["bank"]], 1)

            def step_l3s(s, r, p):
                if r["in_b"] != r["bank"]:
                    pe.wait_ge(m_free[r["in_b"]], r["in"])
                if r["in2_b"] != r["bank"]:
                    pe.wait_ge(m_free[r["in2_b"]], r["in2"])
                pe.wait_ge(m_free[r["bank"]], r["free"])
                bank, fullsem = PM[r["bank"]], m_full[r["bank"]]
                mm(bank[:, :], y2T[:, 128 * s[3]:128 * s[3] + 128], ctxT3[:, :]).then_inc(fullsem, 1)

            def step_l3t(s, r, p):
                pe.wait_ge(p3_ok, r["n"] + 2)
                pe.wait_ge(m_free[r["bank"]], r["free"])
                transposed(PM[r["bank"]], [P3[:, s[3], 128 * t:128 * t + 128] for t in range(KT)]).then_inc(m_full[r["bank"]], 1)

            def step_l3a(s, r, p):
                if r["in_b"] != r["bank"]:
                    pe.wait_ge(m_free[r["in_b"]], r["in"])
                pe.wait_ge(m_free[r["bank"]], r["free"])
                bank, fullsem = PM[r["bank"]], m_full[r["bank"]]
                for t in range(KT):
                    ins = mm(bank[:, 0:LQ], cin3[:, t, :], P3T[:, t, :], t == 0, t == KT - 1)
                ins.then_inc(fullsem, 1)

            def step_l3h(s, r, p):
                if r["in_b"] != r["bank"]:
                    pe.wait_ge(m_free[r["in_b"]], r["in"])
                pe.wait_ge(m_free[r["bank"]], r["free"])
                bank, fullsem = PM[r["bank"]], m_full[r["bank"]]
                for t in range(QT):
                    mm(bank[:, D * t:D * t + D], y2T[:, 128 * t:128 * t + 128], tw[:, 0, :], True, False)
                    ins = mm(bank[:, D * t:D * t + D], tiT[:, 128 * t:128 * t + 128], tw[:, 1, :], False, True)
                ins.then_inc(fullsem, 1)

            walk(pe, {"WB": step_wb, "WT": step_wt, "S": step_s, "NMT": step_nmt, "ST": step_st, "PV": step_pv, "LNT": step_lnt, "QK": step_qk,
                      "Q": step_q, "K": step_k, "V": step_v, "OUTA": step_outa, "OUTB": step_outb, "OUTC": step_outc, "CT": step_ct,
                      "FF1": step_ff1, "FF2": step_ff2, "XT": step_xt, "G1": step_g1, "L1S": step_l1s, "L1T": step_l1t,
                      "L1A": step_l1a, "L1O": step_l1o, "YT": step_yt, "Y2T": step_y2t, "CT3": step_ct3, "L3S": step_l3s,
                      "L3T": step_l3t, "L3A": step_l3a, "L3H": step_l3h})


_INS = ["x", "ctx_1024", "mask_Bx1x1xS2_ff0"] + [f"L0_xattn_{n}" for n in (
    "W_qkv", "W_self_out", "W_q", "W_kv", "W_cross_out", "W1", "b1", "W2", "b2", "ln1_scale", "ln1_bias", "ln2_scale",
    "ln2_bias", "ln3_scale", "ln3_bias")] + [f"L1_xattn_{n}" for n in (
        "Wq", "bq", "Wk", "bk", "Wv", "bv", "Wf", "bf", "ln_gamma", "ln_beta")] + [f"L2_xattn_{n}" for n in (
            "Wq", "Wk", "Wv", "Wo", "gamma", "beta")] + ["L3_xattn_trans_W", "L3_xattn_trans_b"]


def kernel(**inputs):
    import numpy as _np
    import concourse.bacc as _bacc
    from concourse import mybir as _mybir
    from concourse.bass_utils import run_bass_kernel_spmd as _run

    nc = _bacc.Bacc("TRN2", target_bir_lowering=False, num_devices=1)
    arrays, args = {}, {}
    for name in _INS:
        arr = _np.ascontiguousarray(inputs[name])
        arrays[f"in_{name}"] = arr
        args[name] = nc.dram_tensor(f"in_{name}", arr.shape, _mybir.dt.from_np(arr.dtype), kind="ExternalInput").ap()
    o = nc.dram_tensor("out_0", (B, LQ, D), _mybir.dt.float32, kind="ExternalOutput").ap()
    program(nc, args, o)
    r = _run(nc, [arrays], core_ids=[0])
    return r.results[0]["out_0"]
```
